# Optimizing a Trainium2 kernel written in Bass

```python
import numpy as np
import jax
import jax.numpy as jnp

def _softmax(x, axis=-1):
    return jax.nn.softmax(x, axis=axis)

def _gelu(x):
    return jax.nn.gelu(x, approximate=True)

def _silu(x):
    return jax.nn.silu(x)

def _sigmoid(x):
    return jax.nn.sigmoid(x)

def _layernorm(x, axis=-1, eps=1e-05):
    m = jnp.mean(x, axis=axis, keepdims=True)
    v = jnp.var(x, axis=axis, keepdims=True)
    return (x - m) / jnp.sqrt(v + eps)

def _scatter_add(tgt, idx, src, axis=0):
    return tgt.at[idx].add(src)

def _segment_sum(src, seg, n):
    return jax.ops.segment_sum(src, seg, n)
kernel_name = 'mk_gnn_preln_d4_gnn_r8_a5059e'

def setup_inputs(seed: int=0):
    np.random.seed(seed)
    _w = jnp.asarray

    def _rec_inputs():
        import jax
        import jax.numpy as jnp
        _gk = jax.random.key(seed)
        x = -0.000202 + 1 * jax.random.normal(jax.random.fold_in(_gk, 1), (12500, 128), jnp.float32)
        _s = jax.random.randint(jax.random.fold_in(_gk, 2), (100000,), 0, 12500, jnp.int32)
        _d = jax.random.randint(jax.random.fold_in(_gk, 3), (100000,), 0, 12500, jnp.int32)
        _loop = jnp.arange(12500, dtype=jnp.int32)
        src = jnp.concatenate([_s, _d, _loop])
        dst = jnp.concatenate([_d, _s, _loop])
        _o = jnp.argsort(dst, stable=True)
        src = src[_o]
        dst = dst[_o]
        edge_attr_16 = 0.000268479 + 0.999861 * jax.random.normal(jax.random.fold_in(_gk, 11), (212500, 16), jnp.float32)
        edge_attr_9 = -9.17853e-06 + 0.999947 * jax.random.normal(jax.random.fold_in(_gk, 12), (212500, 9), jnp.float32)
        edge_weight = -0.000152433 + 0.999798 * jax.random.normal(jax.random.fold_in(_gk, 14), (212500,), jnp.float32)
        edge_weight1 = 0.000614103 + 0.999867 * jax.random.normal(jax.random.fold_in(_gk, 15), (212500, 1), jnp.float32)
        return (x, src, dst, edge_attr_16, edge_attr_9, edge_weight, edge_weight1)
    x, src, dst, edge_attr_16, edge_attr_9, edge_weight, edge_weight1 = _rec_inputs()

    def _L0_gnn_setup():
        import jax, jax.numpy as jnp
        import numpy as np
        N_NODES = 6250
        N_EDGES = 80000
        IN_DIM = 128
        OUT_DIM = 128
        EDGE_DIM = 16
        N_HEADS = 4
        HEAD_DIM = OUT_DIM // N_HEADS
        LN_EPS = 1e-05

        def _layer_norm(x, scale, bias):
            mu = jnp.mean(x, axis=-1, keepdims=True)
            var = jnp.mean(jnp.square(x - mu), axis=-1, keepdims=True)
            return (x - mu) * jax.lax.rsqrt(var + LN_EPS) * scale + bias
        key = jax.random.key(seed)
        ks = jax.random.split(key, 6)
        h = jax.random.normal(ks[0], (N_NODES, IN_DIM), dtype=jnp.float32)
        edge_index = jax.random.randint(ks[1], (2, N_EDGES), 0, N_NODES, dtype=jnp.int64)
        edge_feat = jax.random.normal(ks[2], (N_EDGES, EDGE_DIM), dtype=jnp.float32)
        W = jax.random.normal(ks[3], (OUT_DIM, IN_DIM), dtype=jnp.float32) * (1.0 / np.sqrt(IN_DIM))
        W_e = jax.random.normal(ks[4], (N_HEADS, EDGE_DIM), dtype=jnp.float32) * (1.0 / np.sqrt(EDGE_DIM))
        a = jax.random.normal(ks[5], (N_HEADS, 2 * HEAD_DIM), dtype=jnp.float32) * (1.0 / np.sqrt(2 * HEAD_DIM))
        ln_scale = jnp.ones((OUT_DIM,), dtype=jnp.float32)
        ln_bias = jnp.zeros((OUT_DIM,), dtype=jnp.float32)
        return {'h': h, 'edge_index': edge_index, 'edge_feat': edge_feat, 'W': W, 'W_e': W_e, 'a': a, 'ln_scale': ln_scale, 'ln_bias': ln_bias}
    _L0_gnn_all = _L0_gnn_setup()
    _L0_gnn_in = {k: v for k, v in _L0_gnn_all.items() if k in ('W', 'W_e', 'a', 'ln_scale', 'ln_bias')}
    del _L0_gnn_all

    def _L1_gnn_setup():
        import jax, jax.numpy as jnp
        import numpy as np
        N_NODES = 6250
        N_EDGES = 100000
        HIDDEN = 128
        key = jax.random.key(seed)
        k1, k2, k3, k4, k5 = jax.random.split(key, 5)
        x_hidden = jax.random.normal(k1, (N_NODES, HIDDEN), dtype=jnp.float32)
        edge_index = jax.random.randint(k2, (2, N_EDGES), 0, N_NODES, dtype=jnp.int64)
        edge_attr = jax.random.normal(k3, (N_EDGES, 1), dtype=jnp.float32)
        lim = 1.0 / np.sqrt(HIDDEN)
        W = jax.random.uniform(k4, (HIDDEN, HIDDEN), minval=-lim, maxval=lim, dtype=jnp.float32)
        b = jax.random.uniform(k5, (HIDDEN,), minval=-lim, maxval=lim, dtype=jnp.float32)
        return {'x_hidden': x_hidden, 'edge_index': edge_index, 'edge_attr': edge_attr, 'W': W, 'b': b}
    _L1_gnn_all = _L1_gnn_setup()
    _L1_gnn_in = {k: v for k, v in _L1_gnn_all.items() if k in ('W', 'b')}
    del _L1_gnn_all

    def _L2_gnn_setup():
        import jax, jax.numpy as jnp
        import numpy as np
        import math
        IRREPS_IN = [(32, 0), (32, 1)]
        IRREPS_SH = [(1, 0), (1, 1), (1, 2)]
        IRREPS_OUT = [(32, 0), (32, 1)]
        PATHS = [(0, 0, 0), (0, 1, 1), (1, 0, 1), (1, 1, 0), (1, 2, 1)]
        NUM_NODES = 6250
        NUM_EDGES = 100000

        def _fact(n):
            return math.factorial(int(round(n)))

        def _su2_cg(j1, j2, j3):
            C = np.zeros((2 * j1 + 1, 2 * j2 + 1, 2 * j3 + 1))
            for m1 in range(-j1, j1 + 1):
                for m2 in range(-j2, j2 + 1):
                    m3 = m1 + m2
                    if abs(m3) > j3:
                        continue
                    vmin = int(max(-j1 + j2 + m3, -j1 + m1, 0))
                    vmax = int(min(j2 + j3 + m1, j3 - j1 + j2, j3 + m3))
                    c = math.sqrt((2 * j3 + 1) * _fact(j3 + j1 - j2) * _fact(j3 - j1 + j2) * _fact(j1 + j2 - j3) / _fact(j1 + j2 + j3 + 1))
                    c *= math.sqrt(_fact(j3 + m3) * _fact(j3 - m3) * _fact(j1 - m1) * _fact(j1 + m1) * _fact(j2 - m2) * _fact(j2 + m2))
                    s = 0.0
                    for v in range(vmin, vmax + 1):
                        s += (-1.0) ** (v + j2 + m2) * _fact(j2 + j3 + m1 - v) * _fact(j1 - m1 + v) / (_fact(v) * _fact(j3 - j1 + j2 - v) * _fact(j3 + m3 - v) * _fact(v + j1 - j2 - m3))
                    C[j1 + m1, j2 + m2, j3 + m3] = c * s
            return C

        def _q(l):
            q = np.zeros((2 * l + 1, 2 * l + 1), dtype=np.complex128)
            for m in range(-l, 0):
                q[l + m, l + abs(m)] = 1.0 / np.sqrt(2.0)
                q[l + m, l - abs(m)] = -1j / np.sqrt(2.0)
            q[l, l] = 1.0
            for m in range(1, l + 1):
                q[l + m, l + abs(m)] = (-1.0) ** m / np.sqrt(2.0)
                q[l + m, l - abs(m)] = 1j * (-1.0) ** m / np.sqrt(2.0)
            return (-1j) ** l * q

        def _real_cg(l1, l2, l3):
            C = _su2_cg(l1, l2, l3).astype(np.complex128)
            C = np.einsum('ij,kl,mn,ikn->jlm', _q(l1), _q(l2), np.conj(_q(l3).T), C)
            C = np.real(C)
            return (C / np.linalg.norm(C)).astype(np.float32)
        CG = [jnp.asarray(_real_cg(IRREPS_IN[i1][1], IRREPS_SH[i2][1], IRREPS_OUT[io][1])) for i1, i2, io in PATHS]
        N_PATHS_TO_OUT = {io: sum((1 for p in PATHS if p[2] == io)) for io in range(len(IRREPS_OUT))}

        def _split(x, irreps):
            blocks, off = ([], 0)
            for mul, l in irreps:
                d = mul * (2 * l + 1)
                blocks.append(x[:, off:off + d].reshape(x.shape[0], mul, 2 * l + 1))
                off += d
            return blocks
        key = jax.random.key(seed)
        k1, k2, k3, k4 = jax.random.split(key, 4)
        in_dim = sum((m * (2 * l + 1) for m, l in IRREPS_IN))
        sh_dim = sum((m * (2 * l + 1) for m, l in IRREPS_SH))
        features = jax.random.normal(k1, (NUM_NODES, in_dim), dtype=jnp.float32)
        edge_sh = jax.random.normal(k2, (NUM_EDGES, sh_dim), dtype=jnp.float32)
        edge_index = jax.random.randint(k3, (2, NUM_EDGES), 0, NUM_NODES, dtype=jnp.int32)
        weights = jax.random.normal(k4, (len(PATHS), 32, 32), dtype=jnp.float32)
        return {'features': features, 'edge_sh': edge_sh, 'edge_index': edge_index, 'weights': weights}
    _L2_gnn_all = _L2_gnn_setup()
    _L2_gnn_in = {k: v for k, v in _L2_gnn_all.items() if k in ('weights',)}
    del _L2_gnn_all

    def _L3_gnn_setup():
        import jax, jax.numpy as jnp
        import numpy as np
        N_NODES = 12500
        N_EDGES = 80000
        D = 128
        BN_EPS = 1e-05
        key = jax.random.key(seed)
        ks = jax.random.split(key, 8)
        scale = 1.0 / np.sqrt(D)
        x = jax.random.normal(ks[0], (N_NODES, D), jnp.float32)
        edge_index = jax.random.randint(ks[1], (2, N_EDGES), 0, N_NODES, jnp.int32)
        edge_attr = jax.random.normal(ks[2], (N_EDGES,), jnp.float32)
        W_l = jax.random.normal(ks[3], (D, D), jnp.float32) * scale
        b_l = jnp.zeros((D,), jnp.float32)
        W_r = jax.random.normal(ks[4], (D, D), jnp.float32) * scale
        gamma = jnp.ones((D,), jnp.float32)
        beta = jnp.zeros((D,), jnp.float32)
        return {'x': x, 'edge_attr': edge_attr, 'W_l': W_l, 'b_l': b_l, 'W_r': W_r, 'gamma': gamma, 'beta': beta, 'edge_index': edge_index}
    _L3_gnn_all = _L3_gnn_setup()
    _L3_gnn_in = {k: v for k, v in _L3_gnn_all.items() if k in ('W_l', 'b_l', 'W_r', 'gamma', 'beta')}
    del _L3_gnn_all
    return {'x': x, 'src': src, 'dst': dst, 'edge_attr_16': edge_attr_16, 'edge_attr_9': edge_attr_9, 'edge_weight': edge_weight, 'edge_weight1': edge_weight1, 'L0_gnn_W': _L0_gnn_in['W'], 'L0_gnn_W_e': _L0_gnn_in['W_e'], 'L0_gnn_a': _L0_gnn_in['a'], 'L0_gnn_ln_scale': _L0_gnn_in['ln_scale'], 'L0_gnn_ln_bias': _L0_gnn_in['ln_bias'], 'L1_gnn_W': _L1_gnn_in['W'], 'L1_gnn_b': _L1_gnn_in['b'], 'L2_gnn_weights': _L2_gnn_in['weights'], 'L3_gnn_W_l': _L3_gnn_in['W_l'], 'L3_gnn_b_l': _L3_gnn_in['b_l'], 'L3_gnn_W_r': _L3_gnn_in['W_r'], 'L3_gnn_gamma': _L3_gnn_in['gamma'], 'L3_gnn_beta': _L3_gnn_in['beta']}

def reference(x, src, dst, edge_attr_16, edge_attr_9, edge_weight, edge_weight1, L0_gnn_W, L0_gnn_W_e, L0_gnn_a, L0_gnn_ln_scale, L0_gnn_ln_bias, L1_gnn_W, L1_gnn_b, L2_gnn_weights, L3_gnn_W_l, L3_gnn_b_l, L3_gnn_W_r, L3_gnn_gamma, L3_gnn_beta):
    import jax
    import jax.numpy as jnp

    def _L0_gnn_ref(h, edge_index, edge_feat, W, W_e, a, ln_scale, ln_bias):
        import jax, jax.numpy as jnp
        import numpy as np
        N_NODES = 6250
        N_EDGES = 80000
        IN_DIM = 128
        OUT_DIM = 128
        EDGE_DIM = 16
        N_HEADS = 4
        HEAD_DIM = OUT_DIM // N_HEADS
        LN_EPS = 1e-05

        def _layer_norm(x, scale, bias):
            mu = jnp.mean(x, axis=-1, keepdims=True)
            var = jnp.mean(jnp.square(x - mu), axis=-1, keepdims=True)
            return (x - mu) * jax.lax.rsqrt(var + LN_EPS) * scale + bias
        N = h.shape[0]
        H, D = (N_HEADS, HEAD_DIM)
        src, dst = (edge_index[0], edge_index[1])
        Wh = (h @ W.T).reshape(N, H, D)
        Wh_src = Wh[src]
        Wh_dst = Wh[dst]
        attn = (jnp.concatenate([Wh_src, Wh_dst], axis=-1) * a[None]).sum(-1)
        attn = jax.nn.leaky_relu(attn, negative_slope=0.2)
        attn = attn + edge_feat @ W_e.T
        max_v = jax.ops.segment_max(attn, dst, num_segments=N)
        max_v = jnp.maximum(max_v, -1000000000.0)
        exp_v = jnp.exp(attn - max_v[dst])
        denom = jax.ops.segment_sum(exp_v, dst, num_segments=N)
        alpha = exp_v / (denom[dst] + 1e-09)
        agg = jax.ops.segment_sum(alpha[..., None] * Wh_src, dst, num_segments=N)
        out = agg.reshape(N, H * D)
        return _layer_norm(jax.nn.gelu(out, approximate=False), ln_scale, ln_bias)

    def _L1_gnn_ref(x_hidden, edge_index, edge_attr, W, b):
        import jax, jax.numpy as jnp
        import numpy as np
        N_NODES = 6250
        N_EDGES = 100000
        HIDDEN = 128
        src, dst = (edge_index[0], edge_index[1])
        msg = x_hidden[src] * edge_attr[:, 0:1]
        agg = jax.ops.segment_sum(msg, dst, num_segments=x_hidden.shape[0])
        h = jax.nn.gelu(agg)
        return jax.nn.gelu(h @ W.T + b)

    def _L2_gnn_ref(features, edge_sh, edge_index, weights):
        import jax, jax.numpy as jnp
        import numpy as np
        import math
        IRREPS_IN = [(32, 0), (32, 1)]
        IRREPS_SH = [(1, 0), (1, 1), (1, 2)]
        IRREPS_OUT = [(32, 0), (32, 1)]
        PATHS = [(0, 0, 0), (0, 1, 1), (1, 0, 1), (1, 1, 0), (1, 2, 1)]
        NUM_NODES = 6250
        NUM_EDGES = 100000

        def _fact(n):
            return math.factorial(int(round(n)))

        def _su2_cg(j1, j2, j3):
            C = np.zeros((2 * j1 + 1, 2 * j2 + 1, 2 * j3 + 1))
            for m1 in range(-j1, j1 + 1):
                for m2 in range(-j2, j2 + 1):
                    m3 = m1 + m2
                    if abs(m3) > j3:
                        continue
                    vmin = int(max(-j1 + j2 + m3, -j1 + m1, 0))
                    vmax = int(min(j2 + j3 + m1, j3 - j1 + j2, j3 + m3))
                    c = math.sqrt((2 * j3 + 1) * _fact(j3 + j1 - j2) * _fact(j3 - j1 + j2) * _fact(j1 + j2 - j3) / _fact(j1 + j2 + j3 + 1))
                    c *= math.sqrt(_fact(j3 + m3) * _fact(j3 - m3) * _fact(j1 - m1) * _fact(j1 + m1) * _fact(j2 - m2) * _fact(j2 + m2))
                    s = 0.0
                    for v in range(vmin, vmax + 1):
                        s += (-1.0) ** (v + j2 + m2) * _fact(j2 + j3 + m1 - v) * _fact(j1 - m1 + v) / (_fact(v) * _fact(j3 - j1 + j2 - v) * _fact(j3 + m3 - v) * _fact(v + j1 - j2 - m3))
                    C[j1 + m1, j2 + m2, j3 + m3] = c * s
            return C

        def _q(l):
            q = np.zeros((2 * l + 1, 2 * l + 1), dtype=np.complex128)
            for m in range(-l, 0):
                q[l + m, l + abs(m)] = 1.0 / np.sqrt(2.0)
                q[l + m, l - abs(m)] = -1j / np.sqrt(2.0)
            q[l, l] = 1.0
            for m in range(1, l + 1):
                q[l + m, l + abs(m)] = (-1.0) ** m / np.sqrt(2.0)
                q[l + m, l - abs(m)] = 1j * (-1.0) ** m / np.sqrt(2.0)
            return (-1j) ** l * q

        def _real_cg(l1, l2, l3):
            C = _su2_cg(l1, l2, l3).astype(np.complex128)
            C = np.einsum('ij,kl,mn,ikn->jlm', _q(l1), _q(l2), np.conj(_q(l3).T), C)
            C = np.real(C)
            return (C / np.linalg.norm(C)).astype(np.float32)
        CG = [jnp.asarray(_real_cg(IRREPS_IN[i1][1], IRREPS_SH[i2][1], IRREPS_OUT[io][1])) for i1, i2, io in PATHS]
        N_PATHS_TO_OUT = {io: sum((1 for p in PATHS if p[2] == io)) for io in range(len(IRREPS_OUT))}

        def _split(x, irreps):
            blocks, off = ([], 0)
            for mul, l in irreps:
                d = mul * (2 * l + 1)
                blocks.append(x[:, off:off + d].reshape(x.shape[0], mul, 2 * l + 1))
                off += d
            return blocks
        src, dst = (edge_index[0], edge_index[1])
        x1 = _split(features[src], IRREPS_IN)
        x2 = _split(edge_sh, IRREPS_SH)
        out_blocks = [None] * len(IRREPS_OUT)
        for p, (i1, i2, io) in enumerate(PATHS):
            u, v = (IRREPS_IN[i1][0], IRREPS_SH[i2][0])
            alpha = 1.0 / math.sqrt(u * v * N_PATHS_TO_OUT[io])
            tmp = jnp.einsum('eui,ej,ijk->euk', x1[i1], x2[i2][:, 0, :], CG[p])
            msg = jnp.einsum('euk,uw->ewk', tmp, weights[p]) * alpha
            out_blocks[io] = msg if out_blocks[io] is None else out_blocks[io] + msg
        E = edge_sh.shape[0]
        msgs = jnp.concatenate([b.reshape(E, -1) for b in out_blocks], axis=1)
        out = jnp.zeros((features.shape[0], msgs.shape[1]), dtype=features.dtype)
        return out.at[dst].add(msgs)

    def _L3_gnn_ref(x, edge_attr, W_l, b_l, W_r, gamma, beta, edge_index):
        import jax, jax.numpy as jnp
        import numpy as np
        N_NODES = 12500
        N_EDGES = 80000
        D = 128
        BN_EPS = 1e-05
        n = x.shape[0]
        h = jax.nn.relu(x)
        src, dst = (edge_index[0], edge_index[1])
        msg = h[src]
        agg = jax.ops.segment_sum(msg, dst, num_segments=n)
        cnt = jax.ops.segment_sum(jnp.ones((msg.shape[0], 1), h.dtype), dst, num_segments=n)
        mean_agg = agg / jnp.maximum(cnt, 1.0)
        out = mean_agg @ W_l.T + b_l + h @ W_r.T
        mu = jnp.mean(out, axis=0)
        var = jnp.mean(jnp.square(out - mu), axis=0)
        xhat = (out - mu) * jax.lax.rsqrt(var + BN_EPS)
        return xhat * gamma + beta
    edge_index = jnp.stack([src, dst])
    h = jnp.maximum(_layernorm(x, axis=-1), 0.0)
    x = x + _L0_gnn_ref(h, edge_index, edge_attr_16, L0_gnn_W, L0_gnn_W_e, L0_gnn_a, L0_gnn_ln_scale, L0_gnn_ln_bias)
    h = jnp.maximum(_layernorm(x, axis=-1), 0.0)
    x = x + _L1_gnn_ref(h, edge_index, edge_weight1, L1_gnn_W, L1_gnn_b)
    h = jnp.maximum(_layernorm(x, axis=-1), 0.0)
    x = x + _L2_gnn_ref(h, edge_attr_9, edge_index, L2_gnn_weights)
    h = jnp.maximum(_layernorm(x, axis=-1), 0.0)
    x = x + _L3_gnn_ref(h, edge_weight, L3_gnn_W_l, L3_gnn_b_l, L3_gnn_W_r, L3_gnn_gamma, L3_gnn_beta, edge_index)
    return x

_drawn_inputs = setup_inputs


def setup_inputs(seed=0):
    import zlib

    import numpy as np

    out = dict(_drawn_inputs(seed))
    spreads = {'L0_gnn_ln_scale': (1.0, 0.2),
     'L0_gnn_ln_bias': (0.0, 0.1),
     'L3_gnn_b_l': (0.0, 0.8),
     'L3_gnn_gamma': (1.0, 0.2),
     'L3_gnn_beta': (0.0, 0.1)}
    factors = {'L1_gnn_b': 2.789}
    for name, (base, spread) in spreads.items():
        noise = np.random.default_rng([zlib.crc32(name.encode()), seed]).standard_normal(out[name].shape)
        drawn = base * np.exp(spread * noise) if base else spread * noise
        out[name] = jnp.asarray(drawn.astype(out[name].dtype))
    for name, factor in factors.items():
        out[name] = (out[name] * factor).astype(out[name].dtype)
    return out
```

```python
import math
from contextlib import ExitStack

import numpy as np
import concourse.bass as bass
from concourse import mybir

ALU = mybir.AluOpType
ACT = mybir.ActivationFunctionType
AX = mybir.AxisListType.X
F32 = mybir.dt.float32
BF16 = mybir.dt.bfloat16
I32 = mybir.dt.int32
ds = bass.ds

P = 128
N = 12500
E = 212500
D = 128
H = 4
HD = D // H
G = 8
NCH = -(-E // (P * G))
T = (NCH + 1) * G
NB = -(-N // P)
NP = NB * P
NW = NP + P
BATCH = 7
STEPS = NB // BATCH
BC = BATCH * P
HC = BC // 2
PG = 1024
PAGES = -(-NCH * NB // PG)
DW = D + H
BIG = float(2.0 ** 100)
FAR = float(1 << 20)
EPS = 1e-5
NSH = 16
PAGE_LINKS = 11
TW = 352
assert NB % BATCH == 0 and NCH < 2 * P and G * P * NCH >= E


def clebsch_gordan():
    def fact(n):
        return math.factorial(int(round(n)))

    def su2(j1, j2, j3):
        c3 = np.zeros((2 * j1 + 1, 2 * j2 + 1, 2 * j3 + 1))
        for m1 in range(-j1, j1 + 1):
            for m2 in range(-j2, j2 + 1):
                m3 = m1 + m2
                if abs(m3) > j3:
                    continue
                vmin = int(max(-j1 + j2 + m3, -j1 + m1, 0))
                vmax = int(min(j2 + j3 + m1, j3 - j1 + j2, j3 + m3))
                c = math.sqrt((2 * j3 + 1) * fact(j3 + j1 - j2) * fact(j3 - j1 + j2) * fact(j1 + j2 - j3)
                              / fact(j1 + j2 + j3 + 1))
                c *= math.sqrt(fact(j3 + m3) * fact(j3 - m3) * fact(j1 - m1) * fact(j1 + m1)
                               * fact(j2 - m2) * fact(j2 + m2))
                s = 0.0
                for v in range(vmin, vmax + 1):
                    s += (-1.0) ** (v + j2 + m2) * fact(j2 + j3 + m1 - v) * fact(j1 - m1 + v) / (
                        fact(v) * fact(j3 - j1 + j2 - v) * fact(j3 + m3 - v) * fact(v + j1 - j2 - m3))
                c3[j1 + m1, j2 + m2, j3 + m3] = c * s
        return c3

    def basis(l):
        q = np.zeros((2 * l + 1, 2 * l + 1), dtype=np.complex128)
        for m in range(-l, 0):
            q[l + m, l + abs(m)] = 1.0 / np.sqrt(2.0)
            q[l + m, l - abs(m)] = -1j / np.sqrt(2.0)
        q[l, l] = 1.0
        for m in range(1, l + 1):
            q[l + m, l + abs(m)] = (-1.0) ** m / np.sqrt(2.0)
            q[l + m, l - abs(m)] = 1j * (-1.0) ** m / np.sqrt(2.0)
        return (-1j) ** l * q

    out = []
    for l1, l2, l3 in [(0, 0, 0), (0, 1, 1), (1, 0, 1), (1, 1, 0), (1, 2, 1)]:
        c = np.einsum("ij,kl,mn,ikn->jlm", basis(l1), basis(l2), np.conj(basis(l3).T), su2(l1, l2, l3))
        c = np.real(c)
        out.append((c / np.linalg.norm(c)).astype(np.float32))
    return out


class Event:

    def __init__(self, sem, per=1):
        self.sem, self.per, self.credit = sem, per, 2 * per

    def start(self, eng):
        eng.sem_inc(self.sem, self.credit)

    def wait(self, eng, v, k=None):
        eng.wait_ge(self.sem, v * self.per + (self.credit + (self.per if k is None else k)))


class Chain:

    def __init__(self, eng, sem, base=0):
        self.eng, self.sem, self.base, self.n = eng, sem, base, 0

    def __call__(self, ins):
        self.n += 1
        ins.then_inc(self.sem, 1)
        self.eng.wait_ge(self.sem, self.base + self.n)


def phase_semaphores(nc, ctx, prefix):
    made = []

    def give_back():
        nc.clear_and_free_semaphores(made)
        nc.all_engine_barrier()

    ctx.callback(give_back)

    def sem(name):
        made.append(nc.alloc_semaphore(prefix + name))
        return made[-1]

    return sem


def build(nc, x, src, dst, w1e, sh, ef, W0, W0T, WeT, aT, ln_scale, ln_bias, W1T, b1, W2b, W2scale,
          WlT, bl, WrT, gamma, beta, ident, iota, out):
    CG = clebsch_gordan()
    outer = ExitStack()

    def dram(name, shape, dt=F32):
        return nc.dram_tensor(name, shape, dt).ap()

    table0 = dram("table0", [NP, DW])
    table1 = dram("table1", [NP, D])
    table2 = dram("table2", [NP, D])
    table3 = dram("table3", [NP, D])
    x1 = dram("x1", [NP, D])
    x2 = dram("x2", [NP, D])
    x3 = dram("x3", [NP, D])
    shx = dram("shx", [P, T * NSH])
    visit_base = dram("visit_base", [PAGES, PG])
    visit_pair = dram("visit_pair", [PAGES, 2 * PG], I32)

    with outer:
        def psb(name, shape, dt=F32):
            return outer.enter_context(nc.sbuf_tensor(name, shape, dt))

        sums = psb("sums", [P, NW])
        aux = psb("aux", [P, NW])
        dstf = psb("dstf", [P, T])
        srci = psb("srci", [P, T], I32)
        identf = psb("identf", [P, P])
        iotaf = psb("iotaf", [P, P])
        epsc = psb("epsc", [P, 1])
        meta = psb("meta", [1, 32], I32)
        pairs = psb("pairs", [1, 2 * PG], I32)
        baseB = psb("baseB", [P, PG])

        phase_visits(nc, dst, src, ident, iota, dstf, srci, identf, iotaf, epsc, meta, sums, aux,
                     visit_base, visit_pair)
        env = (nc, dstf, srci, identf, iotaf, epsc, meta, pairs, baseB, sums, aux, visit_base, visit_pair)
        with nc.sbuf_tensor("efw", [P, T * H], F32) as efw:
            phase_first_table(env, x, W0, W0T, aT, WeT, ef, efw, table0)
            phase_attention(env, efw, table0)
        phase_node(env, 0, x, x1, table1, dict(scale=ln_scale, bias=ln_bias))
        phase_sum(env, 1, table1, w1e)
        phase_node(env, 1, x1, x2, table2, dict(W=W1T, b=b1))
        phase_factors(env, sh, shx, CG)
        phase_tensor_product(env, table2, shx, W2b, W2scale)
        phase_node(env, 2, x2, x3, table3, {})
        phase_sum(env, 3, table3, None)
        phase_last(env, x3, table3, WlT, WrT, bl, gamma, beta, out)



def phase_visits(nc, dst, src, ident, iota, dstf, srci, identf, iotaf, epsc, meta, sums, aux,
                 visit_base, visit_pair):
    with ExitStack() as ctx:
        sb = lambda n, s, d=F32: ctx.enter_context(nc.sbuf_tensor(n, s, d))
        ps = lambda n, s, d=F32: ctx.enter_context(nc.psum_tensor(n, s, d))
        sem = phase_semaphores(nc, ctx, "")
        CP = 2 * P
        dsti = sb("v_dsti", [P, T], I32)
        dpos = sb("v_dpos", [P, T])
        hi = sb("v_hi", [P, CP])
        lo = sb("v_lo", [P, CP])
        k0 = sb("v_k0", [P, PG])
        kcur = sb("v_kcur", [P, PG])
        ind = sb("v_ind", [P, 2, PG])
        tmp = sb("v_tmp", [P, PG])
        ones = sb("v_ones", [P, P])
        tri = sb("v_tri", [P, P])
        st = sb("v_st", [P, 32])
        sti = sb("v_sti", [P, 2], I32)
        ki = sb("v_ki", [1, 2], I32)
        kf = sb("v_kf", [1, 64])
        vb = sb("v_vb", [P, 4, P])
        baserow = sb("v_baserow", [P, PG])
        tilerow = sb("v_tilerow", [P, PG])
        pairrow = sb("v_pairrow", [1, PG, 2], I32)
        pt = ps("v_pt", [P, 4, P])
        pc = ps("v_pc", [P, 512])
        pbase = ps("v_pbase", [P, PG])
        ptile = ps("v_ptile", [P, PG])
        loaded, chain, red, turned, mm, mmd, pgd, pgm, stored, metac = (
            sem(n) for n in ("v_loaded", "v_chain", "v_red", "v_turned", "v_mm", "v_mmd", "v_pgd", "v_pgm",
                             "v_stored", "v_metac"))
        freed, chain2 = sem("v_freed"), sem("v_chain2")
        HI, LO, CNT, IDX, CUM, END, VAL, PRE = (slice(2 * i, 2 * i + 2) for i in range(8))

        with nc.Block() as block:
            @block.sync
            def _(sp):
                sp.dma_start(dsti[:], dst).then_inc(loaded, 16)
                sp.dma_start(srci[:], src).then_inc(loaded, 16)
                sp.dma_start(identf[:], ident).then_inc(loaded, 16)
                sp.dma_start(iotaf[:], iota[:, 0:P]).then_inc(loaded, 16)
                sp.dma_start(k0[:], iota).then_inc(loaded, 16)
                sp.wait_ge(metac, 1)
                npages = sp.value_load(meta[0:1, 0:1], min_val=1, max_val=PAGES)
                with sp.Fori(0, npages) as pg:
                    sp.wait_ge(pgd, pg + 1)
                    sp.dma_start(visit_base[ds(pg, 1), :], baserow[0:1, :]).then_inc(stored, 16)
                    sp.dma_start(visit_pair[ds(pg, 1), :], pairrow[:].rearrange("o k c -> o (k c)")).then_inc(stored, 16)
                    sp.wait_ge(stored, pg * 32 + 32)
                    sp.sem_inc(freed, 1)

            @block.tensor
            def _(pe):
                pe.wait_ge(red, 1)
                pe.wait_ge(loaded, 80)
                for j in range(2):
                    pe.transpose(pt[:, j, :], hi[:, j * P:(j + 1) * P], identf[:])
                    ins = pe.transpose(pt[:, 2 + j, :], lo[:, j * P:(j + 1) * P], identf[:])
                ins.then_inc(turned, 1)
                pe.wait_ge(mm, 1)
                pe.matmul(pc[:, 0:2], tri[:], st[:, CNT], start=True, stop=False)
                pe.matmul(pc[:, 0:2], ones[:], st[:, PRE], start=False, stop=True).then_inc(mmd, 1)
                pe.wait_ge(mm, 2)
                pe.matmul(pc[:, 2:3], ones[:], st[:, 18:19], start=True, stop=True).then_inc(mmd, 1)
                pe.wait_ge(metac, 1)
                npages = pe.value_load(meta[0:1, 0:1], min_val=1, max_val=PAGES)
                with pe.Fori(0, npages) as pg:
                    pe.wait_ge(pgm, pg + 1)
                    for q in range(PG // 512):
                        c = slice(512 * q, 512 * q + 512)
                        for j in range(2):
                            pe.matmul(pbase[:, c], vb[:, j, :], ind[:, j, c], start=(j == 0), stop=(j == 1))
                        for j in range(2):
                            ins = pe.matmul(ptile[:, c], vb[:, 2 + j, :], ind[:, j, c], start=(j == 0), stop=(j == 1))
                    ins.then_inc(mmd, 1)

            @block.vector
            def _(dve):
                v = nc.vector
                c = Chain(dve, chain)
                v.memset(sums[:], 0.0)
                v.memset(aux[:], 0.0)
                v.memset(ones[:], 1.0)
                v.memset(epsc[:], EPS)
                v.memset(st[:], 0.0)
                v.memset(hi[:], 0.0)
                c(v.memset(lo[:], 0.0))
                c(v.memset(aux[0:H, :], -1e9))
                dve.wait_ge(loaded, 80)
                c(v.tensor_copy(dstf[:], dsti[:]))
                c(v.tensor_scalar(dpos[:], dstf[:], 0.0, FAR, ALU.is_lt, ALU.mult))
                c(v.tensor_tensor(dpos[:], dpos[:], dstf[:], ALU.add))
                c(v.tensor_reduce(hi[:, 0:NCH + 1], dstf[:].rearrange("p (c g) -> p c g", g=G), AX, ALU.max))
                v.tensor_reduce(lo[:, 0:NCH + 1], dpos[:].rearrange("p (c g) -> p c g", g=G), AX, ALU.min).then_inc(red, 1)
                dve.wait_ge(turned, 1)
                c(v.tensor_reduce(st[:, HI], pt[:, 0:2, :], AX, ALU.max))
                c(v.tensor_reduce(st[:, LO], pt[:, 2:4, :], AX, ALU.min))
                c(v.tensor_tensor(st[:, CNT], st[:, HI], st[:, LO], ALU.subtract))
                c(v.tensor_copy(sti[:], st[:, CNT]))
                c(v.tensor_single_scalar(sti[:], sti[:], 7, ALU.arith_shift_right))
                c(v.tensor_copy(st[:, CNT], sti[:]))
                c(v.tensor_tensor(tri[:], identf[:], iotaf[:], ALU.mult))
                c(v.tensor_reduce(st[:, 6:7], tri[:], AX, ALU.add))
                c(v.tensor_scalar(st[:, 7:8], st[:, 6:7], float(P), None, ALU.add))
                c(v.tensor_scalar(st[:, 16:18], st[:, IDX], float(NCH), None, ALU.is_lt))
                c(v.tensor_scalar(st[:, CNT], st[:, CNT], 1.0, None, ALU.add))
                c(v.tensor_tensor(st[:, CNT], st[:, CNT], st[:, 16:18], ALU.mult))
                c(v.tensor_scalar(st[:, 16:18], st[:, 16:18], -FAR, FAR, ALU.mult, ALU.add))
                c(v.tensor_tensor(st[:, CNT], st[:, CNT], st[:, 16:18], ALU.add))
                c(v.tensor_copy(st[:, PRE.start + 1:PRE.stop], st[:, CNT.start:CNT.start + 1]))
                v.tensor_scalar(tri[:], iotaf[:], st[:, 6:7], None, ALU.is_gt).then_inc(mm, 1)
                dve.wait_ge(mm, 1)
                dve.wait_ge(mmd, 1)
                c(v.tensor_copy(st[:, CUM], pc[:, 0:2]))
                c(v.tensor_tensor(st[:, END], st[:, CUM], st[:, CNT], ALU.add))
                c(v.tensor_scalar(st[:, 16:18], st[:, CUM], -float(P), None, ALU.mult))
                c(v.tensor_tensor(st[:, VAL], st[:, 16:18], st[:, LO], ALU.add))
                for j in range(2):
                    c(v.tensor_scalar(vb[:, j, :], ones[:], st[:, VAL.start + j:VAL.start + j + 1], None, ALU.mult))
                    c(v.tensor_scalar(vb[:, 2 + j, :], ones[:], st[:, IDX.start + j:IDX.start + j + 1], float(G),
                                      ALU.mult, ALU.mult))
                lr, lp = NCH % P, NCH // P
                v.tensor_scalar(st[:, 18:19], identf[:, lr:lr + 1], st[:, CUM.start + lp:CUM.start + lp + 1],
                                None, ALU.mult).then_inc(mm, 1)
                dve.wait_ge(mmd, 2)
                c(v.tensor_copy(ki[:, 0:1], pc[0:1, 2:3]))
                c(v.tensor_single_scalar(ki[:, 1:2], ki[:, 0:1], 1, ALU.bitwise_and))
                c(v.tensor_tensor(ki[:, 0:1], ki[:, 0:1], ki[:, 1:2], ALU.add))
                c(v.tensor_copy(kf[:, 0:1], ki[:, 0:1]))
                c(v.tensor_scalar(kf[:, 1:1 + PAGES], k0[0:1, 0:PAGES], -float(PG), kf[:, 0:1], ALU.mult, ALU.add))
                c(v.tensor_scalar(kf[:, 32:32 + PAGES], kf[:, 1:1 + PAGES], 0.0, None, ALU.is_gt))
                c(v.tensor_scalar(kf[:, 1:1 + PAGES], kf[:, 1:1 + PAGES], 4.0, float(PG), ALU.max, ALU.min))
                c(v.tensor_scalar(kf[:, 1:1 + PAGES], kf[:, 1:1 + PAGES], 0.5, -2.0, ALU.mult, ALU.add))
                c(v.tensor_reduce(kf[:, 0:1], kf[:, 32:32 + PAGES], AX, ALU.add))
                c(v.tensor_copy(meta[0:1, 0:1 + PAGES], kf[:, 0:1 + PAGES]))
                c(v.tensor_scalar(kcur[:], k0[:], -float(PG), None, ALU.add))
                dve.engine_nop().then_inc(metac, 1)
                dve.wait_ge(metac, 1)
                npages = dve.value_load(meta[0:1, 0:1], min_val=1, max_val=PAGES)
                with dve.Fori(0, npages) as pg:
                    c = Chain(dve, chain2, pg * PAGE_LINKS)
                    c(v.tensor_scalar(kcur[:], kcur[:], float(PG), None, ALU.add))
                    for j in range(2):
                        c(v.tensor_scalar(tmp[:], kcur[:], st[:, CUM.start + j:CUM.start + j + 1], None, ALU.is_ge))
                        c(v.scalar_tensor_tensor(out=ind[:, j, :], in0=kcur[:], scalar=st[:, END.start + j:END.start + j + 1],
                                                 in1=tmp[:], op0=ALU.is_lt, op1=ALU.mult))
                    dve.sem_inc(pgm, 1)
                    dve.wait_ge(mmd, pg + 3)
                    c(v.tensor_copy(tilerow[:], ptile[:]))
                    c(v.tensor_scalar(baserow[:], kcur[:], float(P), None, ALU.mult))
                    c(v.tensor_tensor(baserow[:], baserow[:], pbase[:], ALU.add))
                    c(v.tensor_scalar(baserow[:], baserow[:], 0.0, float(NP), ALU.max, ALU.min))
                    c(v.tensor_copy(pairrow[:, :, 0], tilerow[0:1, :]))
                    c(v.tensor_copy(pairrow[:, :, 1], baserow[0:1, :]))
                    assert c.n == PAGE_LINKS
                    dve.sem_inc(pgd, 1)
                    dve.wait_ge(freed, pg + 1)



class Visits:

    def __init__(self, env, sem):
        (self.nc, self.dstf, self.srci, self.identf, self.iotaf, self.epsc, self.meta, self.pairs, self.baseB,
         self.sums, self.aux, self.visit_base, self.visit_pair) = env
        self.page_loaded, self.page_done = sem("page_loaded"), sem("page_done")

    def serve(self, sp, users):
        npages = sp.value_load(self.meta[0:1, 0:1], min_val=1, max_val=PAGES)
        sp.sem_inc(self.page_done, 1)
        with sp.Fori(0, npages) as pg:
            sp.wait_ge(self.page_done, pg * users + 1)
            sp.dma_start(self.pairs[:], self.visit_pair[ds(pg, 1), :]).then_inc(self.page_loaded, 16)
            sp.dma_start(self.baseB[:], self.visit_base[ds(pg, 1), :].to_broadcast([P, PG])).then_inc(self.page_loaded, 16)

    def loop(self, eng, body):
        npages = eng.value_load(self.meta[0:1, 0:1], min_val=1, max_val=PAGES)
        with eng.Fori(0, npages) as pg:
            eng.wait_ge(self.page_loaded, pg * 32 + 32)
            count = eng.value_load(self.meta[0:1, ds(pg + 1, 1)], min_val=0, max_val=PG // 2 - 2) + 2
            with eng.Fori(0, count) as half:
                i = half * 2
                for r in range(2):
                    body(i + r, r, pg * PG + i + r)
            eng.drain().then_inc(self.page_done, 1)

    def lagged(self, eng, first, second):
        npages = eng.value_load(self.meta[0:1, 0:1], min_val=1, max_val=PAGES)
        with eng.Fori(0, npages) as pg:
            eng.wait_ge(self.page_loaded, pg * 32 + 32)
            count = eng.value_load(self.meta[0:1, ds(pg + 1, 1)], min_val=0, max_val=PG // 2 - 2) + 2
            first(0, 0, pg * PG)
            with eng.Fori(0, count - 1) as half:
                i = half * 2
                for r in range(2):
                    first(i + r + 1, 1 - r, pg * PG + i + r + 1)
                    second(i + r, r, pg * PG + i + r)
            last = count * 2 - 1
            first(last, 1, pg * PG + last)
            second(last - 1, 0, pg * PG + last - 1)
            second(last, 1, pg * PG + last)
            eng.drain().then_inc(self.page_done, 1)

    def pair(self, eng, i):
        regs = [eng.alloc_register(f"pair{k}_{self.nc.next_id()}") for k in range(2)]
        eng.load(regs, self.pairs[0:1, ds(i * 2, 2)])
        tile = eng.snap(regs[0], min_val=0, max_val=T - G)
        node = eng.snap(regs[1], min_val=0, max_val=NP)
        return tile, node


def gather_rows(vis, pool, table, width, slots, rows, copied, landed, free):
    g = vis.nc.gpsimd
    copied.start(pool)

    def visit(i, r, v):
        tile, _ = vis.pair(pool, i)
        free.wait(pool, v - 2)
        g.tensor_copy(slots[:, r * G:(r + 1) * G], vis.srci[:, ds(tile, G)]).then_inc(copied.sem, 1)
        copied.wait(pool, v)
        g.nop(nofuse=True)
        for t in range(G):
            g.indirect_dma_start(rows[:, r, t, 0:width], None, table,
                                 bass.IndirectOffsetOnAxis(slots[:, r * G + t:r * G + t + 1], 0)).then_inc(landed[r], 16)

    vis.loop(pool, visit)


def norm_vector(nc, dve, c, ev, it, k, xin, xc, sq, s):
    v = nc.vector
    c(v.tensor_reduce(s[:, 0:BATCH], xin, AX, ALU.add))
    c(v.tensor_scalar(s[:, 8:8 + BATCH], s[:, 0:BATCH], -1.0 / D, None, ALU.mult))
    v.tensor_tensor(xc, xin, s[:, 8:8 + BATCH].unsqueeze(2).to_broadcast([P, BATCH, D]), ALU.add).then_inc(ev["centred"].sem, 1)
    ev["squared"].wait(dve, it, k)
    v.tensor_reduce(s[:, 16:16 + BATCH], sq, AX, ALU.add).then_inc(ev["varied"].sem, 1)
    ev["rooted"].wait(dve, it, k)
    c(v.reciprocal(s[:, 32:32 + BATCH], s[:, 24:24 + BATCH]))
    c(v.tensor_tensor(xc, xc, s[:, 32:32 + BATCH].unsqueeze(2).to_broadcast([P, BATCH, D]), ALU.mult))


def norm_scalar(nc, act, ev, it, k, xc, sq, s, epsc):
    ev["centred"].wait(act, it, k)
    nc.scalar.activation(sq, xc, ACT.Square).then_inc(ev["squared"].sem, 1)
    ev["varied"].wait(act, it, k)
    nc.scalar.activation(s[:, 24:24 + BATCH], s[:, 16:16 + BATCH], ACT.Sqrt, bias=epsc[:], scale=1.0 / D).then_inc(ev["rooted"].sem, 1)


def blocks_of(table, it):
    return table.rearrange("(b p) f -> p b f", p=P)[:, ds(it * BATCH, BATCH), :]


def load_blocks(nc, pool, streams, used):
    with pool.Fori(0, STEPS // 2) as half:
        i = half * 2
        for r in range(2):
            used.wait(pool, i + r - 2)
            pool.nop(nofuse=True)
            for table, slot, landed in streams:
                pool.dma_start(slot[:, r], blocks_of(table, i + r)).then_inc(landed[r], 16)



def phase_first_table(env, x, W0, W0T, aT, WeT, ef, efw, table0):
    nc, dstf, srci, identf, iotaf, epsc, meta, pairs, baseB, sums, aux, visit_base, visit_pair = env
    with ExitStack() as ctx:
        sb = lambda n, s, d=F32: ctx.enter_context(nc.sbuf_tensor(n, s, d))
        ps = lambda n, s, d=F32: ctx.enter_context(nc.psum_tensor(n, s, d))
        sem = phase_semaphores(nc, ctx, "")
        w0 = sb("t_w0", [P, D])
        wext = sb("t_wext", [P, DW])
        asrc = sb("t_asrc", [P, H])
        adst = sb("t_adst", [P, 36])
        wad = sb("t_wad", [P, 36])
        we = sb("t_we", [P, G * H])
        xin = sb("t_xin", [P, 2, BATCH, D])
        xc = sb("t_xc", [P, BATCH, D])
        sq = sb("t_sq", [P, BATCH, D])
        s = sb("t_s", [P, 40])
        hT = sb("t_hT", [P, BC])
        row = sb("t_row", [P, BATCH, DW])
        eft = sb("t_eft", [P, 2, P])
        pT = ps("t_pT", [P, 1024])
        pw = ps("t_pw", [P, 3, 512])
        pd = ps("t_pd", [P, 2, 512])
        pe_ = ps("t_pe", [P, 512])
        loaded, zeroed, placed, wready = (sem(n) for n in ("t_loaded", "t_zeroed", "t_placed", "t_wready"))
        xl = [sem("t_xl0"), sem("t_xl1")]
        stored, efl0, efl1, chain = sem("t_stored"), sem("t_efl0"), sem("t_efl1"), sem("t_chain")
        efl = [efl0, efl1]
        ev = {n: Event(sem("t_" + n)) for n in
              ("centred", "squared", "varied", "rooted", "normed", "turned", "copied", "projected", "rowed", "ef_mm", "ef_out", "kept")}

        with nc.Block() as block:
            @block.sync
            def _(sp):
                sp.dma_start(w0[:], W0).then_inc(loaded, 16)
                sp.dma_start(wext[:, 0:D], W0T).then_inc(loaded, 16)
                sp.wait_ge(zeroed, 1)
                with nc.allow_non_contiguous_dma(reason="attention vectors and W_e into block diagonals"):
                    for h in range(H):
                        sp.dma_start(asrc[h * HD:(h + 1) * HD, h:h + 1], aT[0:HD, h:h + 1]).then_inc(placed, 16)
                        sp.dma_start(adst[h * HD:(h + 1) * HD, 32 + h:33 + h], aT[HD:2 * HD, h:h + 1]).then_inc(placed, 16)
                    for t in range(G):
                        sp.dma_start(we[16 * t:16 * t + 16, H * t:H * t + H], WeT).then_inc(placed, 16)
                ev["kept"].start(sp)
                with sp.Fori(0, STEPS) as it:
                    ev["rowed"].wait(sp, it)
                    sp.dma_start(blocks_of(table0, it), row[:]).then_inc(stored, 16)
                    sp.wait_ge(stored, it * 16 + 16)
                    sp.sem_inc(ev["kept"].sem, 1)

            @block.gpsimd
            def _(pool):
                load_blocks(nc, pool, ((x, xin, xl),), ev["centred"])
                with pool.Fori(0, NCH // 2) as half:
                    i = half * 2
                    for r in range(2):
                        ev["ef_mm"].wait(pool, i + r - 2)
                        pool.nop(nofuse=True)
                        pool.dma_start(eft[:, r], ef[ds(i + r, 1)].rearrange("o p e -> (o p) e")).then_inc(efl[r], 16)

            @block.tensor
            def _(pe):
                for n in ("turned", "projected", "ef_mm"):
                    ev[n].start(pe)
                pe.wait_ge(loaded, 32)
                pe.wait_ge(placed, 16 * (2 * H + G))
                pe.matmul(pe_[:, 0:H], w0[:], asrc[:], start=True, stop=True)
                pe.matmul(pe_[:, 64:100], w0[:], adst[:], start=True, stop=True).then_inc(wready, 1)
                pe.wait_ge(wready, 2)
                with pe.Fori(0, STEPS) as it:
                    ev["normed"].wait(pe, it)
                    ev["copied"].wait(pe, it - 1)
                    for b in range(BATCH):
                        ins = pe.transpose(pT[:, b * P:(b + 1) * P], xc[:, b, :], identf[:])
                    ins.then_inc(ev["turned"].sem, 1)
                    ev["copied"].wait(pe, it)
                    ev["rowed"].wait(pe, it - 1)
                    for b in range(BATCH):
                        pe.matmul(pw[:, b // 3, (b % 3) * DW:(b % 3 + 1) * DW], hT[:, b * P:(b + 1) * P], wext[:],
                                  start=True, stop=True)
                    for q in range(2):
                        ins = pe.matmul(pd[0:36, q, 0:HC], wad[:], hT[:, q * HC:(q + 1) * HC], start=True, stop=True)
                    ins.then_inc(ev["projected"].sem, 1)
                with pe.Fori(0, NCH // 2) as half:
                    i = half * 2
                    for r in range(2):
                        c = i + r
                        pe.wait_ge(efl[r], i * 8 + 16)
                        ev["ef_out"].wait(pe, c - 2)
                        pe.matmul(pT[:, 512 * r:512 * r + G * H], eft[:, r], we[:], start=True,
                                  stop=True).then_inc(ev["ef_mm"].sem, 1)

            @block.scalar
            def _(act):
                for n in ("squared", "rooted", "copied", "ef_out"):
                    ev[n].start(act)
                with act.Fori(0, STEPS) as it:
                    norm_scalar(nc, act, ev, it, 1, xc[:], sq[:], s, epsc)
                    ev["turned"].wait(act, it)
                    nc.scalar.activation(hT[:], pT[:, 0:BC], ACT.Copy).then_inc(ev["copied"].sem, 1)
                with act.Fori(0, NCH // 2) as half:
                    i = half * 2
                    for r in range(2):
                        ev["ef_mm"].wait(act, i + r)
                        act.nop(nofuse=True)
                        nc.scalar.activation(efw[:, ds((i + r) * (G * H), G * H)],
                                             pT[:, 512 * r:512 * r + G * H], ACT.Copy).then_inc(ev["ef_out"].sem, 1)

            @block.vector
            def _(dve):
                v = nc.vector
                for n in ("centred", "varied", "normed", "rowed"):
                    ev[n].start(dve)
                v.memset(efw[:, NCH * G * H:], 0.0)
                v.memset(asrc[:], 0.0)
                v.memset(adst[:], 0.0)
                v.memset(we[:], 0.0).then_inc(zeroed, 1)
                dve.wait_ge(wready, 1)
                dve.wait_ge(loaded, 32)
                v.tensor_copy(wad[:], pe_[:, 64:100])
                v.tensor_copy(wext[:, D:DW], pe_[:, 0:H]).then_inc(wready, 1)
                with dve.Fori(0, STEPS // 2) as half:
                    i = half * 2
                    for r in range(2):
                        it = i + r
                        c = Chain(dve, chain, it * 9)
                        dve.wait_ge(xl[r], i * 8 + 16)
                        ev["turned"].wait(dve, it - 1)
                        norm_vector(nc, dve, c, ev, it, 1, xin[:, r], xc[:], sq[:], s)
                        v.tensor_single_scalar(xc[:], xc[:], 0.0, ALU.max).then_inc(ev["normed"].sem, 1)
                        ev["projected"].wait(dve, it)
                        ev["kept"].wait(dve, it - 1)
                        c(v.tensor_copy(row[:, 0:3, :], pw[:, 0, 0:3 * DW].rearrange("p (b f) -> p b f", f=DW)))
                        c(v.tensor_copy(row[:, 3:6, :], pw[:, 1, 0:3 * DW].rearrange("p (b f) -> p b f", f=DW)))
                        c(v.tensor_copy(row[:, 6:7, :], pw[:, 2, 0:DW].rearrange("p (b f) -> p b f", f=DW)))
                        c(v.tensor_copy(aux[32:36, ds(it * BC, HC)], pd[32:36, 0, 0:HC]))
                        c(v.tensor_copy(aux[32:36, ds(it * BC + HC, HC)], pd[32:36, 1, 0:HC]))
                        assert c.n == 9, c.n
                        dve.sem_inc(ev["rowed"].sem, 1)



def phase_attention(env, efw, table0):
    nc, dstf, srci, identf, iotaf, epsc, meta, pairs, baseB, sums, aux, visit_base, visit_pair = env
    with ExitStack() as ctx:
        sb = lambda n, s, d=F32: ctx.enter_context(nc.sbuf_tensor(n, s, d))
        ps = lambda n, s, d=F32: ctx.enter_context(nc.psum_tensor(n, s, d))
        sem = phase_semaphores(nc, ctx, "")
        vis = Visits(env, sem)
        GH = G * H
        slots = sb("a_slots", [P, 2 * G], I32)
        rows = sb("a_rows", [P, 2, G, DW])
        rel = sb("a_rel", [P, 2, G])
        far = sb("a_far", [P, 2, G, P], BF16)
        hot = sb("a_hot", [P, 2, G, P])
        hotT = sb("a_hotT", [P, 2, G, P])
        wsd = sb("a_wsd", [H, P])
        sdn = sb("a_sdn", [P, H])
        z = sb("a_z", [P, GH])
        z2 = sb("a_z2", [P, GH])
        attn = sb("a_attn", [P, 2, GH])
        parts = sb("a_parts", [P, 3, GH], BF16)
        rest = sb("a_rest", [P, 2, GH])
        partsT = sb("a_partsT", [3 * GH, P], BF16)
        pick = sb("a_pick", [3 * GH, GH, P], BF16)
        id3 = sb("a_id3", [3 * GH, GH])
        identb = sb("a_identb", [P, P], BF16)
        ident4 = sb("a_ident4", [P, H, P], BF16)
        iotab = sb("a_iotab", [P, P], BF16)
        tmax = sb("a_tmax", [P, 2, H, G])
        cmax = sb("a_cmax", [P, 2, H])
        wm = sb("a_wm", [H, P])
        pack = sb("a_pack", [P, 68])
        pack2 = sb("a_pack2", [P, 68])
        dm = sb("a_dm", [P, H])
        e1 = sb("a_e1", [P, GH])
        e2 = sb("a_e2", [P, GH])
        msg = sb("a_msg", [P, 2, G, DW])
        agg = sb("a_agg", [P, D])
        scale_rows = sb("a_scale_rows", [P, D])
        pz = ps("a_pz", [P, 3, 512])
        phT = ps("a_phT", [P, G * P], BF16)
        psm = ps("a_psm", [P, 512])
        ppT = ps("a_ppT", [P, 2 * P], BF16)
        pagg = ps("a_pagg", [P, 512])
        ptr = ps("a_ptr", [P, 512])
        SD, NM, SG, MG = slice(0, H), slice(8, 8 + H), (32, 64), (96, 128)
        landed = [sem("a_landed0"), sem("a_landed1")]
        setup, setup_chain = sem("a_setup"), sem("a_setup_chain")
        names = ("copied free rel_ far_ wsd_ sdn_ hot_ phT_ hotT_ sg z_ z2_ attn_ hi_ r1_ mid_ r2_ lo_ ppT_ partsT_ "
                 "cmax_ wm_ nm mnew dm_ sc mg e1_ e2_ ex msg_ pagg_ agg_ aggden ptr_ num1 num2 den1 den2 mput").split()
        ev = {n: Event(sem("a_" + n)) for n in names}
        ev["zmm"], ev["zred"] = Event(sem("a_zmm"), G), Event(sem("a_zred"), G)

        def owns(eng, names):
            for n in names.split():
                ev[n].start(eng)

        with nc.Block() as block:
            @block.sync
            def _(sp):
                vis.serve(sp, 4)

            @block.gpsimd
            def _(pool):
                gather_rows(vis, pool, table0, DW, slots, rows, ev["copied"], landed, ev["msg_"])

            @block.tensor
            def _(pe):
                owns(pe, "sg phT_ ppT_ zmm nm mg pagg_ ptr_")
                pe.wait_ge(setup, 1)

                def scores(i, r, v):
                    ev["wsd_"].wait(pe, v)
                    ev["e1_"].wait(pe, v - 2)
                    pe.nop(nofuse=True)
                    pe.transpose(psm[:, SD], wsd[:], identf[0:H, 0:H])
                    ev["far_"].wait(pe, v)
                    ev["hotT_"].wait(pe, v - 1)
                    for t in range(G):
                        ins = pe.transpose(phT[:, t * P:(t + 1) * P], far[:, r, t, :], identb[:])
                    ins.then_inc(ev["phT_"].sem, 1)
                    ev["sdn_"].wait(pe, v)
                    ev["hotT_"].wait(pe, v)
                    for t in range(G):
                        ins = pe.matmul(psm[:, SG[r] + t * H:SG[r] + (t + 1) * H], hotT[:, r, t, :], sdn[:], start=True, stop=True)
                    ins.then_inc(ev["sg"].sem, 1)
                    ev["lo_"].wait(pe, v)
                    pe.transpose(ppT[0:3 * GH, 0:P], parts[:].rearrange("p a b -> p (a b)"), identb[:]).then_inc(ev["ppT_"].sem, 1)
                    ev["partsT_"].wait(pe, v)
                    for t in range(G):
                        ev["zred"].wait(pe, v, (-1, 0, 0)[t] if t < 3 else t - 2)
                        pe.matmul(pz[:, t % 3, :], far[:, r, t, :], ident4[:].rearrange("p h e -> p (h e)"), start=True, stop=False)
                        for h in range(H):
                            ins = pe.matmul(pz[:, t % 3, h * P:(h + 1) * P], pick[:, t * H + h, :], partsT[:],
                                            start=False, stop=(h == H - 1))
                        ins.then_inc(ev["zmm"].sem, 1)

                def weighted(i, r, v):
                    ev["wm_"].wait(pe, v)
                    pe.nop(nofuse=True)
                    pe.transpose(psm[:, NM], wm[:], identf[0:H, 0:H]).then_inc(ev["nm"].sem, 1)
                    ev["mnew"].wait(pe, v)
                    ev["dm_"].wait(pe, v)
                    for t in range(G):
                        ins = pe.matmul(psm[:, MG[r] + t * H:MG[r] + (t + 1) * H], hotT[:, r, t, :], pack[:, 0:H], start=True, stop=True)
                    ins.then_inc(ev["mg"].sem, 1)
                    ev["msg_"].wait(pe, v)
                    ev["mput"].wait(pe, v - 1)
                    for t in range(G):
                        ins = pe.matmul(pagg[:, 0:DW], hot[:, r, t, :], msg[:, r, t, :], start=(t == 0), stop=(t == G - 1))
                    ins.then_inc(ev["pagg_"].sem, 1)
                    ev["sc"].wait(pe, v)
                    ev["aggden"].wait(pe, v)
                    ev["num2"].wait(pe, v - 1)
                    ev["den2"].wait(pe, v - 1)
                    pe.transpose(pagg[0:68, 2 * P:3 * P], pack[:], identf[:])
                    pe.transpose(ptr[:, 0:P], agg[:], identf[:])
                    pe.matmul(ptr[:, P:2 * P], scale_rows[:], identf[:], start=True, stop=True)
                    pe.transpose(ptr[0:68, 2 * P:3 * P], pack[:], identf[:])
                    pe.transpose(ptr[0:68, 3 * P:4 * P], pack2[:], identf[:]).then_inc(ev["ptr_"].sem, 1)

                vis.lagged(pe, scores, weighted)

            @block.scalar
            def _(act):
                a = nc.scalar
                owns(act, "wsd_ sdn_ hot_ hotT_ partsT_ wm_ sc ex agg_ aggden mput")
                act.wait_ge(setup, 1)

                def scores(i, r, v):
                    tile, node = vis.pair(act, i)
                    ev["phT_"].wait(act, v - 1)
                    act.nop(nofuse=True)
                    a.activation(wsd[:], aux[32:32 + H, ds(node, P)], ACT.Copy).then_inc(ev["wsd_"].sem, 1)
                    ev["far_"].wait(act, v)
                    ev["pagg_"].wait(act, v - 2)
                    a.activation(hot[:, r], far[:, r], ACT.Copy, scale=1.0 / BIG, bias=1.0).then_inc(ev["hot_"].sem, 1)
                    ev["phT_"].wait(act, v)
                    ev["sg"].wait(act, v - 1)
                    a.activation(sdn[:], psm[:, SD], ACT.Copy).then_inc(ev["sdn_"].sem, 1)
                    ev["mg"].wait(act, v - 2)
                    a.activation(hotT[:, r].rearrange("p t e -> p (t e)"), phT[:], ACT.Copy, scale=1.0 / BIG, bias=1.0)\
                        .then_inc(ev["hotT_"].sem, 1)
                    ev["ppT_"].wait(act, v)
                    ev["zmm"].wait(act, v - 1)
                    a.activation(partsT[:], ppT[0:3 * GH, 0:P], ACT.Copy).then_inc(ev["partsT_"].sem, 1)

                def weighted(i, r, v):
                    tile, node = vis.pair(act, i)
                    ev["mput"].wait(act, v - 1)
                    ev["nm"].wait(act, v - 1)
                    act.nop(nofuse=True)
                    a.activation(wm[:], aux[0:H, ds(node, P)], ACT.Copy).then_inc(ev["wm_"].sem, 1)
                    ev["dm_"].wait(act, v)
                    ev["ptr_"].wait(act, v - 1)
                    a.activation(pack2[:, 64:68], dm[:], ACT.Exp).then_inc(ev["sc"].sem, 1)
                    ev["sc"].wait(act, v)
                    a.activation(scale_rows[:].rearrange("p (h d) -> p h d", h=H),
                                 pack2[:, 64:68].unsqueeze(2).to_broadcast([P, H, HD]), ACT.Copy)
                    ev["e2_"].wait(act, v)
                    ev["pagg_"].wait(act, v - 2)
                    a.activation(msg[:, r, :, D:DW], e2[:].rearrange("p (t h) -> p t h", h=H), ACT.Exp).then_inc(ev["ex"].sem, 1)
                    ev["pagg_"].wait(act, v)
                    a.activation(agg[:], pagg[:, 0:D], ACT.Copy)
                    a.activation(pack[:, 64:68], pagg[:, D:DW], ACT.Copy).then_inc(ev["aggden"].sem, 1)
                    ev["ptr_"].wait(act, v)
                    act.nop(nofuse=True)
                    a.activation(aux[0:H, ds(node, P)], pagg[0:H, 2 * P:3 * P], ACT.Copy).then_inc(ev["mput"].sem, 1)

                vis.lagged(act, scores, weighted)

            @block.vector
            def _(dve):
                v_ = nc.vector
                owns(dve, "rel_ far_ z_ z2_ attn_ hi_ r1_ mid_ r2_ lo_ zred cmax_ mnew dm_ e1_ e2_ msg_ num1 num2 den1 den2")
                c = Chain(dve, setup_chain)
                c(v_.memset(pack[:], 0.0))
                c(v_.memset(pack2[:], 0.0))
                for k in range(3):
                    c(v_.tensor_copy(id3[k * GH:(k + 1) * GH, :], identf[k * GH:(k + 1) * GH, k * GH:(k + 1) * GH]))
                c(v_.tensor_copy(pick[:], id3[:].unsqueeze(2).to_broadcast([3 * GH, GH, P])))
                c(v_.tensor_copy(identb[:], identf[:]))
                c(v_.tensor_copy(iotab[:], iotaf[:]))
                c(v_.tensor_copy(ident4[:], identf[:].unsqueeze(1).to_broadcast([P, H, P])))
                dve.sem_inc(setup, 1)

                def scores(i, r, v):
                    tile, node = vis.pair(dve, i)
                    ev["zmm"].wait(dve, v - 2)
                    ev["hot_"].wait(dve, v - 2)
                    v_.tensor_scalar(rel[:, r], dstf[:, ds(tile, G)], baseB[:, ds(i, 1)], None, ALU.subtract).then_inc(ev["rel_"].sem, 1)
                    ev["rel_"].wait(dve, v)
                    for t in range(G):
                        ins = v_.tensor_scalar(far[:, r, t, :], iotab[:], rel[:, r, t:t + 1], -BIG, ALU.not_equal, ALU.mult)
                    ins.then_inc(ev["far_"].sem, 1)
                    dve.wait_ge(landed[r], (v - r) * 64 + 128)
                    ev["sg"].wait(dve, v)
                    v_.tensor_tensor(z[:].rearrange("p (t h) -> p t h", h=H), rows[:, r, :, D:DW],
                                     psm[:, SG[r]:SG[r] + GH].rearrange("p (t h) -> p t h", h=H), ALU.add).then_inc(ev["z_"].sem, 1)
                    ev["z_"].wait(dve, v)
                    v_.scalar_tensor_tensor(out=z2[:], in0=z[:], scalar=0.2, in1=z[:], op0=ALU.mult, op1=ALU.max).then_inc(ev["z2_"].sem, 1)
                    ev["z2_"].wait(dve, v)
                    v_.tensor_tensor(attn[:, r], z2[:], efw[:, ds(tile * H, GH)], ALU.add).then_inc(ev["attn_"].sem, 1)
                    ev["attn_"].wait(dve, v)
                    ev["ppT_"].wait(dve, v - 1)
                    v_.tensor_copy(parts[:, 0], attn[:, r]).then_inc(ev["hi_"].sem, 1)
                    ev["hi_"].wait(dve, v)
                    v_.tensor_tensor(rest[:, 0], attn[:, r], parts[:, 0], ALU.subtract).then_inc(ev["r1_"].sem, 1)
                    ev["r1_"].wait(dve, v)
                    v_.tensor_copy(parts[:, 1], rest[:, 0]).then_inc(ev["mid_"].sem, 1)
                    ev["mid_"].wait(dve, v)
                    v_.tensor_tensor(parts[:, 2], rest[:, 0], parts[:, 1], ALU.subtract).then_inc(ev["lo_"].sem, 1)
                    for t in range(G):
                        ev["zmm"].wait(dve, v, t + 1)
                        v_.tensor_reduce(tmax[:, r, :, t], pz[:, t % 3, :].rearrange("p (h e) -> p h e", h=H), AX, ALU.max)\
                            .then_inc(ev["zred"].sem, 1)
                    ev["zred"].wait(dve, v)
                    v_.tensor_reduce(cmax[:, r], tmax[:, r], AX, ALU.max).then_inc(ev["cmax_"].sem, 1)

                def weighted(i, r, v):
                    tile, node = vis.pair(dve, i)
                    win = ds(node, P)
                    ev["nm"].wait(dve, v)
                    ev["cmax_"].wait(dve, v)
                    ev["ptr_"].wait(dve, v - 1)
                    v_.tensor_tensor(pack[:, 0:H], psm[:, NM], cmax[:, r], ALU.max).then_inc(ev["mnew"].sem, 1)
                    ev["mnew"].wait(dve, v)
                    v_.tensor_tensor(dm[:], psm[:, NM], pack[:, 0:H], ALU.subtract).then_inc(ev["dm_"].sem, 1)
                    ev["mg"].wait(dve, v)
                    v_.tensor_tensor(e1[:], attn[:, r], psm[:, MG[r]:MG[r] + GH], ALU.subtract).then_inc(ev["e1_"].sem, 1)
                    ev["e1_"].wait(dve, v)
                    v_.tensor_single_scalar(e2[:], e1[:], 0.0, ALU.min).then_inc(ev["e2_"].sem, 1)
                    ev["ex"].wait(dve, v)
                    v_.tensor_tensor(msg[:, r, :, 0:D].rearrange("p t (h d) -> p t h d", h=H),
                                     rows[:, r, :, 0:D].rearrange("p t (h d) -> p t h d", h=H),
                                     msg[:, r, :, D:DW].unsqueeze(3).to_broadcast([P, G, H, HD]), ALU.mult).then_inc(ev["msg_"].sem, 1)
                    ev["num2"].wait(dve, v - 1)
                    ev["den2"].wait(dve, v - 1)
                    ev["ptr_"].wait(dve, v)
                    v_.tensor_tensor(sums[:, win], sums[:, win], ptr[:, P:2 * P], ALU.mult).then_inc(ev["num1"].sem, 1)
                    v_.tensor_tensor(aux[64:68, win], aux[64:68, win], ptr[64:68, 3 * P:4 * P], ALU.mult).then_inc(ev["den1"].sem, 1)
                    ev["num1"].wait(dve, v)
                    v_.tensor_tensor(sums[:, win], sums[:, win], ptr[:, 0:P], ALU.add).then_inc(ev["num2"].sem, 1)
                    ev["den1"].wait(dve, v)
                    v_.tensor_tensor(aux[64:68, win], aux[64:68, win], ptr[64:68, 2 * P:3 * P], ALU.add).then_inc(ev["den2"].sem, 1)

                vis.lagged(dve, scores, weighted)



def phase_sum(env, layer, table, weights):
    nc, dstf, srci, identf, iotaf, epsc, meta, pairs, baseB, sums, aux, visit_base, visit_pair = env
    counts = weights is None
    with ExitStack() as ctx:
        sb = lambda n, s, d=F32: ctx.enter_context(nc.sbuf_tensor(f"s{layer}_" + n, s, d))
        sem = phase_semaphores(nc, ctx, f"s{layer}_")
        vis = Visits(env, sem)
        slots = sb("slots", [P, 2 * G], I32)
        rows = sb("rows", [P, 2, G, D])
        rel = sb("rel", [P, 2, G])
        hot = sb("hot", [P, 2, G, P])
        wts = sb("wts", [P, T])
        ones = sb("ones", [P, P])
        pagg = ctx.enter_context(nc.psum_tensor(f"s{layer}_pagg", [P, 2, 2, 512], F32))
        landed = [sem("landed0"), sem("landed1")]
        loaded, cleared = sem("loaded"), sem("cleared")
        ev = {n: Event(sem(n)) for n in ("copied", "rel_", "hot_", "agg", "added", "counted")}

        with nc.Block() as block:
            @block.sync
            def _(sp):
                if not counts:
                    sp.dma_start(wts[:], weights).then_inc(loaded, 16)
                vis.serve(sp, 3)

            @block.gpsimd
            def _(pool):
                gather_rows(vis, pool, table, D, slots, rows, ev["copied"], landed, ev["agg"])

            @block.vector
            def _(dve):
                v_ = nc.vector
                for n in ("rel_", "hot_", "added", "counted"):
                    ev[n].start(dve)
                v_.memset(ones[:], 1.0).then_inc(cleared, 1)
                v_.memset(sums[:], 0.0).then_inc(cleared, 1)
                v_.memset(aux[:], 0.0).then_inc(cleared, 1)
                dve.wait_ge(cleared, 3)
                if not counts:
                    dve.wait_ge(loaded, 16)

                def onehot(i, r, v):
                    tile, node = vis.pair(dve, i)
                    ev["agg"].wait(dve, v - 2)
                    v_.tensor_scalar(rel[:, r], dstf[:, ds(tile, G)], baseB[:, ds(i, 1)], None, ALU.subtract).then_inc(ev["rel_"].sem, 1)
                    ev["rel_"].wait(dve, v)
                    for t in range(G):
                        if counts:
                            ins = v_.tensor_scalar(hot[:, r, t, :], iotaf[:], rel[:, r, t:t + 1], None, ALU.is_equal)
                        else:
                            ins = v_.tensor_scalar(hot[:, r, t, :], iotaf[:], rel[:, r, t:t + 1], wts[:, ds(tile + t, 1)],
                                                   ALU.is_equal, ALU.mult)
                    ins.then_inc(ev["hot_"].sem, 1)

                def add(i, r, v):
                    tile, node = vis.pair(dve, i)
                    ev["agg"].wait(dve, v)
                    ev["added"].wait(dve, v - 1)
                    v_.tensor_tensor(sums[:, ds(node, P)], sums[:, ds(node, P)], pagg[:, r, 0, 0:P], ALU.add).then_inc(ev["added"].sem, 1)
                    if counts:
                        ev["counted"].wait(dve, v - 1)
                        v_.tensor_tensor(aux[:, ds(node, P)], aux[:, ds(node, P)], pagg[:, r, 1, 0:P], ALU.add).then_inc(ev["counted"].sem, 1)

                vis.lagged(dve, onehot, add)

            @block.tensor
            def _(pe):
                ev["agg"].start(pe)
                pe.wait_ge(cleared, 1)

                def product(i, r, v):
                    pe.wait_ge(landed[r], (v - r) * 64 + 128)
                    ev["hot_"].wait(pe, v)
                    ev["added"].wait(pe, v - 2)
                    if counts:
                        ev["counted"].wait(pe, v - 2)
                        for t in range(G):
                            pe.matmul(pagg[:, r, 1, 0:P], ones[:], hot[:, r, t, :], start=(t == 0), stop=(t == G - 1))
                    for t in range(G):
                        ins = pe.matmul(pagg[:, r, 0, 0:P], rows[:, r, t, :], hot[:, r, t, :], start=(t == 0), stop=(t == G - 1))
                    ins.then_inc(ev["agg"].sem, 1)

                vis.loop(pe, product)



def phase_factors(env, sh, shx, CG):
    nc = env[0]
    with ExitStack() as ctx:
        sb = lambda n, s, d=F32: ctx.enter_context(nc.sbuf_tensor(n, s, d))
        sem = phase_semaphores(nc, ctx, "")
        CT = T // 11
        assert CT * 11 == T
        raw = sb("f_raw", [P, CT, 9])
        fac = sb("f_fac", [P, CT, NSH])
        loaded, stored, chain = (sem(n) for n in ("f_loaded", "f_stored", "f_chain"))
        made, kept = Event(sem("f_made")), Event(sem("f_kept"))
        C011, C110, C121 = CG[1], CG[3], CG[4]
        plan = [(0, [(0, 1.0)])]
        plan += [(1 + k, [(1 + k, float(C011[0, k, k]))]) for k in range(3)]
        plan += [(4 + i, [(1 + i, float(C110[i, i, 0]))]) for i in range(3)]
        for i in range(3):
            for k in range(3):
                plan.append((7 + 3 * i + k, [(4 + j, float(C121[i, j, k])) for j in range(5) if abs(C121[i, j, k]) > 1e-7]))
        LINKS = sum(len(terms) for _, terms in plan)

        with nc.Block() as block:
            @block.sync
            def _(sp):
                kept.start(sp)
                with sp.Fori(0, 11) as it:
                    made.wait(sp, it - 1)
                    sp.dma_start(raw[:].rearrange("p t j -> p (t j)"), sh[:, ds(it * (CT * 9), CT * 9)]).then_inc(loaded, 16)
                    made.wait(sp, it)
                    sp.dma_start(shx[:, ds(it * (CT * NSH), CT * NSH)], fac[:].rearrange("p t j -> p (t j)")).then_inc(stored, 16)
                    sp.wait_ge(stored, it * 16 + 16)
                    sp.sem_inc(kept.sem, 1)

            @block.vector
            def _(dve):
                made.start(dve)
                with dve.Fori(0, 11) as it:
                    c = Chain(dve, chain, it * LINKS)
                    dve.wait_ge(loaded, it * 16 + 16)
                    kept.wait(dve, it - 1)
                    for col, terms in plan:
                        for n, (j, f) in enumerate(terms):
                            if n == 0:
                                c(nc.vector.tensor_scalar(fac[:, :, col], raw[:, :, j], f, None, ALU.mult))
                            else:
                                c(nc.vector.scalar_tensor_tensor(out=fac[:, :, col], in0=raw[:, :, j], scalar=f,
                                                                 in1=fac[:, :, col], op0=ALU.mult, op1=ALU.add))
                    assert c.n == LINKS
                    dve.sem_inc(made.sem, 1)


def phase_tensor_product(env, table, shx, W2b, W2scale):
    nc, dstf, srci, identf, iotaf, epsc, meta, pairs, baseB, sums, aux, visit_base, visit_pair = env
    with ExitStack() as ctx:
        sb = lambda n, s, d=F32: ctx.enter_context(nc.sbuf_tensor("p_" + n, s, d))
        ps = lambda n, s, d=F32: ctx.enter_context(nc.psum_tensor("p_" + n, s, d))
        sem = phase_semaphores(nc, ctx, "p_")
        vis = Visits(env, sem)
        slots = sb("slots", [P, 2 * G], I32)
        rows = sb("rows", [P, 2, G, D])
        rel = sb("rel", [P, 2, G])
        hot = sb("hot", [P, 2, G, P])
        fac = sb("fac", [P, 2, G, NSH])
        prod = sb("prod", [P, 2, G, TW])
        t4 = sb("t4", [P, 3, G, 3, 32])
        t3 = sb("t3", [P, 3, G, 32])
        a4 = sb("a4", [P, G, 3, 32])
        a3 = sb("a3", [P, G, 32])
        w2 = sb("w2", [P, 3, D])
        w2s = sb("w2s", [P, 3])
        win = sb("win", [P, 3, P])
        pagg = ps("pagg", [P, 2, 3, 512])
        pmsg = ps("pmsg", [P, 512])
        landed = [sem("landed0"), sem("landed1")]
        facl = [sem("facl0"), sem("facl1")]
        loaded, cleared, wchain = sem("loaded"), sem("cleared"), sem("wchain")
        ev = {n: Event(sem(n)) for n in
              ("copied", "rel_", "hot_", "t4_", "t3_", "a4_", "a3_", "x1_", "made", "made0", "agg", "win_", "msg_", "added")}
        BLK = ((0, 128), (128, 128), (256, 96))

        with nc.Block() as block:
            @block.sync
            def _(sp):
                sp.dma_start(w2[:], W2b).then_inc(loaded, 16)
                sp.dma_start(w2s[:], W2scale).then_inc(loaded, 16)
                npages = sp.value_load(meta[0:1, 0:1], min_val=1, max_val=PAGES)
                sp.sem_inc(vis.page_done, 1)
                with sp.Fori(0, npages) as pg:
                    sp.wait_ge(vis.page_done, pg * 4 + 1)
                    sp.dma_start(pairs[:], visit_pair[ds(pg, 1), :]).then_inc(vis.page_loaded, 16)
                    sp.dma_start(baseB[:], visit_base[ds(pg, 1), :].to_broadcast([P, PG])).then_inc(vis.page_loaded, 16)
                    sp.wait_ge(vis.page_loaded, pg * 32 + 32)
                    count = sp.value_load(meta[0:1, ds(pg + 1, 1)], min_val=0, max_val=PG // 2 - 2) + 2
                    with sp.Fori(0, count) as half:
                        i = half * 2
                        for r in range(2):
                            v = pg * PG + i + r
                            tile, node = vis.pair(sp, i + r)
                            ev["made"].wait(sp, v - 2)
                            ev["made0"].wait(sp, v - 2)
                            sp.dma_start(fac[:, r].rearrange("p t j -> p (t j)"), shx[:, ds(tile * NSH, G * NSH)]).then_inc(facl[r], 16)

            @block.gpsimd
            def _(pool):
                gather_rows(vis, pool, table, D, slots, rows, ev["copied"], landed, ev["made0"])

            @block.scalar
            def _(act):
                a = nc.scalar
                for n in ("made0", "win_"):
                    ev[n].start(act)

                def scalars(i, r, v):
                    act.wait_ge(landed[r], (v - r) * 64 + 128)
                    act.wait_ge(facl[r], (v - r) * 8 + 16)
                    ev["agg"].wait(act, v - 2)
                    for t in range(G):
                        a.activation(prod[:, r, t, 0:D], rows[:, r, t, :], ACT.Copy, scale=fac[:, r, t, 0:1])
                    for k in range(3):
                        for t in range(G):
                            a.activation(prod[:, r, t, D + 32 * k:D + 32 * k + 32], rows[:, r, t, 0:32], ACT.Copy,
                                         scale=fac[:, r, t, 1 + k:2 + k])
                    ev["x1_"].wait(act, v)
                    act.nop(nofuse=True)
                    act.drain().then_inc(ev["made0"].sem, 1)

                def window(i, r, v):
                    ev["agg"].wait(act, v)
                    ev["msg_"].wait(act, v - 1)
                    for b, (o, w) in enumerate(BLK):
                        ins = a.activation(win[0:w, b, :], pagg[0:w, r, b, 0:P], ACT.Copy)
                    ins.then_inc(ev["win_"].sem, 1)

                vis.lagged(act, scalars, window)

            @block.vector
            def _(dve):
                v_ = nc.vector
                for n in ("rel_", "hot_", "t4_", "t3_", "a4_", "a3_", "x1_", "made", "added"):
                    ev[n].start(dve)
                v_.memset(sums[:], 0.0).then_inc(cleared, 1)
                dve.wait_ge(loaded, 32)
                c = Chain(dve, wchain)
                for b in range(3):
                    c(v_.tensor_scalar(w2[:, b, :], w2[:, b, :], w2s[:, b:b + 1], None, ALU.mult))
                dve.sem_inc(cleared, 1)
                dve.wait_ge(cleared, 2)

                def products(i, r, v):
                    tile, node = vis.pair(dve, i)
                    ev["agg"].wait(dve, v - 2)
                    v_.tensor_scalar(rel[:, r], dstf[:, ds(tile, G)], baseB[:, ds(i, 1)], None, ALU.subtract).then_inc(ev["rel_"].sem, 1)
                    ev["rel_"].wait(dve, v)
                    for t in range(G):
                        ins = v_.tensor_scalar(hot[:, r, t, :], iotaf[:], rel[:, r, t:t + 1], None, ALU.is_equal)
                    ins.then_inc(ev["hot_"].sem, 1)
                    dve.wait_ge(landed[r], (v - r) * 64 + 128)
                    dve.wait_ge(facl[r], (v - r) * 8 + 16)
                    x1 = rows[:, r, :, 32:D].rearrange("p t (u i) -> p t i u", i=3)
                    for i1 in range(3):
                        ins = v_.tensor_tensor(t4[:, i1], x1[:, :, i1, :].unsqueeze(2).to_broadcast([P, G, 3, 32]),
                                         fac[:, r, :, 7 + 3 * i1:10 + 3 * i1].unsqueeze(3).to_broadcast([P, G, 3, 32]), ALU.mult)
                    ins.then_inc(ev["t4_"].sem, 1)
                    for i1 in range(3):
                        ins = v_.tensor_tensor(t3[:, i1], x1[:, :, i1, :],
                                         fac[:, r, :, 4 + i1].unsqueeze(2).to_broadcast([P, G, 32]), ALU.mult)
                    ins.then_inc(ev["x1_"].sem, 1)
                    ev["t4_"].wait(dve, v)
                    v_.tensor_tensor(a4[:], t4[:, 0], t4[:, 1], ALU.add).then_inc(ev["a4_"].sem, 1)
                    ev["x1_"].wait(dve, v)
                    v_.tensor_tensor(a3[:], t3[:, 0], t3[:, 1], ALU.add).then_inc(ev["a3_"].sem, 1)
                    ev["a4_"].wait(dve, v)
                    v_.tensor_tensor(prod[:, r, :, 256:352].rearrange("p t (k u) -> p t k u", k=3), a4[:], t4[:, 2], ALU.add)
                    ev["a3_"].wait(dve, v)
                    v_.tensor_tensor(prod[:, r, :, 224:256], a3[:], t3[:, 2], ALU.add).then_inc(ev["made"].sem, 1)

                def add(i, r, v):
                    tile, node = vis.pair(dve, i)
                    ev["msg_"].wait(dve, v)
                    ev["added"].wait(dve, v - 1)
                    v_.tensor_tensor(sums[:, ds(node, P)], sums[:, ds(node, P)], pmsg[:, 0:P], ALU.add).then_inc(ev["added"].sem, 1)

                vis.lagged(dve, products, add)

            @block.tensor
            def _(pe):
                for n in ("agg", "msg_"):
                    ev[n].start(pe)
                pe.wait_ge(cleared, 2)

                def by_window(i, r, v):
                    ev["hot_"].wait(pe, v)
                    ev["made"].wait(pe, v)
                    ev["made0"].wait(pe, v)
                    ev["win_"].wait(pe, v - 2)
                    for b, (o, w) in enumerate(BLK):
                        for t in range(G):
                            ins = pe.matmul(pagg[0:w, r, b, 0:P], prod[:, r, t, o:o + w], hot[:, r, t, :],
                                            start=(t == 0), stop=(t == G - 1))
                    ins.then_inc(ev["agg"].sem, 1)

                def weigh(i, r, v):
                    ev["win_"].wait(pe, v)
                    ev["added"].wait(pe, v - 1)
                    for b, (o, w) in enumerate(BLK):
                        ins = pe.matmul(pmsg[:, 0:P], w2[0:w, b, :], win[0:w, b, :], start=(b == 0), stop=(b == 2))
                    ins.then_inc(ev["msg_"].sem, 1)

                vis.lagged(pe, by_window, weigh)



def phase_node(env, layer, xold, xnew, table, params):
    nc, dstf, srci, identf, iotaf, epsc, meta, pairs, baseB, sums, aux, visit_base, visit_pair = env
    with ExitStack() as ctx:
        sb = lambda n, s, d=F32: ctx.enter_context(nc.sbuf_tensor(f"n{layer}_" + n, s, d))
        ps = lambda n, s, d=F32: ctx.enter_context(nc.psum_tensor(f"n{layer}_" + n, s, d))
        sem = phase_semaphores(nc, ctx, f"n{layer}_")
        xin = sb("xin", [P, 2, BATCH, D])
        xout = sb("xout", [P, 2, BATCH, D])
        hout = sb("hout", [P, 2, BATCH, D])
        xc = sb("xc", [P, BATCH, D])
        sq = sb("sq", [P, BATCH, D])
        s = sb("s", [P, 40])
        fm = sb("fm", [P, BC])
        gm = sb("gm", [P, BC])
        row = sb("row", [P, 2, D])
        w = sb("w", [P, D])
        sel = sb("sel", [68, P])
        pden = ps("pden", [P, 2, 512])
        pT = ps("pT", [P, 1024])
        xl = [sem("xl0"), sem("xl1")]
        stored = [sem("stored0"), sem("stored1")]
        loaded, setup, chain, xchain = sem("loaded"), sem("setup"), sem("chain"), sem("xchain")
        ev = {n: Event(sem(n)) for n in ("fm_", "gelu_", "nodes", "pre", "act_", "den", "xnew_", "hnew", "kept")}
        for n in ("centred", "squared", "varied", "rooted"):
            ev[n] = Event(sem(n), 2 if layer == 0 else 1)

        with nc.Block() as block:
            @block.sync
            def _(sp):
                n = 0
                if layer == 0:
                    sp.dma_start(row[:, 0, :], params["scale"].to_broadcast([P, D])).then_inc(loaded, 16)
                    sp.dma_start(row[:, 1, :], params["bias"].to_broadcast([P, D])).then_inc(loaded, 16)
                if layer == 1:
                    sp.dma_start(row[:, 0, :], params["b"].to_broadcast([P, D])).then_inc(loaded, 16)
                    sp.dma_start(w[:], params["W"]).then_inc(loaded, 16)
                ev["kept"].start(sp)
                with sp.Fori(0, STEPS // 2) as half:
                    i = half * 2
                    for r in range(2):
                        ev["hnew"].wait(sp, i + r)
                        sp.dma_start(blocks_of(xnew, i + r), xout[:, r]).then_inc(stored[r], 16)
                        sp.dma_start(blocks_of(table, i + r), hout[:, r]).then_inc(stored[r], 16)
                        sp.wait_ge(stored[r], i * 16 + 32)
                        sp.sem_inc(ev["kept"].sem, 1)

            @block.gpsimd
            def _(pool):
                load_blocks(nc, pool, ((xold, xin, xl),), ev["xnew_"])

            @block.tensor
            def _(pe):
                for n in ("nodes", "den"):
                    ev[n].start(pe)
                pe.wait_ge(setup, 1)
                with pe.Fori(0, STEPS) as it:
                    if layer == 0:
                        ev["fm_"].wait(pe, it - 1)
                        for q in range(2):
                            ins = pe.matmul(pden[:, q, 0:HC], sel[:], aux[0:68, ds(it * BC + q * HC, HC)], start=True, stop=True)
                        ins.then_inc(ev["den"].sem, 1)
                    ev["gelu_"].wait(pe, it)
                    ev["xnew_"].wait(pe, it - 1)
                    ev["pre"].wait(pe, it - 1)
                    for b in range(BATCH):
                        c = slice(b * P, (b + 1) * P)
                        if layer == 1:
                            ins = pe.matmul(pT[:, c], gm[:, c], w[:], start=True, stop=True)
                        else:
                            ins = pe.transpose(pT[:, c], gm[:, c], identf[:])
                    ins.then_inc(ev["nodes"].sem, 1)

            @block.scalar
            def _(act):
                a = nc.scalar
                for n in ("squared", "rooted", "gelu_", "act_"):
                    ev[n].start(act)
                act.wait_ge(setup, 1)
                with act.Fori(0, STEPS) as it:
                    ev["nodes"].wait(act, it - 1)
                    act.nop(nofuse=True)
                    if layer == 0:
                        ev["fm_"].wait(act, it)
                        a.activation(gm[:], fm[:], ACT.Gelu).then_inc(ev["gelu_"].sem, 1)
                        norm_scalar(nc, act, ev, it, 1, xc[:], sq[:], s, epsc)
                    elif layer == 1:
                        a.activation(gm[:], sums[:, ds(it * BC, BC)], ACT.Gelu_apprx_tanh).then_inc(ev["gelu_"].sem, 1)
                        ev["pre"].wait(act, it)
                        a.activation(sq[:], xc[:], ACT.Gelu_apprx_tanh).then_inc(ev["act_"].sem, 1)
                    else:
                        a.activation(gm[:], sums[:, ds(it * BC, BC)], ACT.Copy).then_inc(ev["gelu_"].sem, 1)
                    norm_scalar(nc, act, ev, it, 2 if layer == 0 else 1, xc[:], sq[:], s, epsc)

            @block.vector
            def _(dve):
                v = nc.vector
                for n in ("centred", "varied", "fm_", "pre", "xnew_", "hnew"):
                    ev[n].start(dve)
                if layer < 2:
                    dve.wait_ge(loaded, 32)
                if layer == 0:
                    c = Chain(dve, xchain)
                    c(v.memset(sel[:], 0.0))
                    for h in range(H):
                        c(v.tensor_copy(sel[64:68, h * HD:(h + 1) * HD],
                                        identf[64:68, 64 + h:65 + h].to_broadcast([H, HD])))
                dve.sem_inc(setup, 1)
                links = {0: 12, 1: 4, 2: 4}[layer]
                with dve.Fori(0, STEPS // 2) as half:
                    i = half * 2
                    for r in range(2):
                        it = i + r
                        c = Chain(dve, chain, it * links)
                        node_rows = pT[:, 0:BC].rearrange("p (b f) -> p b f", f=D)
                        wide = lambda k: row[:, k, :].unsqueeze(1).to_broadcast([P, BATCH, D])
                        if layer == 0:
                            ev["den"].wait(dve, it)
                            ev["gelu_"].wait(dve, it - 1)
                            c(v.tensor_scalar(fm[:].rearrange("p (q n) -> p q n", q=2), pden[:, :, 0:HC], 1e-9, None, ALU.add))
                            c(v.reciprocal(fm[:], fm[:]))
                            v.tensor_tensor(fm[:], fm[:], sums[:, ds(it * BC, BC)], ALU.mult).then_inc(ev["fm_"].sem, 1)
                        ev["nodes"].wait(dve, it)
                        ev["hnew"].wait(dve, it - 1)
                        dve.wait_ge(xl[r], i * 8 + 16)
                        ev["kept"].wait(dve, it - 2)
                        if layer == 0:
                            norm_vector(nc, dve, c, ev, it, 1, node_rows, xc[:], sq[:], s)
                            dve.sem_inc(ev["pre"].sem, 1)
                            c(v.tensor_tensor(xc[:], xc[:], wide(0), ALU.mult))
                            c(v.tensor_tensor(xc[:], xc[:], wide(1), ALU.add))
                            new = xc[:]
                        elif layer == 1:
                            v.tensor_tensor(xc[:], node_rows, wide(0), ALU.add).then_inc(ev["pre"].sem, 1)
                            ev["act_"].wait(dve, it)
                            new = sq[:]
                        else:
                            dve.sem_inc(ev["pre"].sem, 1)
                            new = node_rows
                        v.tensor_tensor(xout[:, r], xin[:, r], new, ALU.add).then_inc(ev["xnew_"].sem, 1)
                        ev["xnew_"].wait(dve, it)
                        norm_vector(nc, dve, c, ev, it, 2 if layer == 0 else 1, xout[:, r], xc[:], sq[:], s)
                        v.tensor_single_scalar(hout[:, r], xc[:], 0.0, ALU.max).then_inc(ev["hnew"].sem, 1)
                        assert c.n == links, c.n



def phase_last(env, x3, table, WlT, WrT, bl, gamma, beta, out):
    nc, dstf, srci, identf, iotaf, epsc, meta, pairs, baseB, sums, aux, visit_base, visit_pair = env
    with ExitStack() as ctx:
        sb = lambda n, s, d=F32: ctx.enter_context(nc.sbuf_tensor("l_" + n, s, d))
        ps = lambda n, s, d=F32: ctx.enter_context(nc.psum_tensor("l_" + n, s, d))
        sem = phase_semaphores(nc, ctx, "l_")
        hin = sb("hin", [P, 2, BATCH, D])
        xin = sb("xin", [P, 2, BATCH, D])
        xout = sb("xout", [P, 2, BATCH, D])
        hT = sb("hT", [P, BC])
        mean = sb("mean", [P, BC])
        wl, wr = sb("wl", [P, D]), sb("wr", [P, D])
        par = sb("par", [P, 3, D])
        ones = sb("ones", [P, P])
        stat = sb("stat", [P, 8, D])
        tot = sb("tot", [P, BATCH, D])
        pT = ps("pT", [P, 1024])
        py = ps("py", [P, 1024])
        pst = ps("pst", [P, 512])
        hl = [sem("hl0"), sem("hl1")]
        xl = [sem("xl0"), sem("xl1")]
        stored = [sem("stored0"), sem("stored1")]
        loaded, setup, chain, schain, stm, ychain, roots = (
            sem(n) for n in ("loaded", "setup", "chain", "schain", "stm", "ychain", "roots"))
        ev = {n: Event(sem(n)) for n in ("mean_", "turned", "hT_", "y_", "kept", "done", "saved")}
        y = sums[:, 0:NP].rearrange("p (b f) -> p b f", f=D)
        LAST = N - (NB - 1) * P

        with nc.Block() as block:
            @block.sync
            def _(sp):
                for t, src in ((wl[:], WlT), (wr[:], WrT), (par[:, 0, :], bl.to_broadcast([P, D])),
                               (par[:, 1, :], gamma.to_broadcast([P, D])), (par[:, 2, :], beta.to_broadcast([P, D]))):
                    sp.dma_start(t, src).then_inc(loaded, 16)
                ev["saved"].start(sp)
                with sp.Fori(0, STEPS // 2) as half:
                    i = half * 2
                    for r in range(2):
                        ev["done"].wait(sp, i + r)
                        sp.dma_start(blocks_of(out, i + r), xout[:, r]).then_inc(stored[r], 16)
                        sp.wait_ge(stored[r], i * 8 + 16)
                        sp.sem_inc(ev["saved"].sem, 1)

            @block.gpsimd
            def _(pool):
                load_blocks(nc, pool, ((table, hin, hl),), ev["turned"])
                load_blocks(nc, pool, ((x3, xin, xl),), ev["done"])

            @block.tensor
            def _(pe):
                for n in ("turned", "y_"):
                    ev[n].start(pe)
                pe.wait_ge(loaded, 80)
                with pe.Fori(0, STEPS // 2) as half:
                    i = half * 2
                    for r in range(2):
                        it = i + r
                        pe.wait_ge(hl[r], i * 8 + 16)
                        ev["hT_"].wait(pe, it - 1)
                        for b in range(BATCH):
                            ins = pe.transpose(pT[:, b * P:(b + 1) * P], hin[:, r, b, :], identf[:])
                        ins.then_inc(ev["turned"].sem, 1)
                        ev["hT_"].wait(pe, it)
                        ev["mean_"].wait(pe, it)
                        ev["kept"].wait(pe, it - 1)
                        for b in range(BATCH):
                            c = slice(b * P, (b + 1) * P)
                            pe.matmul(py[:, c], mean[:, c], wl[:], start=True, stop=False)
                            ins = pe.matmul(py[:, c], hT[:, c], wr[:], start=False, stop=True)
                        ins.then_inc(ev["y_"].sem, 1)
                for n in range(2):
                    pe.wait_ge(stm, n + 1)
                    pe.matmul(pst[:, n * D:(n + 1) * D], ones[:], stat[:, 2 * n, :], start=True, stop=False)
                    pe.matmul(pst[:, n * D:(n + 1) * D], ones[0:LAST, :], stat[0:LAST, 2 * n + 1, :], start=False, stop=True).then_inc(setup, 1)

            @block.scalar
            def _(act):
                a = nc.scalar
                ev["hT_"].start(act)
                with act.Fori(0, STEPS) as it:
                    ev["turned"].wait(act, it)
                    ev["y_"].wait(act, it - 1)
                    a.activation(hT[:], pT[:, 0:BC], ACT.Copy).then_inc(ev["hT_"].sem, 1)
                act.wait_ge(roots, 1)
                a.activation(stat[:, 5, :], stat[:, 4, :], ACT.Sqrt, bias=epsc[:], scale=1.0 / N).then_inc(roots, 1)

            @block.vector
            def _(dve):
                v = nc.vector
                for n in ("mean_", "kept", "done"):
                    ev[n].start(dve)
                c = Chain(dve, schain)
                c(v.memset(ones[:], 1.0))
                dve.wait_ge(loaded, 80)
                with dve.Fori(0, STEPS) as it:
                    cc = Chain(dve, chain, it * 3)
                    cols = ds(it * BC, BC)
                    ev["y_"].wait(dve, it - 1)
                    cc(v.tensor_scalar(mean[:], aux[:, cols], 1.0, None, ALU.max))
                    cc(v.reciprocal(mean[:], mean[:]))
                    v.tensor_tensor(mean[:], mean[:], sums[:, cols], ALU.mult).then_inc(ev["mean_"].sem, 1)
                    ev["mean_"].wait(dve, it)
                    ev["y_"].wait(dve, it)
                    cc(v.tensor_tensor(sums[:, cols].rearrange("p (b f) -> p b f", f=D), py[:, 0:BC].rearrange("p (b f) -> p b f", f=D),
                                    par[:, 0, :].unsqueeze(1).to_broadcast([P, BATCH, D]), ALU.add))
                    dve.sem_inc(ev["kept"].sem, 1)
                by_feature = y[:, 0:NB - 1, :].rearrange("p b f -> p f b")
                c(v.tensor_reduce(stat[:, 0, :], by_feature, AX, ALU.add))
                c(v.tensor_copy(stat[:, 1, :], y[:, NB - 1, :]))
                dve.sem_inc(stm, 1)
                dve.wait_ge(setup, 1)
                c(v.tensor_scalar(stat[:, 6, :], pst[:, 0:D], -1.0 / N, None, ALU.mult))
                c(v.tensor_tensor(y, y, stat[:, 6, :].unsqueeze(1).to_broadcast([P, NB, D]), ALU.add))
                sqv = aux[:, 0:NP].rearrange("p (b f) -> p b f", f=D)
                c(v.tensor_tensor(sqv, y, y, ALU.mult))
                c(v.tensor_reduce(stat[:, 2, :], sqv[:, 0:NB - 1, :].rearrange("p b f -> p f b"), AX, ALU.add))
                c(v.tensor_copy(stat[:, 3, :], sqv[:, NB - 1, :]))
                dve.sem_inc(stm, 1)
                dve.wait_ge(setup, 2)
                c(v.tensor_copy(stat[:, 4, :], pst[:, D:2 * D]))
                dve.sem_inc(roots, 1)
                dve.wait_ge(roots, 2)
                c(v.reciprocal(stat[:, 7, :], stat[:, 5, :]))
                c(v.tensor_tensor(stat[:, 7, :], stat[:, 7, :], par[:, 1, :], ALU.mult))
                with dve.Fori(0, STEPS // 2) as half:
                    i = half * 2
                    for r in range(2):
                        it = i + r
                        cc = Chain(dve, ychain, it * 2)
                        dve.wait_ge(xl[r], i * 8 + 16)
                        ev["saved"].wait(dve, it - 2)
                        ev["done"].wait(dve, it - 1)
                        ys = sums[:, ds(it * BC, BC)].rearrange("p (b f) -> p b f", f=D)
                        cc(v.tensor_tensor(tot[:], ys, stat[:, 7, :].unsqueeze(1).to_broadcast([P, BATCH, D]), ALU.mult))
                        cc(v.tensor_tensor(tot[:], tot[:], par[:, 2, :].unsqueeze(1).to_broadcast([P, BATCH, D]), ALU.add))
                        v.tensor_tensor(xout[:, r], tot[:], xin[:, r], ALU.add).then_inc(ev["done"].sem, 1)



def kernel(x, src, dst, edge_attr_16, edge_attr_9, edge_weight, edge_weight1, L0_gnn_W, L0_gnn_W_e, L0_gnn_a,
           L0_gnn_ln_scale, L0_gnn_ln_bias, L1_gnn_W, L1_gnn_b, L2_gnn_weights, L3_gnn_W_l, L3_gnn_b_l,
           L3_gnn_W_r, L3_gnn_gamma, L3_gnn_beta):
    import concourse.bacc as bacc
    from concourse.bass_utils import run_bass_kernel_spmd

    def by_tile(a, fill=0):
        a = np.asarray(a)
        full = np.full((T * P,) + a.shape[1:], fill, a.dtype)
        full[:E] = a
        return np.ascontiguousarray(np.swapaxes(full.reshape((T, P) + a.shape[1:]), 0, 1))

    xp = np.zeros((NP, D), np.float32)
    xp[:N] = np.asarray(x)
    ef = np.zeros((NCH * G * P, 16), np.float32)
    ef[:E] = np.asarray(edge_attr_16)
    ef = np.ascontiguousarray(ef.reshape(NCH, G, P, 16).transpose(0, 1, 3, 2)).reshape(NCH, P, P)
    CG = clebsch_gordan()
    W2 = np.asarray(L2_gnn_weights)
    a0, a1 = 1.0 / math.sqrt(2 * 32), 1.0 / math.sqrt(3 * 32)
    w2b = np.zeros((3, P, D), np.float32)
    scale = np.ones((3, P), np.float32)
    w2b[0, 0:32, 0:32] = W2[0]
    scale[0, 0:32] = a0 * float(CG[0][0, 0, 0])
    for k in range(3):
        w2b[0, 32 + k:P:3, 32 + k:P:3] = W2[2]
        scale[0, 32 + k:P:3] = a1 * float(CG[2][k, 0, k])
        w2b[1, 32 * k:32 * k + 32, 32 + k:P:3] = W2[1]
        w2b[2, 32 * k:32 * k + 32, 32 + k:P:3] = W2[4]
    scale[1, 0:96] = a1
    w2b[1, 96:128, 0:32] = W2[3]
    scale[1, 96:128] = a0
    scale[2, 0:96] = a1
    flat = lambda a: np.ascontiguousarray(np.asarray(a))
    arrays = dict(
        x=xp, src=by_tile(src), dst=by_tile(dst, -1), w1e=by_tile(np.asarray(edge_weight1)[:, 0]),
        sh=by_tile(edge_attr_9).reshape(P, T * 9), ef=ef, W0=flat(L0_gnn_W), W0T=flat(np.asarray(L0_gnn_W).T),
        WeT=flat(np.asarray(L0_gnn_W_e).T), aT=flat(np.asarray(L0_gnn_a).T),
        ln_scale=flat(L0_gnn_ln_scale)[None], ln_bias=flat(L0_gnn_ln_bias)[None],
        W1T=flat(np.asarray(L1_gnn_W).T), b1=flat(L1_gnn_b)[None], W2b=flat(w2b.transpose(1, 0, 2)),
        W2scale=flat(scale.T), WlT=flat(np.asarray(L3_gnn_W_l).T), bl=flat(L3_gnn_b_l)[None],
        WrT=flat(np.asarray(L3_gnn_W_r).T), gamma=flat(L3_gnn_gamma)[None], beta=flat(L3_gnn_beta)[None],
        ident=np.eye(P, dtype=np.float32), iota=np.tile(np.arange(PG, dtype=np.float32), (P, 1)),
    )
    nc = bacc.Bacc("TRN2", target_bir_lowering=False, num_devices=1)
    given = {k: nc.dram_tensor("in_" + k, a.shape, mybir.dt.from_np(a.dtype), kind="ExternalInput").ap()
             for k, a in arrays.items()}
    out = nc.dram_tensor("out_x", [NP, D], F32, kind="ExternalOutput").ap()
    build(nc, out=out, **given)
    r = run_bass_kernel_spmd(nc, [{"in_" + k: a for k, a in arrays.items()}], core_ids=[0])
    return r.results[0]["out_x"][:N]
```

```python
import math
from contextlib import ExitStack

import numpy as np
import concourse.bass as bass
from concourse import mybir

ALU = mybir.AluOpType
ACT = mybir.ActivationFunctionType
AX = mybir.AxisListType.X
F32 = mybir.dt.float32
BF16 = mybir.dt.bfloat16
I32 = mybir.dt.int32
ds = bass.ds

P = 128
N = 12500
E = 212500
D = 128
H = 4
HD = D // H
G = 8
NCH = -(-E // (P * G))
T = (NCH + 1) * G
NB = -(-N // P)
NP = NB * P
NW = NP + P
BATCH = 7
STEPS = NB // BATCH
BC = BATCH * P
EC = -(-T // (G * STEPS))
HC = BC // 2
PG = 512
R = 4
PAGES = -(-NCH * NB // PG)
DW = D + H
BIG = float(2.0 ** 100)
FAR = float(1 << 20)
EPS = 1e-5
NSH = 16
PAGE_LINKS = 11
TW = 352
assert NB % BATCH == 0 and NCH < 2 * P and G * P * NCH >= E


def clebsch_gordan():
    def fact(n):
        return math.factorial(int(round(n)))

    def su2(j1, j2, j3):
        c3 = np.zeros((2 * j1 + 1, 2 * j2 + 1, 2 * j3 + 1))
        for m1 in range(-j1, j1 + 1):
            for m2 in range(-j2, j2 + 1):
                m3 = m1 + m2
                if abs(m3) > j3:
                    continue
                vmin = int(max(-j1 + j2 + m3, -j1 + m1, 0))
                vmax = int(min(j2 + j3 + m1, j3 - j1 + j2, j3 + m3))
                c = math.sqrt((2 * j3 + 1) * fact(j3 + j1 - j2) * fact(j3 - j1 + j2) * fact(j1 + j2 - j3)
                              / fact(j1 + j2 + j3 + 1))
                c *= math.sqrt(fact(j3 + m3) * fact(j3 - m3) * fact(j1 - m1) * fact(j1 + m1)
                               * fact(j2 - m2) * fact(j2 + m2))
                s = 0.0
                for v in range(vmin, vmax + 1):
                    s += (-1.0) ** (v + j2 + m2) * fact(j2 + j3 + m1 - v) * fact(j1 - m1 + v) / (
                        fact(v) * fact(j3 - j1 + j2 - v) * fact(j3 + m3 - v) * fact(v + j1 - j2 - m3))
                c3[j1 + m1, j2 + m2, j3 + m3] = c * s
        return c3

    def basis(l):
        q = np.zeros((2 * l + 1, 2 * l + 1), dtype=np.complex128)
        for m in range(-l, 0):
            q[l + m, l + abs(m)] = 1.0 / np.sqrt(2.0)
            q[l + m, l - abs(m)] = -1j / np.sqrt(2.0)
        q[l, l] = 1.0
        for m in range(1, l + 1):
            q[l + m, l + abs(m)] = (-1.0) ** m / np.sqrt(2.0)
            q[l + m, l - abs(m)] = 1j * (-1.0) ** m / np.sqrt(2.0)
        return (-1j) ** l * q

    out = []
    for l1, l2, l3 in [(0, 0, 0), (0, 1, 1), (1, 0, 1), (1, 1, 0), (1, 2, 1)]:
        c = np.einsum("ij,kl,mn,ikn->jlm", basis(l1), basis(l2), np.conj(basis(l3).T), su2(l1, l2, l3))
        c = np.real(c)
        out.append((c / np.linalg.norm(c)).astype(np.float32))
    return out


class Event:

    def __init__(self, sem, per=1):
        self.sem, self.per, self.credit = sem, per, R * per

    def start(self, eng):
        eng.sem_inc(self.sem, self.credit)

    def wait(self, eng, v, k=None):
        eng.wait_ge(self.sem, v * self.per + (self.credit + (self.per if k is None else k)))


class Chain:

    def __init__(self, eng, sem, base=0):
        self.eng, self.sem, self.base, self.n = eng, sem, base, 0

    def __call__(self, ins):
        self.n += 1
        ins.then_inc(self.sem, 1)
        self.eng.wait_ge(self.sem, self.base + self.n)


def phase_semaphores(nc, ctx, prefix):
    made = []

    def give_back():
        nc.clear_and_free_semaphores(made)
        nc.all_engine_barrier()

    ctx.callback(give_back)

    def sem(name):
        made.append(nc.alloc_semaphore(prefix + name))
        return made[-1]

    return sem


def build(nc, x, src, dst, w1e, sh, ef, W0, W0T, WeT, aT, ln_scale, ln_bias, W1T, b1, W2b, W2scale,
          WlT, bl, WrT, gamma, beta, ident, iota, out):
    CG = clebsch_gordan()
    outer = ExitStack()

    def dram(name, shape, dt=F32):
        return nc.dram_tensor(name, shape, dt).ap()

    table0 = dram("table0", [NP, DW])
    table1 = dram("table1", [NP, D])
    table2 = dram("table2", [NP, D])
    table3 = dram("table3", [NP, D])
    x1 = dram("x1", [NP, D])
    x2 = dram("x2", [NP, D])
    x3 = dram("x3", [NP, D])
    shx = dram("shx", [P, T * NSH])
    visit_base = dram("visit_base", [PAGES, PG])
    visit_pair = dram("visit_pair", [PAGES, 2 * PG], I32)

    with outer:
        def psb(name, shape, dt=F32):
            return outer.enter_context(nc.sbuf_tensor(name, shape, dt))

        sums = psb("sums", [P, NW])
        aux = psb("aux", [P, NW])
        dstf = psb("dstf", [P, T])
        srci = psb("srci", [P, T], I32)
        identf = psb("identf", [P, P])
        iotaf = psb("iotaf", [P, P])
        epsc = psb("epsc", [P, 1])
        meta = psb("meta", [1, 64], I32)
        pairs = psb("pairs", [1, 2 * PG], I32)
        baseB = psb("baseB", [P, PG])

        phase_visits(nc, dst, src, ident, iota, dstf, srci, identf, iotaf, epsc, meta, sums, aux,
                     visit_base, visit_pair)
        env = (nc, dstf, srci, identf, iotaf, epsc, meta, pairs, baseB, sums, aux, visit_base, visit_pair)
        with nc.sbuf_tensor("efw", [P, STEPS * EC * G * H], F32) as efw:
            phase_first_table(env, x, W0, W0T, aT, WeT, ef, efw, table0)
            phase_attention(env, efw, table0)
        phase_node(env, 0, x, x1, table1, dict(scale=ln_scale, bias=ln_bias))
        phase_sum(env, 1, table1, w1e)
        phase_node(env, 1, x1, x2, table2, dict(W=W1T, b=b1))
        phase_factors(env, sh, shx, CG)
        phase_tensor_product(env, table2, shx, W2b, W2scale)
        phase_node(env, 2, x2, x3, table3, {})
        phase_sum(env, 3, table3, None)
        phase_last(env, x3, table3, WlT, WrT, bl, gamma, beta, out)



def phase_visits(nc, dst, src, ident, iota, dstf, srci, identf, iotaf, epsc, meta, sums, aux,
                 visit_base, visit_pair):
    with ExitStack() as ctx:
        sb = lambda n, s, d=F32: ctx.enter_context(nc.sbuf_tensor(n, s, d))
        ps = lambda n, s, d=F32: ctx.enter_context(nc.psum_tensor(n, s, d))
        sem = phase_semaphores(nc, ctx, "")
        CP = 2 * P
        dsti = sb("v_dsti", [P, T], I32)
        dpos = sb("v_dpos", [P, T])
        hi = sb("v_hi", [P, CP])
        lo = sb("v_lo", [P, CP])
        k0 = sb("v_k0", [P, PG])
        kcur = sb("v_kcur", [P, PG])
        ind = sb("v_ind", [P, 2, PG])
        tmp = sb("v_tmp", [P, PG])
        ones = sb("v_ones", [P, P])
        tri = sb("v_tri", [P, P])
        st = sb("v_st", [P, 32])
        sti = sb("v_sti", [P, 2], I32)
        ki = sb("v_ki", [1, 1], I32)
        kf = sb("v_kf", [1, 128])
        vb = sb("v_vb", [P, 4, P])
        baserow = sb("v_baserow", [P, PG])
        tilerow = sb("v_tilerow", [P, PG])
        pairrow = sb("v_pairrow", [1, PG, 2], I32)
        pt = ps("v_pt", [P, 4, P])
        pc = ps("v_pc", [P, 512])
        pbase = ps("v_pbase", [P, PG])
        ptile = ps("v_ptile", [P, PG])
        loaded, chain, red, turned, mm, mmd, pgd, pgm, stored, metac = (
            sem(n) for n in ("v_loaded", "v_chain", "v_red", "v_turned", "v_mm", "v_mmd", "v_pgd", "v_pgm",
                             "v_stored", "v_metac"))
        freed, chain2 = sem("v_freed"), sem("v_chain2")
        HI, LO, CNT, IDX, CUM, END, VAL, PRE = (slice(2 * i, 2 * i + 2) for i in range(8))

        with nc.Block() as block:
            @block.sync
            def _(sp):
                sp.dma_start(dsti[:], dst).then_inc(loaded, 16)
                sp.dma_start(srci[:], src).then_inc(loaded, 16)
                sp.dma_start(identf[:], ident).then_inc(loaded, 16)
                sp.dma_start(iotaf[:], iota[:, 0:P]).then_inc(loaded, 16)
                sp.dma_start(k0[:], iota).then_inc(loaded, 16)
                sp.wait_ge(metac, 1)
                npages = sp.value_load(meta[0:1, 0:1], min_val=1, max_val=PAGES)
                with sp.Fori(0, npages) as pg:
                    sp.wait_ge(pgd, pg + 1)
                    sp.dma_start(visit_base[ds(pg, 1), :], baserow[0:1, :]).then_inc(stored, 16)
                    sp.dma_start(visit_pair[ds(pg, 1), :], pairrow[:].rearrange("o k c -> o (k c)")).then_inc(stored, 16)
                    sp.wait_ge(stored, pg * 32 + 32)
                    sp.sem_inc(freed, 1)

            @block.tensor
            def _(pe):
                pe.wait_ge(red, 1)
                pe.wait_ge(loaded, 80)
                for j in range(2):
                    pe.transpose(pt[:, j, :], hi[:, j * P:(j + 1) * P], identf[:])
                    ins = pe.transpose(pt[:, 2 + j, :], lo[:, j * P:(j + 1) * P], identf[:])
                ins.then_inc(turned, 1)
                pe.wait_ge(mm, 1)
                pe.matmul(pc[:, 0:2], tri[:], st[:, CNT], start=True, stop=False)
                pe.matmul(pc[:, 0:2], ones[:], st[:, PRE], start=False, stop=True).then_inc(mmd, 1)
                pe.wait_ge(mm, 2)
                pe.matmul(pc[:, 2:3], ones[:], st[:, 18:19], start=True, stop=True).then_inc(mmd, 1)
                pe.wait_ge(metac, 1)
                npages = pe.value_load(meta[0:1, 0:1], min_val=1, max_val=PAGES)
                with pe.Fori(0, npages) as pg:
                    pe.wait_ge(pgm, pg + 1)
                    for q in range(PG // 512):
                        c = slice(512 * q, 512 * q + 512)
                        for j in range(2):
                            pe.matmul(pbase[:, c], vb[:, j, :], ind[:, j, c], start=(j == 0), stop=(j == 1))
                        for j in range(2):
                            ins = pe.matmul(ptile[:, c], vb[:, 2 + j, :], ind[:, j, c], start=(j == 0), stop=(j == 1))
                    ins.then_inc(mmd, 1)

            @block.vector
            def _(dve):
                v = nc.vector
                c = Chain(dve, chain)
                v.memset(sums[:], 0.0)
                v.memset(aux[:], 0.0)
                v.memset(ones[:], 1.0)
                v.memset(epsc[:], EPS)
                v.memset(st[:], 0.0)
                v.memset(hi[:], 0.0)
                c(v.memset(lo[:], 0.0))
                c(v.memset(aux[0:H, :], -1e9))
                dve.wait_ge(loaded, 80)
                c(v.tensor_copy(dstf[:], dsti[:]))
                c(v.tensor_scalar(dpos[:], dstf[:], 0.0, FAR, ALU.is_lt, ALU.mult))
                c(v.tensor_tensor(dpos[:], dpos[:], dstf[:], ALU.add))
                c(v.tensor_reduce(hi[:, 0:NCH + 1], dstf[:].rearrange("p (c g) -> p c g", g=G), AX, ALU.max))
                v.tensor_reduce(lo[:, 0:NCH + 1], dpos[:].rearrange("p (c g) -> p c g", g=G), AX, ALU.min).then_inc(red, 1)
                dve.wait_ge(turned, 1)
                c(v.tensor_reduce(st[:, HI], pt[:, 0:2, :], AX, ALU.max))
                c(v.tensor_reduce(st[:, LO], pt[:, 2:4, :], AX, ALU.min))
                c(v.tensor_tensor(st[:, CNT], st[:, HI], st[:, LO], ALU.subtract))
                c(v.tensor_copy(sti[:], st[:, CNT]))
                c(v.tensor_single_scalar(sti[:], sti[:], 7, ALU.arith_shift_right))
                c(v.tensor_copy(st[:, CNT], sti[:]))
                c(v.tensor_tensor(tri[:], identf[:], iotaf[:], ALU.mult))
                c(v.tensor_reduce(st[:, 6:7], tri[:], AX, ALU.add))
                c(v.tensor_scalar(st[:, 7:8], st[:, 6:7], float(P), None, ALU.add))
                c(v.tensor_scalar(st[:, 16:18], st[:, IDX], float(NCH), None, ALU.is_lt))
                c(v.tensor_scalar(st[:, CNT], st[:, CNT], 1.0, None, ALU.add))
                c(v.tensor_tensor(st[:, CNT], st[:, CNT], st[:, 16:18], ALU.mult))
                c(v.tensor_scalar(st[:, 16:18], st[:, 16:18], -FAR, FAR, ALU.mult, ALU.add))
                c(v.tensor_tensor(st[:, CNT], st[:, CNT], st[:, 16:18], ALU.add))
                c(v.tensor_copy(st[:, PRE.start + 1:PRE.stop], st[:, CNT.start:CNT.start + 1]))
                v.tensor_scalar(tri[:], iotaf[:], st[:, 6:7], None, ALU.is_gt).then_inc(mm, 1)
                dve.wait_ge(mm, 1)
                dve.wait_ge(mmd, 1)
                c(v.tensor_copy(st[:, CUM], pc[:, 0:2]))
                c(v.tensor_tensor(st[:, END], st[:, CUM], st[:, CNT], ALU.add))
                c(v.tensor_scalar(st[:, 16:18], st[:, CUM], -float(P), None, ALU.mult))
                c(v.tensor_tensor(st[:, VAL], st[:, 16:18], st[:, LO], ALU.add))
                for j in range(2):
                    c(v.tensor_scalar(vb[:, j, :], ones[:], st[:, VAL.start + j:VAL.start + j + 1], None, ALU.mult))
                    c(v.tensor_scalar(vb[:, 2 + j, :], ones[:], st[:, IDX.start + j:IDX.start + j + 1], float(G),
                                      ALU.mult, ALU.mult))
                lr, lp = NCH % P, NCH // P
                v.tensor_scalar(st[:, 18:19], identf[:, lr:lr + 1], st[:, CUM.start + lp:CUM.start + lp + 1],
                                None, ALU.mult).then_inc(mm, 1)
                dve.wait_ge(mmd, 2)
                c(v.tensor_copy(ki[:, 0:1], pc[0:1, 2:3]))
                c(v.tensor_single_scalar(ki[:, 0:1], ki[:, 0:1], R - 1, ALU.add))
                c(v.tensor_single_scalar(ki[:, 0:1], ki[:, 0:1], R.bit_length() - 1, ALU.arith_shift_right))
                c(v.tensor_copy(kf[:, 0:1], ki[:, 0:1]))
                turns = PG // R
                c(v.tensor_scalar(kf[:, 1:1 + PAGES], k0[0:1, 0:PAGES], -float(turns), kf[:, 0:1], ALU.mult, ALU.add))
                c(v.tensor_scalar(kf[:, 64:64 + PAGES], kf[:, 1:1 + PAGES], 0.0, None, ALU.is_gt))
                c(v.tensor_scalar(kf[:, 1:1 + PAGES], kf[:, 1:1 + PAGES], 2.0, float(turns), ALU.max, ALU.min))
                c(v.tensor_scalar(kf[:, 1:1 + PAGES], kf[:, 1:1 + PAGES], -2.0, None, ALU.add))
                c(v.tensor_reduce(kf[:, 0:1], kf[:, 64:64 + PAGES], AX, ALU.add))
                c(v.tensor_copy(meta[0:1, 0:1 + PAGES], kf[:, 0:1 + PAGES]))
                c(v.tensor_scalar(kcur[:], k0[:], -float(PG), None, ALU.add))
                dve.engine_nop().then_inc(metac, 1)
                dve.wait_ge(metac, 1)
                npages = dve.value_load(meta[0:1, 0:1], min_val=1, max_val=PAGES)
                with dve.Fori(0, npages) as pg:
                    c = Chain(dve, chain2, pg * PAGE_LINKS)
                    c(v.tensor_scalar(kcur[:], kcur[:], float(PG), None, ALU.add))
                    for j in range(2):
                        c(v.tensor_scalar(tmp[:], kcur[:], st[:, CUM.start + j:CUM.start + j + 1], None, ALU.is_ge))
                        c(v.scalar_tensor_tensor(out=ind[:, j, :], in0=kcur[:], scalar=st[:, END.start + j:END.start + j + 1],
                                                 in1=tmp[:], op0=ALU.is_lt, op1=ALU.mult))
                    dve.sem_inc(pgm, 1)
                    dve.wait_ge(mmd, pg + 3)
                    c(v.tensor_copy(tilerow[:], ptile[:]))
                    c(v.tensor_scalar(baserow[:], kcur[:], float(P), None, ALU.mult))
                    c(v.tensor_tensor(baserow[:], baserow[:], pbase[:], ALU.add))
                    c(v.tensor_scalar(baserow[:], baserow[:], 0.0, float(NP), ALU.max, ALU.min))
                    c(v.tensor_copy(pairrow[:, :, 0], tilerow[0:1, :]))
                    c(v.tensor_copy(pairrow[:, :, 1], baserow[0:1, :]))
                    assert c.n == PAGE_LINKS
                    dve.sem_inc(pgd, 1)
                    dve.wait_ge(freed, pg + 1)



class Visits:

    def __init__(self, env, sem):
        (self.nc, self.dstf, self.srci, self.identf, self.iotaf, self.epsc, self.meta, self.pairs, self.baseB,
         self.sums, self.aux, self.visit_base, self.visit_pair) = env
        self.page_loaded, self.page_done = sem("page_loaded"), sem("page_done")
        self.regs = {}

    def serve(self, sp, users, turn=None):
        npages = sp.value_load(self.meta[0:1, 0:1], min_val=1, max_val=PAGES)
        sp.sem_inc(self.page_done, 1)
        with sp.Fori(0, npages) as pg:
            sp.wait_ge(self.page_done, pg * users + 1)
            sp.dma_start(self.pairs[:], self.visit_pair[ds(pg, 1), :]).then_inc(self.page_loaded, 16)
            sp.dma_start(self.baseB[:], self.visit_base[ds(pg, 1), :].to_broadcast([P, PG])).then_inc(self.page_loaded, 16)
            if turn:
                self.page(sp, pg, turn, 0)

    def page(self, eng, pg, turn, depth):
        assert depth <= R
        eng.wait_ge(self.page_loaded, pg * 32 + 32)
        groups = eng.value_load(self.meta[0:1, ds(pg + 1, 1)], min_val=0, max_val=PG // R - 2) + 2

        def visit(first, off):
            return first + off, off % R, pg * PG + first + off

        for u in range(R):
            turn(*(visit(0, u - lag) if u >= lag else None for lag in range(depth + 1)))
        with eng.Fori(0, groups - 1) as g:
            for u in range(R):
                turn(*(visit(g * R, R + u - lag) for lag in range(depth + 1)))
        for u in range(depth):
            turn(*(visit(groups * R - R, R + u - lag) if lag > u else None for lag in range(depth + 1)))

    def loop(self, eng, turn, depth=0):
        npages = eng.value_load(self.meta[0:1, 0:1], min_val=1, max_val=PAGES)
        with eng.Fori(0, npages) as pg:
            self.page(eng, pg, turn, depth)
            eng.drain().then_inc(self.page_done, 1)

    def pair(self, eng, i, slot=None):
        if (eng, slot) not in self.regs:
            self.regs[eng, slot] = [eng.alloc_register(f"pair{k}_{self.nc.next_id()}") for k in range(2)]
        regs = self.regs[eng, slot]
        eng.load(regs, self.pairs[0:1, ds(i * 2, 2)])
        return self.held(eng, slot)

    def held(self, eng, slot):
        tile, node = self.regs[eng, slot]
        return eng.snap(tile, min_val=0, max_val=T - G), eng.snap(node, min_val=0, max_val=NP)


def gather_rows(vis, pool, table, width, slots, rows, copied, landed, free):
    g = vis.nc.gpsimd
    copied.start(pool)

    def turn(visit):
        i, r, v = visit
        tile, _ = vis.pair(pool, i)
        for used in free:
            used.wait(pool, v - R)
        g.tensor_copy(slots[:, r * G:(r + 1) * G], vis.srci[:, ds(tile, G)]).then_inc(copied.sem, 1)
        copied.wait(pool, v)
        g.nop(nofuse=True)
        for t in range(G):
            g.indirect_dma_start(rows[:, r, t, 0:width], None, table,
                                 bass.IndirectOffsetOnAxis(slots[:, r * G + t:r * G + t + 1], 0)).then_inc(landed[r], 16)

    vis.loop(pool, turn)


def wait_landed(eng, landed, r, v):
    eng.wait_ge(landed[r], (v - r) * (16 * G // R) + 16 * G)


def norm_vector(nc, dve, c, ev, it, k, xin, xc, sq, s):
    v = nc.vector
    c(v.tensor_reduce(s[:, 0:BATCH], xin, AX, ALU.add))
    c(v.tensor_scalar(s[:, 8:8 + BATCH], s[:, 0:BATCH], -1.0 / D, None, ALU.mult))
    v.tensor_tensor(xc, xin, s[:, 8:8 + BATCH].unsqueeze(2).to_broadcast([P, BATCH, D]), ALU.add).then_inc(ev["centred"].sem, 1)
    ev["squared"].wait(dve, it, k)
    v.tensor_reduce(s[:, 16:16 + BATCH], sq, AX, ALU.add).then_inc(ev["varied"].sem, 1)
    ev["rooted"].wait(dve, it, k)
    c(v.reciprocal(s[:, 32:32 + BATCH], s[:, 24:24 + BATCH]))
    c(v.tensor_tensor(xc, xc, s[:, 32:32 + BATCH].unsqueeze(2).to_broadcast([P, BATCH, D]), ALU.mult))


def norm_scalar(nc, act, ev, it, k, xc, sq, s, epsc):
    ev["centred"].wait(act, it, k)
    nc.scalar.activation(sq, xc, ACT.Square).then_inc(ev["squared"].sem, 1)
    ev["varied"].wait(act, it, k)
    nc.scalar.activation(s[:, 24:24 + BATCH], s[:, 16:16 + BATCH], ACT.Sqrt, bias=epsc[:], scale=1.0 / D).then_inc(ev["rooted"].sem, 1)


def blocks_of(table, it):
    return table.rearrange("(b p) f -> p b f", p=P)[:, ds(it * BATCH, BATCH), :]


def load_blocks(nc, pool, streams, used):
    with pool.Fori(0, STEPS // 2) as half:
        i = half * 2
        for r in range(2):
            used.wait(pool, i + r - 2)
            pool.nop(nofuse=True)
            for table, slot, landed in streams:
                pool.dma_start(slot[:, r], blocks_of(table, i + r)).then_inc(landed[r], 16)



def phase_first_table(env, x, W0, W0T, aT, WeT, ef, efw, table0):
    nc, dstf, srci, identf, iotaf, epsc, meta, pairs, baseB, sums, aux, visit_base, visit_pair = env
    with ExitStack() as ctx:
        sb = lambda n, s, d=F32: ctx.enter_context(nc.sbuf_tensor(n, s, d))
        ps = lambda n, s, d=F32: ctx.enter_context(nc.psum_tensor(n, s, d))
        sem = phase_semaphores(nc, ctx, "")
        WX = DW + H
        w0 = sb("t_w0", [P, D])
        wext = sb("t_wext", [P, DW + H])
        asrc = sb("t_asrc", [P, H])
        adst = sb("t_adst", [P, H])
        we = sb("t_we", [P, G * H])
        xin = sb("t_xin", [P, 2, BATCH, D])
        xc = sb("t_xc", [P, BATCH, D])
        sq = sb("t_sq", [P, BATCH, D])
        s = sb("t_s", [P, 40])
        hT = sb("t_hT", [P, BC])
        row = sb("t_row", [P, BATCH, DW])
        sdp = sb("t_sdp", [P, BATCH, 32 + 3 * H])
        sdh = sb("t_sdh", [P, 2, BATCH, H], BF16)
        sdf = sb("t_sdf", [P, BATCH, H])
        eft = sb("t_eft", [P, 2, EC, P])
        pT = ps("t_pT", [P, 1024])
        pw = ps("t_pw", [P, 3, 512])
        pd = ps("t_pd", [P, 2, 512])
        pe_ = ps("t_pe", [P, 512])
        loaded, zeroed, placed, wready = (sem(n) for n in ("t_loaded", "t_zeroed", "t_placed", "t_wready"))
        xl = [sem("t_xl0"), sem("t_xl1")]
        stored, efl0, efl1, chain = sem("t_stored"), sem("t_efl0"), sem("t_efl1"), sem("t_chain")
        efl = [efl0, efl1]
        ev = {n: Event(sem("t_" + n)) for n in
              ("centred", "squared", "varied", "rooted", "normed", "turned", "copied", "projected", "rowed", "ef_mm", "ef_out", "kept", "parted", "spread")}

        with nc.Block() as block:
            @block.sync
            def _(sp):
                sp.dma_start(w0[:], W0).then_inc(loaded, 16)
                sp.dma_start(wext[:, 0:D], W0T).then_inc(loaded, 16)
                sp.wait_ge(zeroed, 1)
                with nc.allow_non_contiguous_dma(reason="attention vectors and W_e into block diagonals"):
                    for h in range(H):
                        sp.dma_start(asrc[h * HD:(h + 1) * HD, h:h + 1], aT[0:HD, h:h + 1]).then_inc(placed, 16)
                        sp.dma_start(adst[h * HD:(h + 1) * HD, h:h + 1], aT[HD:2 * HD, h:h + 1]).then_inc(placed, 16)
                    for t in range(G):
                        sp.dma_start(we[16 * t:16 * t + 16, H * t:H * t + H], WeT).then_inc(placed, 16)
                ev["kept"].start(sp)
                with sp.Fori(0, STEPS) as it:
                    ev["rowed"].wait(sp, it)
                    sp.dma_start(blocks_of(table0, it), row[:]).then_inc(stored, 16)
                    sp.wait_ge(stored, it * 16 + 16)
                    sp.sem_inc(ev["kept"].sem, 1)

            @block.gpsimd
            def _(pool):
                with pool.Fori(0, STEPS // 2) as half:
                    i = half * 2
                    for r in range(2):
                        ev["centred"].wait(pool, i + r - 2)
                        ev["ef_mm"].wait(pool, i + r - 2)
                        pool.nop(nofuse=True)
                        pool.dma_start(xin[:, r], blocks_of(x, i + r)).then_inc(xl[r], 16)
                        pool.dma_start(eft[:, r], ef[:, ds((i + r) * EC, EC), :]).then_inc(efl[r], 16)

            @block.tensor
            def _(pe):
                for n in ("turned", "projected", "spread", "ef_mm"):
                    ev[n].start(pe)
                pe.wait_ge(loaded, 32)
                pe.wait_ge(placed, 16 * (2 * H + G))
                pe.matmul(pe_[:, 0:H], w0[:], asrc[:], start=True, stop=True)
                pe.matmul(pe_[:, H:2 * H], w0[:], adst[:], start=True, stop=True).then_inc(wready, 1)
                pe.wait_ge(wready, 2)
                with pe.Fori(0, STEPS // 2) as half:
                    i = half * 2
                    for r in range(2):
                        it = i + r
                        pe.wait_ge(efl[r], i * 8 + 16)
                        ev["ef_out"].wait(pe, it - 1)
                        for k in range(EC):
                            ins = pe.matmul(pe_[:, k * G * H:(k + 1) * G * H], eft[:, r, k, :], we[:], start=True, stop=True)
                        ins.then_inc(ev["ef_mm"].sem, 1)
                        ev["normed"].wait(pe, it)
                        ev["copied"].wait(pe, it - 1)
                        for b in range(BATCH):
                            ins = pe.transpose(pT[:, b * P:(b + 1) * P], xc[:, b, :], identf[:])
                        ins.then_inc(ev["turned"].sem, 1)
                        ev["copied"].wait(pe, it)
                        ev["rowed"].wait(pe, it - 1)
                        for b in range(BATCH):
                            ins = pe.matmul(pw[:, b // 3, (b % 3) * WX:(b % 3 + 1) * WX], hT[:, b * P:(b + 1) * P], wext[:],
                                            start=True, stop=True)
                        ins.then_inc(ev["projected"].sem, 1)
                        ev["parted"].wait(pe, it)
                        pe.nop(nofuse=True)
                        for b in range(BATCH):
                            ins = pe.transpose(pd[0:32 + 3 * H, b // 4, (b % 4) * P:(b % 4 + 1) * P], sdp[:, b, :], identf[:])
                        ins.then_inc(ev["spread"].sem, 1)

            @block.scalar
            def _(act):
                for n in ("squared", "rooted", "copied", "ef_out"):
                    ev[n].start(act)
                with act.Fori(0, STEPS) as it:
                    norm_scalar(nc, act, ev, it, 1, xc[:], sq[:], s, epsc)
                    ev["ef_mm"].wait(act, it)
                    act.nop(nofuse=True)
                    nc.scalar.activation(efw[:, ds(it * (EC * G * H), EC * G * H)], pe_[:, 0:EC * G * H], ACT.Copy)\
                        .then_inc(ev["ef_out"].sem, 1)
                    ev["turned"].wait(act, it)
                    ev["projected"].wait(act, it - 1)
                    nc.scalar.activation(hT[:], pT[:, 0:BC], ACT.Copy).then_inc(ev["copied"].sem, 1)

            @block.vector
            def _(dve):
                v = nc.vector
                for n in ("centred", "varied", "normed", "rowed", "parted"):
                    ev[n].start(dve)
                v.memset(asrc[:], 0.0)
                v.memset(adst[:], 0.0)
                v.memset(we[:], 0.0).then_inc(zeroed, 1)
                dve.wait_ge(wready, 1)
                dve.wait_ge(loaded, 32)
                v.memset(sdp[:], 0.0)
                v.tensor_copy(wext[:, D:WX], pe_[:, 0:2 * H]).then_inc(wready, 1)
                with dve.Fori(0, STEPS // 2) as half:
                    i = half * 2
                    for r in range(2):
                        it = i + r
                        c = Chain(dve, chain, it * 12)
                        dve.wait_ge(xl[r], i * 8 + 16)
                        ev["turned"].wait(dve, it - 1)
                        norm_vector(nc, dve, c, ev, it, 1, xin[:, r], xc[:], sq[:], s)
                        v.tensor_single_scalar(xc[:], xc[:], 0.0, ALU.max).then_inc(ev["normed"].sem, 1)
                        ev["projected"].wait(dve, it)
                        ev["kept"].wait(dve, it - 1)
                        three = lambda q, n: pw[:, q, 0:n * WX].rearrange("p (b f) -> p b f", f=WX)
                        for q, n in ((0, 3), (1, 3), (2, 1)):
                            v.tensor_copy(row[:, 3 * q:3 * q + n, :], three(q, n)[:, :, 0:DW])
                            ins = v.tensor_copy(sdf[:, 3 * q:3 * q + n, :], three(q, n)[:, :, DW:WX])
                        c(ins)
                        part = lambda k: sdp[:, :, 32 + k * H:32 + (k + 1) * H]
                        ev["spread"].wait(dve, it - 1)
                        c(v.tensor_copy(sdh[:, 0], sdf[:]))
                        c(v.tensor_copy(part(0), sdh[:, 0]))
                        c(v.tensor_tensor(sdf[:], sdf[:], part(0), ALU.subtract))
                        c(v.tensor_copy(sdh[:, 1], sdf[:]))
                        c(v.tensor_copy(part(1), sdh[:, 1]))
                        c(v.tensor_tensor(part(2), sdf[:], part(1), ALU.subtract))
                        dve.sem_inc(ev["parted"].sem, 1)
                        ev["spread"].wait(dve, it)
                        v.tensor_copy(aux[32:32 + 3 * H, ds(it * BC, 4 * P)], pd[32:32 + 3 * H, 0, :])
                        c(v.tensor_copy(aux[32:32 + 3 * H, ds(it * BC + 4 * P, 3 * P)], pd[32:32 + 3 * H, 1, 0:3 * P]))
                        assert c.n == 12, c.n
                        dve.sem_inc(ev["rowed"].sem, 1)



def phase_attention(env, efw, table0):
    nc, dstf, srci, identf, iotaf, epsc, meta, pairs, baseB, sums, aux, visit_base, visit_pair = env
    with ExitStack() as ctx:
        sb = lambda n, s, d=F32: ctx.enter_context(nc.sbuf_tensor(n, s, d))
        ps = lambda n, s, d=F32: ctx.enter_context(nc.psum_tensor(n, s, d))
        sem = phase_semaphores(nc, ctx, "a_")
        vis = Visits(env, sem)
        GH = G * H
        PH = 3 * H
        slots = sb("a_slots", [P, R * G], I32)
        rows = sb("a_rows", [P, R, G, DW])
        rel = sb("a_rel", [P, 2, G])
        far = sb("a_far", [P, R, G, P], BF16)
        hot = sb("a_hot", [P, G, P])
        hotT = sb("a_hotT", [P, R, G, P], BF16)
        wsd = sb("a_wsd", [PH, P])
        sdn = sb("a_sdn", [P, PH], BF16)
        zs = sb("a_zs", [P, GH])
        z = sb("a_z", [P, GH])
        z2 = sb("a_z2", [P, GH])
        attn = sb("a_attn", [P, R, GH])
        parts = sb("a_parts", [P, 3, GH], BF16)
        rest = sb("a_rest", [P, GH])
        partsT = sb("a_partsT", [3 * GH, 2, P], BF16)
        pick = sb("a_pick", [3 * GH, GH, P], BF16)
        id3 = sb("a_id3", [3 * GH, GH])
        identb = sb("a_identb", [P, P], BF16)
        ident4 = sb("a_ident4", [P, H, P], BF16)
        iotab = sb("a_iotab", [P, P], BF16)
        tmax = sb("a_tmax", [P, H, G])
        cmax = sb("a_cmax", [P, 2, H])
        wm = sb("a_wm", [H, P])
        top = sb("a_top", [P, H])
        pack = sb("a_pack", [P, 68])
        pack2 = sb("a_pack2", [P, 2, 68])
        mparts = sb("a_mparts", [P, 3, H], BF16)
        mrest = sb("a_mrest", [P, H])
        dm = sb("a_dm", [P, H])
        ms = sb("a_ms", [P, GH])
        e1 = sb("a_e1", [P, GH])
        e2 = sb("a_e2", [P, GH])
        msg = sb("a_msg", [P, 2, G, DW])
        agg = sb("a_agg", [P, D])
        scale_rows = sb("a_scale_rows", [P, 2, D])
        pz = ps("a_pz", [P, 3, 512])
        phT = ps("a_phT", [P, G * P], BF16)
        pa = ps("a_pa", [P, 512])
        pm = ps("a_pm", [P, 512])
        pagg = ps("a_pagg", [P, 512])
        ptr = ps("a_ptr", [P, 512])
        SD, NM, EDGES = slice(0, PH), slice(0, H), slice(32, 32 + G * PH)
        ptop = phT[:, 0:2 * P].bitcast(F32)
        ppT = pa[:, 256:256 + P // 2].bitcast(BF16)
        landed = [sem(f"landed{r}") for r in range(R)]
        setup, setup_chain = sem("setup"), sem("setup_chain")
        names = ("copied rel_ far_ wsd_ sdn_ hot_ phT_ hotT_ sd sg zs_ z_ z2_ attn_ hi_ r1_ mid_ lo_ ppT_ partsT_ "
                 "cmax_ wm_ nm mnew dm_ mhi_ mr1_ mmid_ mlo_ sc mg ms_ e1_ e2_ ex msg_ pagg_ aggden topT_ ptr_ num1 num2 "
                 "den1 den2 mput").split()
        ev = {n: Event(sem(n)) for n in names}
        ev["zmm"], ev["zred"] = Event(sem("zmm"), G), Event(sem("zred"), G)

        def owns(eng, names):
            for n in names.split():
                ev[n].start(eng)

        with nc.Block() as block:
            @block.sync
            def _(sp):
                vis.serve(sp, 4)

            @block.gpsimd
            def _(pool):
                gather_rows(vis, pool, table0, DW, slots, rows, ev["copied"], landed, [ev["msg_"]])

            @block.tensor
            def _(pe):
                owns(pe, "sd sg phT_ ppT_ zmm nm mg pagg_ topT_ ptr_")
                pe.wait_ge(setup, 1)

                def turn(now, mid, old, fin):
                    def highest(*tiles):
                        if mid:
                            i, r, v = mid
                            for t in tiles:
                                if t == 0:
                                    ev["partsT_"].wait(pe, v)
                                ev["zred"].wait(pe, v, (-1, 0, 0)[t] if t < 3 else t - 2)
                                pe.matmul(pz[:, t % 3, :], far[:, r, t, :], ident4[:].rearrange("p h e -> p (h e)"),
                                          start=True, stop=False)
                                for h in range(H):
                                    ins = pe.matmul(pz[:, t % 3, h * P:(h + 1) * P], pick[:, t * H + h, :], partsT[:, r % 2],
                                                    start=False, stop=(h == H - 1))
                                ins.then_inc(ev["zmm"].sem, 1)

                    highest(0, 1, 2)
                    if now:
                        i, r, v = now
                        ev["wsd_"].wait(pe, v)
                        ev["partsT_"].wait(pe, v - 1)
                        pe.nop(nofuse=True)
                        pe.transpose(pa[:, SD], wsd[:], identf[0:PH, 0:PH]).then_inc(ev["sd"].sem, 1)
                        ev["far_"].wait(pe, v)
                        ev["hotT_"].wait(pe, v - 1)
                        ev["mput"].wait(pe, v - 3)
                        for t in range(G):
                            ins = pe.transpose(phT[:, t * P:(t + 1) * P], far[:, r, t, :], identb[:])
                        ins.then_inc(ev["phT_"].sem, 1)
                    highest(3)
                    if old:
                        i, r, v = old
                        ev["mlo_"].wait(pe, v)
                        ev["dm_"].wait(pe, v)
                        for t in range(G):
                            ins = pe.matmul(pm[:, 32 + t * PH:32 + (t + 1) * PH], hotT[:, r, t, :],
                                            mparts[:].rearrange("p k h -> p (k h)"), start=True, stop=True)
                        ins.then_inc(ev["mg"].sem, 1)
                    if now:
                        i, r, v = now
                        ev["sdn_"].wait(pe, v)
                        ev["hotT_"].wait(pe, v)
                        for t in range(G):
                            ins = pe.matmul(pa[:, 32 + t * PH:32 + (t + 1) * PH], hotT[:, r, t, :], sdn[:], start=True, stop=True)
                        ins.then_inc(ev["sg"].sem, 1)
                    if old:
                        pe.transpose(ptop[0:H, 0:P], top[:], identf[:]).then_inc(ev["topT_"].sem, 1)
                    highest(4, 5)
                    highest(6)
                    if mid:
                        i, r, v = mid
                        ev["wm_"].wait(pe, v)
                        ev["ms_"].wait(pe, v - 1)
                        pe.nop(nofuse=True)
                        pe.transpose(pm[:, NM], wm[:], identf[0:H, 0:H]).then_inc(ev["nm"].sem, 1)
                    highest(7)
                    if fin:
                        i, r, v = fin
                        q = r % 2
                        ev["msg_"].wait(pe, v)
                        ev["hot_"].wait(pe, v)
                        ev["aggden"].wait(pe, v - 1)
                        for t in range(G):
                            ins = pe.matmul(pagg[:, 0:DW], hot[:, t, :], msg[:, q, t, :], start=(t == 0), stop=(t == G - 1))
                        ins.then_inc(ev["pagg_"].sem, 1)
                        ev["sc"].wait(pe, v)
                        ev["aggden"].wait(pe, v)
                        ev["num2"].wait(pe, v - 1)
                        ev["den2"].wait(pe, v - 1)
                        pe.transpose(ptr[:, 0:P], agg[:], identf[:])
                        pe.matmul(ptr[:, P:2 * P], scale_rows[:, q], identf[:], start=True, stop=True)
                        pe.transpose(ptr[0:68, 2 * P:3 * P], pack[:], identf[:])
                        pe.transpose(ptr[0:68, 3 * P:4 * P], pack2[:, q], identf[:]).then_inc(ev["ptr_"].sem, 1)
                    if now:
                        i, r, v = now
                        ev["lo_"].wait(pe, v)
                        pe.transpose(ppT[0:3 * GH, :], parts[:].rearrange("p a b -> p (a b)"), identb[:]).then_inc(ev["ppT_"].sem, 1)

                vis.loop(pe, turn, 3)

            @block.scalar
            def _(act):
                a = nc.scalar
                owns(act, "wsd_ sdn_ hot_ hotT_ partsT_ wm_ sc ex aggden mput")
                act.wait_ge(setup, 1)

                def turn(now, mid, old, fin):
                    if now:
                        i, r, v = now
                        _, node = vis.pair(act, i)
                        ev["sd"].wait(act, v - 1)
                        act.nop(nofuse=True)
                        a.activation(wsd[:], aux[32:32 + PH, ds(node, P)], ACT.Copy).then_inc(ev["wsd_"].sem, 1)
                    if old:
                        i, r, v = old
                        q = r % 2
                        _, old_node = vis.pair(act, i)
                        ev["dm_"].wait(act, v)
                        ev["ptr_"].wait(act, v - 2)
                        a.activation(pack2[:, q, 64:68], dm[:], ACT.Exp).then_inc(ev["sc"].sem, 1)
                    if now:
                        i, r, v = now
                        ev["sd"].wait(act, v)
                        ev["sg"].wait(act, v - 1)
                        a.activation(sdn[:], pa[:, SD], ACT.Copy).then_inc(ev["sdn_"].sem, 1)
                    if old:
                        i, r, v = old
                        ev["sc"].wait(act, v)
                        a.activation(scale_rows[:, q].rearrange("p (h d) -> p h d", h=H),
                                     pack2[:, q, 64:68].unsqueeze(2).to_broadcast([P, H, HD]), ACT.Copy)
                    if now:
                        i, r, v = now
                        ev["phT_"].wait(act, v)
                        ev["mg"].wait(act, v - R)
                        a.activation(hotT[:, r].rearrange("p t e -> p (t e)"), phT[:], ACT.Copy, scale=1.0 / BIG, bias=1.0)\
                            .then_inc(ev["hotT_"].sem, 1)
                    if fin:
                        i, r, v = fin
                        ev["pagg_"].wait(act, v - 1)
                        a.activation(hot[:], far[:, r], ACT.Copy, scale=1.0 / BIG, bias=1.0).then_inc(ev["hot_"].sem, 1)
                    if old:
                        i, r, v = old
                        q = r % 2
                        ev["topT_"].wait(act, v)
                        act.nop(nofuse=True)
                        a.activation(aux[0:H, ds(old_node, P)], ptop[0:H, 0:P], ACT.Copy).then_inc(ev["mput"].sem, 1)
                    if mid:
                        i, r, v = mid
                        _, mid_node = vis.pair(act, i)
                        ev["mput"].wait(act, v - 1)
                        ev["nm"].wait(act, v - 1)
                        act.nop(nofuse=True)
                        a.activation(wm[:], aux[0:H, ds(mid_node, P)], ACT.Copy).then_inc(ev["wm_"].sem, 1)
                    if old:
                        i, r, v = old
                        ev["e2_"].wait(act, v)
                        ev["pagg_"].wait(act, v - 2)
                        a.activation(msg[:, q, :, D:DW], e2[:].rearrange("p (t h) -> p t h", h=H), ACT.Exp).then_inc(ev["ex"].sem, 1)
                    if fin:
                        i, r, v = fin
                        ev["pagg_"].wait(act, v)
                        ev["ptr_"].wait(act, v - 1)
                        a.activation(agg[:], pagg[:, 0:D], ACT.Copy)
                        a.activation(pack[:, 64:68], pagg[:, D:DW], ACT.Copy).then_inc(ev["aggden"].sem, 1)
                    if now:
                        i, r, v = now
                        ev["ppT_"].wait(act, v)
                        ev["zmm"].wait(act, v - 2)
                        a.activation(partsT[:, r % 2], ppT[0:3 * GH, :], ACT.Copy).then_inc(ev["partsT_"].sem, 1)

                vis.loop(act, turn, 3)

            @block.vector
            def _(dve):
                v_ = nc.vector
                owns(dve, "rel_ far_ zs_ z_ z2_ attn_ hi_ r1_ mid_ lo_ zred cmax_ mnew dm_ mhi_ mr1_ mmid_ mlo_ ms_ e1_ e2_ "
                          "msg_ num1 num2 den1 den2")
                c = Chain(dve, setup_chain)
                c(v_.memset(pack[:], 0.0))
                c(v_.memset(pack2[:], 0.0))
                for k in range(3):
                    c(v_.tensor_copy(id3[k * GH:(k + 1) * GH, :], identf[k * GH:(k + 1) * GH, k * GH:(k + 1) * GH]))
                c(v_.tensor_copy(pick[:], id3[:].unsqueeze(2).to_broadcast([3 * GH, GH, P])))
                c(v_.tensor_copy(identb[:], identf[:]))
                c(v_.tensor_copy(iotab[:], iotaf[:]))
                c(v_.tensor_copy(ident4[:], identf[:].unsqueeze(1).to_broadcast([P, H, P])))
                dve.sem_inc(setup, 1)
                by_head = lambda ap: ap.rearrange("p (t h) -> p t h", h=H)
                by_part = lambda bank: bank[:, EDGES].rearrange("p (t k h) -> p t h k", t=G, k=3)

                def turn(now, mid, old, _, fin):
                    def highest(t):
                        if mid:
                            i, r, v = mid
                            ev["zmm"].wait(dve, v, t + 1)
                            if t == 0:
                                ev["cmax_"].wait(dve, v - 1)
                            v_.tensor_reduce(tmax[:, :, t], pz[:, t % 3, :].rearrange("p (h e) -> p h e", h=H), AX, ALU.max)\
                                .then_inc(ev["zred"].sem, 1)

                    def fars(t0, t1):
                        if now:
                            i, r, v = now
                            for t in range(t0, t1):
                                ins = v_.tensor_scalar(far[:, r, t, :], iotab[:], rel[:, r % 2, t:t + 1], -BIG, ALU.not_equal, ALU.mult)
                            if t1 == G:
                                ins.then_inc(ev["far_"].sem, 1)

                    if fin:
                        fi, fr, fv = fin
                        _, fin_node = vis.held(dve, fr)
                    if now:
                        i, r, v = now
                        tile, _ = vis.pair(dve, i, r)
                        ev["zmm"].wait(dve, v - R)
                        ev["hot_"].wait(dve, v - R)
                        ev["far_"].wait(dve, v - 1)
                        v_.tensor_scalar(rel[:, r % 2], dstf[:, ds(tile, G)], baseB[:, ds(i, 1)], None, ALU.subtract).then_inc(ev["rel_"].sem, 1)
                    if old:
                        i, r, v = old
                        q = r % 2
                        ev["nm"].wait(dve, v)
                        ev["cmax_"].wait(dve, v)
                        ev["topT_"].wait(dve, v - 1)
                        ev["mg"].wait(dve, v - 1)
                        v_.tensor_tensor(top[:], pm[:, NM], cmax[:, q], ALU.max).then_inc(ev["mnew"].sem, 1)
                    if now:
                        ev["rel_"].wait(dve, now[2])
                    fars(0, 4)
                    if old:
                        ev["mnew"].wait(dve, v)
                        v_.tensor_copy(mparts[:, 0], top[:]).then_inc(ev["mhi_"].sem, 1)
                        ev["sc"].wait(dve, v - 1)
                        v_.tensor_tensor(dm[:], pm[:, NM], top[:], ALU.subtract).then_inc(ev["dm_"].sem, 1)
                    fars(4, 8)
                    if fin:
                        win = ds(fin_node, P)
                        ev["num2"].wait(dve, fv - 1)
                        ev["den2"].wait(dve, fv - 1)
                        ev["ptr_"].wait(dve, fv)
                        v_.tensor_tensor(sums[:, win], sums[:, win], ptr[:, P:2 * P], ALU.mult).then_inc(ev["num1"].sem, 1)
                        v_.tensor_tensor(aux[64:68, win], aux[64:68, win], ptr[64:68, 3 * P:4 * P], ALU.mult).then_inc(ev["den1"].sem, 1)
                        ev["num1"].wait(dve, fv)
                        v_.tensor_tensor(sums[:, win], sums[:, win], ptr[:, 0:P], ALU.add).then_inc(ev["num2"].sem, 1)
                        ev["den1"].wait(dve, fv)
                        v_.tensor_tensor(aux[64:68, win], aux[64:68, win], ptr[64:68, 2 * P:3 * P], ALU.add).then_inc(ev["den2"].sem, 1)
                    if old:
                        ev["mhi_"].wait(dve, v)
                        v_.tensor_tensor(mrest[:], top[:], mparts[:, 0], ALU.subtract).then_inc(ev["mr1_"].sem, 1)
                    highest(0)
                    if old:
                        ev["mr1_"].wait(dve, v)
                        v_.tensor_copy(mparts[:, 1], mrest[:]).then_inc(ev["mmid_"].sem, 1)
                    highest(1)
                    if old:
                        ev["mmid_"].wait(dve, v)
                        v_.tensor_tensor(mparts[:, 2], mrest[:], mparts[:, 1], ALU.subtract).then_inc(ev["mlo_"].sem, 1)
                    highest(2)
                    if old:
                        ev["mg"].wait(dve, v)
                        v_.tensor_reduce(by_head(ms[:]), by_part(pm), AX, ALU.add).then_inc(ev["ms_"].sem, 1)
                    highest(3)
                    if old:
                        ev["ms_"].wait(dve, v)
                        v_.tensor_tensor(e1[:], attn[:, r], ms[:], ALU.subtract).then_inc(ev["e1_"].sem, 1)
                    if now:
                        i1, r1, v1 = now
                        ev["sg"].wait(dve, v1)
                        v_.tensor_reduce(by_head(zs[:]), by_part(pa), AX, ALU.add).then_inc(ev["zs_"].sem, 1)
                    if old:
                        ev["e1_"].wait(dve, v)
                        ev["ex"].wait(dve, v - 1)
                        v_.tensor_single_scalar(e2[:], e1[:], 0.0, ALU.min).then_inc(ev["e2_"].sem, 1)
                    highest(4)
                    if now:
                        wait_landed(dve, landed, r1, v1)
                        ev["zs_"].wait(dve, v1)
                        v_.tensor_tensor(by_head(z[:]), rows[:, r1, :, D:DW], by_head(zs[:]), ALU.add).then_inc(ev["z_"].sem, 1)
                    highest(5)
                    if now:
                        ev["z_"].wait(dve, v1)
                        v_.scalar_tensor_tensor(out=z2[:], in0=z[:], scalar=0.2, in1=z[:], op0=ALU.mult, op1=ALU.max).then_inc(ev["z2_"].sem, 1)
                    highest(6)
                    if now:
                        ev["z2_"].wait(dve, v1)
                        v_.tensor_tensor(attn[:, r1], z2[:], efw[:, ds(tile * H, GH)], ALU.add).then_inc(ev["attn_"].sem, 1)
                    highest(7)
                    if now:
                        ev["attn_"].wait(dve, v1)
                        ev["ppT_"].wait(dve, v1 - 1)
                        v_.tensor_copy(parts[:, 0], attn[:, r1]).then_inc(ev["hi_"].sem, 1)
                    if mid:
                        im, rm, vm = mid
                        ev["zred"].wait(dve, vm)
                        v_.tensor_reduce(cmax[:, rm % 2], tmax[:], AX, ALU.max).then_inc(ev["cmax_"].sem, 1)
                    if now:
                        ev["hi_"].wait(dve, v1)
                        v_.tensor_tensor(rest[:], attn[:, r1], parts[:, 0], ALU.subtract).then_inc(ev["r1_"].sem, 1)
                    def weigh(t0, t1):
                        if old:
                            if t0 == 0:
                                ev["ex"].wait(dve, v)
                            part = slice(t0, t1)
                            ins = v_.tensor_tensor(msg[:, q, part, 0:D].rearrange("p t (h d) -> p t h d", h=H),
                                                   rows[:, r, part, 0:D].rearrange("p t (h d) -> p t h d", h=H),
                                                   msg[:, q, part, D:DW].unsqueeze(3).to_broadcast([P, t1 - t0, H, HD]), ALU.mult)
                            if t1 == G:
                                ins.then_inc(ev["msg_"].sem, 1)
                    weigh(0, 2)
                    if now:
                        ev["r1_"].wait(dve, v1)
                        v_.tensor_copy(parts[:, 1], rest[:]).then_inc(ev["mid_"].sem, 1)
                    weigh(2, 4)
                    if now:
                        ev["mid_"].wait(dve, v1)
                        v_.tensor_tensor(parts[:, 2], rest[:], parts[:, 1], ALU.subtract).then_inc(ev["lo_"].sem, 1)
                    weigh(4, 8)

                vis.loop(dve, turn, 4)



def phase_sum(env, layer, table, weights):
    nc, dstf, srci, identf, iotaf, epsc, meta, pairs, baseB, sums, aux, visit_base, visit_pair = env
    counts = weights is None
    with ExitStack() as ctx:
        sb = lambda n, s, d=F32: ctx.enter_context(nc.sbuf_tensor(f"s{layer}_" + n, s, d))
        sem = phase_semaphores(nc, ctx, f"s{layer}_")
        vis = Visits(env, sem)
        slots = sb("slots", [P, R * G], I32)
        rows = sb("rows", [P, R, G, D])
        rel = sb("rel", [P, 2, G])
        hot = sb("hot", [P, 2, G, P])
        wts = sb("wts", [P, T])
        ones = sb("ones", [P, P])
        pagg = ctx.enter_context(nc.psum_tensor(f"s{layer}_pagg", [P, 2, 2, 512], F32))
        landed = [sem(f"landed{r}") for r in range(R)]
        loaded, cleared = sem("loaded"), sem("cleared")
        ev = {n: Event(sem(n)) for n in ("copied", "rel_", "hot_", "agg", "added", "counted")}

        with nc.Block() as block:
            @block.sync
            def _(sp):
                if not counts:
                    sp.dma_start(wts[:], weights).then_inc(loaded, 16)
                vis.serve(sp, 3)

            @block.gpsimd
            def _(pool):
                gather_rows(vis, pool, table, D, slots, rows, ev["copied"], landed, [ev["agg"]])

            @block.vector
            def _(dve):
                v_ = nc.vector
                for n in ("rel_", "hot_", "added", "counted"):
                    ev[n].start(dve)
                v_.memset(ones[:], 1.0).then_inc(cleared, 1)
                v_.memset(sums[:], 0.0).then_inc(cleared, 1)
                v_.memset(aux[:], 0.0).then_inc(cleared, 1)
                dve.wait_ge(cleared, 3)
                if not counts:
                    dve.wait_ge(loaded, 16)

                def turn(now, last):
                    if now:
                        i, r, v = now
                        tile, node = vis.pair(dve, i)
                        q = r % 2
                        ev["agg"].wait(dve, v - 2)
                        v_.tensor_scalar(rel[:, q], dstf[:, ds(tile, G)], baseB[:, ds(i, 1)], None, ALU.subtract).then_inc(ev["rel_"].sem, 1)
                        ev["rel_"].wait(dve, v)
                        for t in range(G):
                            if counts:
                                ins = v_.tensor_scalar(hot[:, q, t, :], iotaf[:], rel[:, q, t:t + 1], None, ALU.is_equal)
                            else:
                                ins = v_.tensor_scalar(hot[:, q, t, :], iotaf[:], rel[:, q, t:t + 1], wts[:, ds(tile + t, 1)],
                                                       ALU.is_equal, ALU.mult)
                        ins.then_inc(ev["hot_"].sem, 1)
                    if last:
                        i, r, v = last
                        tile, node = vis.pair(dve, i)
                        q = r % 2
                        ev["agg"].wait(dve, v)
                        ev["added"].wait(dve, v - 1)
                        v_.tensor_tensor(sums[:, ds(node, P)], sums[:, ds(node, P)], pagg[:, q, 0, 0:P], ALU.add).then_inc(ev["added"].sem, 1)
                        if counts:
                            ev["counted"].wait(dve, v - 1)
                            v_.tensor_tensor(aux[:, ds(node, P)], aux[:, ds(node, P)], pagg[:, q, 1, 0:P], ALU.add).then_inc(ev["counted"].sem, 1)

                vis.loop(dve, turn, 1)

            @block.tensor
            def _(pe):
                ev["agg"].start(pe)
                pe.wait_ge(cleared, 1)

                def turn(visit):
                    i, r, v = visit
                    q = r % 2
                    wait_landed(pe, landed, r, v)
                    ev["hot_"].wait(pe, v)
                    ev["added"].wait(pe, v - 2)
                    if counts:
                        ev["counted"].wait(pe, v - 2)
                        for t in range(G):
                            pe.matmul(pagg[:, q, 1, 0:P], ones[:], hot[:, q, t, :], start=(t == 0), stop=(t == G - 1))
                    for t in range(G):
                        ins = pe.matmul(pagg[:, q, 0, 0:P], rows[:, r, t, :], hot[:, q, t, :], start=(t == 0), stop=(t == G - 1))
                    ins.then_inc(ev["agg"].sem, 1)

                vis.loop(pe, turn)



def phase_factors(env, sh, shx, CG):
    nc = env[0]
    with ExitStack() as ctx:
        sb = lambda n, s, d=F32: ctx.enter_context(nc.sbuf_tensor(n, s, d))
        sem = phase_semaphores(nc, ctx, "")
        FS = 22
        CT = T // FS
        assert CT * FS == T and FS % 2 == 0
        raw = sb("f_raw", [P, 2, CT, 9])
        fac = sb("f_fac", [P, 2, CT, NSH])
        loaded, stored = ([sem(f"f_{n}{r}") for r in range(2)] for n in ("loaded", "stored"))
        chain = sem("f_chain")
        made = Event(sem("f_made"))
        C011, C110, C121 = CG[1], CG[3], CG[4]
        plan = [(0, [(0, 1.0)])]
        plan += [(1 + k, [(1 + k, float(C011[0, k, k]))]) for k in range(3)]
        plan += [(4 + i, [(1 + i, float(C110[i, i, 0]))]) for i in range(3)]
        for i in range(3):
            for k in range(3):
                plan.append((7 + 3 * i + k, [(4 + j, float(C121[i, j, k])) for j in range(5) if abs(C121[i, j, k]) > 1e-7]))
        LINKS = max(len(terms) for _, terms in plan)

        with nc.Block() as block:
            @block.sync
            def _(sp):
                with sp.Fori(0, FS // 2) as half:
                    i = half * 2
                    for r in range(2):
                        made.wait(sp, i + r)
                        sp.dma_start(shx[:, ds((i + r) * (CT * NSH), CT * NSH)], fac[:, r].rearrange("p t j -> p (t j)"))\
                            .then_inc(stored[r], 16)
                for r in range(2):
                    sp.wait_ge(stored[r], FS // 2 * 16 + 16)

            @block.scalar
            def _(act):
                with act.Fori(0, FS // 2) as half:
                    i = half * 2
                    for r in range(2):
                        made.wait(act, i + r - 2)
                        act.dma_start(raw[:, r].rearrange("p t j -> p (t j)"), sh[:, ds((i + r) * (CT * 9), CT * 9)])\
                            .then_inc(loaded[r], 16)

            @block.vector
            def _(dve):
                made.start(dve)
                for r in range(2):
                    dve.sem_inc(stored[r], 16)
                with dve.Fori(0, FS // 2) as half:
                    i = half * 2
                    for r in range(2):
                        c = Chain(dve, chain, (i + r) * LINKS)
                        dve.wait_ge(loaded[r], i * 8 + 16)
                        dve.wait_ge(stored[r], i * 8 + 16)
                        for n in range(LINKS):
                            for col, terms in plan:
                                if n == 0:
                                    j, f = terms[0]
                                    ins = nc.vector.tensor_scalar(fac[:, r, :, col], raw[:, r, :, j], f, None, ALU.mult)
                                elif n < len(terms):
                                    j, f = terms[n]
                                    ins = nc.vector.scalar_tensor_tensor(out=fac[:, r, :, col], in0=raw[:, r, :, j], scalar=f,
                                                                         in1=fac[:, r, :, col], op0=ALU.mult, op1=ALU.add)
                            c(ins)
                        dve.sem_inc(made.sem, 1)


def phase_tensor_product(env, table, shx, W2b, W2scale):
    nc, dstf, srci, identf, iotaf, epsc, meta, pairs, baseB, sums, aux, visit_base, visit_pair = env
    with ExitStack() as ctx:
        sb = lambda n, s, d=F32: ctx.enter_context(nc.sbuf_tensor("p_" + n, s, d))
        ps = lambda n, s, d=F32: ctx.enter_context(nc.psum_tensor("p_" + n, s, d))
        sem = phase_semaphores(nc, ctx, "p_")
        vis = Visits(env, sem)
        slots = sb("slots", [P, R * G], I32)
        rows = sb("rows", [P, R, G, D])
        rel = sb("rel", [P, 2, G])
        hot = sb("hot", [P, 2, G, P])
        fac = sb("fac", [P, R, G, NSH])
        prod = sb("prod", [P, 2, G, TW])
        t4 = sb("t4", [P, 3, G, 3, 32])
        t3 = sb("t3", [P, 3, G, 32])
        a4 = sb("a4", [P, G, 3, 32])
        a3 = sb("a3", [P, G, 32])
        w2 = sb("w2", [P, 3, D])
        w2s = sb("w2s", [P, 3])
        win = sb("win", [P, 3, P])
        pagg = ps("pagg", [P, 2, 3, 512])
        pmsg = ps("pmsg", [P, 2, 512])
        landed = [sem(f"landed{r}") for r in range(R)]
        facl = [sem(f"facl{r}") for r in range(R)]
        loaded, cleared, wchain = sem("loaded"), sem("cleared"), sem("wchain")
        ev = {n: Event(sem(n)) for n in
              ("copied", "rel_", "hot_", "t4_", "a4_", "a3_", "x1_", "made", "scalars", "agg", "win_", "msg_", "added")}
        BLK = ((0, 128), (128, 128), (256, 96))

        with nc.Block() as block:
            @block.sync
            def _(sp):
                sp.dma_start(w2[:], W2b).then_inc(loaded, 16)
                sp.dma_start(w2s[:], W2scale).then_inc(loaded, 16)
                def turn(visit):
                    i, r, v = visit
                    tile, node = vis.pair(sp, i)
                    ev["made"].wait(sp, v - R)
                    ev["scalars"].wait(sp, v - R)
                    sp.dma_start(fac[:, r].rearrange("p t j -> p (t j)"), shx[:, ds(tile * NSH, G * NSH)]).then_inc(facl[r], 16)

                vis.serve(sp, 4, turn)

            @block.gpsimd
            def _(pool):
                gather_rows(vis, pool, table, D, slots, rows, ev["copied"], landed, [ev["scalars"], ev["x1_"]])

            @block.scalar
            def _(act):
                a = nc.scalar
                for n in ("scalars", "win_"):
                    ev[n].start(act)

                def turn(now, last):
                    if now:
                        i, r, v = now
                        q = r % 2
                        wait_landed(act, landed, r, v)
                        act.wait_ge(facl[r], (v - r) * (16 // R) + 16)
                        ev["agg"].wait(act, v - 2)
                        for t in range(G):
                            a.activation(prod[:, q, t, 0:D], rows[:, r, t, :], ACT.Copy, scale=fac[:, r, t, 0:1])
                        for k in range(3):
                            for t in range(G):
                                ins = a.activation(prod[:, q, t, D + 32 * k:D + 32 * k + 32], rows[:, r, t, 0:32], ACT.Copy,
                                                   scale=fac[:, r, t, 1 + k:2 + k])
                        ins.then_inc(ev["scalars"].sem, 1)
                    if last:
                        i, r, v = last
                        q = r % 2
                        ev["agg"].wait(act, v)
                        ev["msg_"].wait(act, v - 1)
                        for b, (o, w) in enumerate(BLK):
                            ins = a.activation(win[0:w, b, :], pagg[0:w, q, b, 0:P], ACT.Copy)
                        ins.then_inc(ev["win_"].sem, 1)

                vis.loop(act, turn, 1)

            @block.vector
            def _(dve):
                v_ = nc.vector
                for n in ("rel_", "hot_", "t4_", "a4_", "a3_", "x1_", "made", "added"):
                    ev[n].start(dve)
                v_.memset(sums[:], 0.0).then_inc(cleared, 1)
                dve.wait_ge(loaded, 32)
                c = Chain(dve, wchain)
                for b in range(3):
                    c(v_.tensor_scalar(w2[:, b, :], w2[:, b, :], w2s[:, b:b + 1], None, ALU.mult))
                dve.sem_inc(cleared, 1)
                dve.wait_ge(cleared, 2)

                def turn(now, _, old):
                    if now:
                        i, r, v = now
                        tile, node = vis.pair(dve, i)
                        q = r % 2
                        ev["agg"].wait(dve, v - 2)
                        v_.tensor_scalar(rel[:, q], dstf[:, ds(tile, G)], baseB[:, ds(i, 1)], None, ALU.subtract).then_inc(ev["rel_"].sem, 1)
                        wait_landed(dve, landed, r, v)
                        dve.wait_ge(facl[r], (v - r) * (16 // R) + 16)
                        ev["made"].wait(dve, v - 1)
                        x1 = rows[:, r, :, 32:D].rearrange("p t (u i) -> p t i u", i=3)
                        for i1 in range(3):
                            ins = v_.tensor_tensor(t4[:, i1], x1[:, :, i1, :].unsqueeze(2).to_broadcast([P, G, 3, 32]),
                                             fac[:, r, :, 7 + 3 * i1:10 + 3 * i1].unsqueeze(3).to_broadcast([P, G, 3, 32]), ALU.mult)
                        ins.then_inc(ev["t4_"].sem, 1)
                        for i1 in range(3):
                            ins = v_.tensor_tensor(t3[:, i1], x1[:, :, i1, :],
                                             fac[:, r, :, 4 + i1].unsqueeze(2).to_broadcast([P, G, 32]), ALU.mult)
                        ins.then_inc(ev["x1_"].sem, 1)
                        ev["t4_"].wait(dve, v)
                        v_.tensor_tensor(a4[:], t4[:, 0], t4[:, 1], ALU.add).then_inc(ev["a4_"].sem, 1)
                        ev["x1_"].wait(dve, v)
                        v_.tensor_tensor(a3[:], t3[:, 0], t3[:, 1], ALU.add).then_inc(ev["a3_"].sem, 1)
                        ev["rel_"].wait(dve, v)
                        for t in range(G):
                            ins = v_.tensor_scalar(hot[:, q, t, :], iotaf[:], rel[:, q, t:t + 1], None, ALU.is_equal)
                        ins.then_inc(ev["hot_"].sem, 1)
                        ev["a4_"].wait(dve, v)
                        v_.tensor_tensor(prod[:, q, :, 256:352].rearrange("p t (k u) -> p t k u", k=3), a4[:], t4[:, 2], ALU.add)
                        ev["a3_"].wait(dve, v)
                        v_.tensor_tensor(prod[:, q, :, 224:256], a3[:], t3[:, 2], ALU.add).then_inc(ev["made"].sem, 1)
                    if old:
                        i, r, v = old
                        tile, node = vis.pair(dve, i)
                        ev["msg_"].wait(dve, v)
                        ev["added"].wait(dve, v - 1)
                        v_.tensor_tensor(sums[:, ds(node, P)], sums[:, ds(node, P)], pmsg[:, r % 2, 0:P], ALU.add).then_inc(ev["added"].sem, 1)

                vis.loop(dve, turn, 2)

            @block.tensor
            def _(pe):
                for n in ("agg", "msg_"):
                    ev[n].start(pe)
                pe.wait_ge(cleared, 2)

                def turn(now, last):
                    if now:
                        i, r, v = now
                        q = r % 2
                        ev["hot_"].wait(pe, v)
                        ev["made"].wait(pe, v)
                        ev["scalars"].wait(pe, v)
                        ev["win_"].wait(pe, v - 2)
                        for b, (o, w) in enumerate(BLK):
                            for t in range(G):
                                ins = pe.matmul(pagg[0:w, q, b, 0:P], prod[:, q, t, o:o + w], hot[:, q, t, :],
                                                start=(t == 0), stop=(t == G - 1))
                        ins.then_inc(ev["agg"].sem, 1)
                    if last:
                        i, r, v = last
                        q = r % 2
                        ev["win_"].wait(pe, v)
                        ev["added"].wait(pe, v - 2)
                        for b, (o, w) in enumerate(BLK):
                            ins = pe.matmul(pmsg[:, q, 0:P], w2[0:w, b, :], win[0:w, b, :], start=(b == 0), stop=(b == 2))
                        ins.then_inc(ev["msg_"].sem, 1)

                vis.loop(pe, turn, 1)



def phase_node(env, layer, xold, xnew, table, params):
    nc, dstf, srci, identf, iotaf, epsc, meta, pairs, baseB, sums, aux, visit_base, visit_pair = env
    with ExitStack() as ctx:
        sb = lambda n, s, d=F32: ctx.enter_context(nc.sbuf_tensor(f"n{layer}_" + n, s, d))
        ps = lambda n, s, d=F32: ctx.enter_context(nc.psum_tensor(f"n{layer}_" + n, s, d))
        sem = phase_semaphores(nc, ctx, f"n{layer}_")
        xin = sb("xin", [P, 2, BATCH, D])
        xout = sb("xout", [P, 2, BATCH, D])
        hout = sb("hout", [P, 2, BATCH, D])
        xc = sb("xc", [P, BATCH, D])
        sq = sb("sq", [P, BATCH, D])
        s = sb("s", [P, 40])
        fm = sb("fm", [P, BC])
        gm = sb("gm", [P, BC])
        row = sb("row", [P, 2, D])
        w = sb("w", [P, D])
        sel = sb("sel", [68, P])
        pden = ps("pden", [P, 2, 512])
        pT = ps("pT", [P, 1024])
        xl = [sem("xl0"), sem("xl1")]
        stored = [sem("stored0"), sem("stored1")]
        loaded, setup, chain, xchain = sem("loaded"), sem("setup"), sem("chain"), sem("xchain")
        ev = {n: Event(sem(n)) for n in ("fm_", "gelu_", "nodes", "pre", "act_", "den", "xnew_", "hnew", "kept")}
        for n in ("centred", "squared", "varied", "rooted"):
            ev[n] = Event(sem(n), 2 if layer == 0 else 1)

        with nc.Block() as block:
            @block.sync
            def _(sp):
                n = 0
                if layer == 0:
                    sp.dma_start(row[:, 0, :], params["scale"].to_broadcast([P, D])).then_inc(loaded, 16)
                    sp.dma_start(row[:, 1, :], params["bias"].to_broadcast([P, D])).then_inc(loaded, 16)
                if layer == 1:
                    sp.dma_start(row[:, 0, :], params["b"].to_broadcast([P, D])).then_inc(loaded, 16)
                    sp.dma_start(w[:], params["W"]).then_inc(loaded, 16)
                ev["kept"].start(sp)
                with sp.Fori(0, STEPS // 2) as half:
                    i = half * 2
                    for r in range(2):
                        ev["hnew"].wait(sp, i + r)
                        sp.dma_start(blocks_of(xnew, i + r), xout[:, r]).then_inc(stored[r], 16)
                        sp.dma_start(blocks_of(table, i + r), hout[:, r]).then_inc(stored[r], 16)
                        sp.wait_ge(stored[r], i * 16 + 32)
                        sp.sem_inc(ev["kept"].sem, 1)

            @block.gpsimd
            def _(pool):
                load_blocks(nc, pool, ((xold, xin, xl),), ev["xnew_"])

            @block.tensor
            def _(pe):
                for n in ("nodes", "den"):
                    ev[n].start(pe)
                pe.wait_ge(setup, 1)
                with pe.Fori(0, STEPS) as it:
                    if layer == 0:
                        ev["fm_"].wait(pe, it - 1)
                        for q in range(2):
                            ins = pe.matmul(pden[:, q, 0:HC], sel[:], aux[0:68, ds(it * BC + q * HC, HC)], start=True, stop=True)
                        ins.then_inc(ev["den"].sem, 1)
                    ev["gelu_"].wait(pe, it)
                    ev["xnew_"].wait(pe, it - 1)
                    ev["pre"].wait(pe, it - 1)
                    for b in range(BATCH):
                        c = slice(b * P, (b + 1) * P)
                        if layer == 1:
                            ins = pe.matmul(pT[:, c], gm[:, c], w[:], start=True, stop=True)
                        else:
                            ins = pe.transpose(pT[:, c], gm[:, c], identf[:])
                    ins.then_inc(ev["nodes"].sem, 1)

            @block.scalar
            def _(act):
                a = nc.scalar
                for n in ("squared", "rooted", "gelu_", "act_"):
                    ev[n].start(act)
                act.wait_ge(setup, 1)
                with act.Fori(0, STEPS) as it:
                    ev["nodes"].wait(act, it - 1)
                    act.nop(nofuse=True)
                    if layer == 0:
                        ev["fm_"].wait(act, it)
                        a.activation(gm[:], fm[:], ACT.Gelu).then_inc(ev["gelu_"].sem, 1)
                        norm_scalar(nc, act, ev, it, 1, xc[:], sq[:], s, epsc)
                    elif layer == 1:
                        a.activation(gm[:], sums[:, ds(it * BC, BC)], ACT.Gelu_apprx_tanh).then_inc(ev["gelu_"].sem, 1)
                        ev["pre"].wait(act, it)
                        a.activation(sq[:], xc[:], ACT.Gelu_apprx_tanh).then_inc(ev["act_"].sem, 1)
                    else:
                        a.activation(gm[:], sums[:, ds(it * BC, BC)], ACT.Copy).then_inc(ev["gelu_"].sem, 1)
                    norm_scalar(nc, act, ev, it, 2 if layer == 0 else 1, xc[:], sq[:], s, epsc)

            @block.vector
            def _(dve):
                v = nc.vector
                for n in ("centred", "varied", "fm_", "pre", "xnew_", "hnew"):
                    ev[n].start(dve)
                if layer < 2:
                    dve.wait_ge(loaded, 32)
                if layer == 0:
                    c = Chain(dve, xchain)
                    c(v.memset(sel[:], 0.0))
                    for h in range(H):
                        c(v.tensor_copy(sel[64:68, h * HD:(h + 1) * HD],
                                        identf[64:68, 64 + h:65 + h].to_broadcast([H, HD])))
                dve.sem_inc(setup, 1)
                links = {0: 12, 1: 4, 2: 4}[layer]
                with dve.Fori(0, STEPS // 2) as half:
                    i = half * 2
                    for r in range(2):
                        it = i + r
                        c = Chain(dve, chain, it * links)
                        node_rows = pT[:, 0:BC].rearrange("p (b f) -> p b f", f=D)
                        wide = lambda k: row[:, k, :].unsqueeze(1).to_broadcast([P, BATCH, D])
                        if layer == 0:
                            ev["den"].wait(dve, it)
                            ev["gelu_"].wait(dve, it - 1)
                            c(v.tensor_scalar(fm[:].rearrange("p (q n) -> p q n", q=2), pden[:, :, 0:HC], 1e-9, None, ALU.add))
                            c(v.reciprocal(fm[:], fm[:]))
                            v.tensor_tensor(fm[:], fm[:], sums[:, ds(it * BC, BC)], ALU.mult).then_inc(ev["fm_"].sem, 1)
                        ev["nodes"].wait(dve, it)
                        ev["hnew"].wait(dve, it - 1)
                        dve.wait_ge(xl[r], i * 8 + 16)
                        ev["kept"].wait(dve, it - 2)
                        if layer == 0:
                            norm_vector(nc, dve, c, ev, it, 1, node_rows, xc[:], sq[:], s)
                            dve.sem_inc(ev["pre"].sem, 1)
                            c(v.tensor_tensor(xc[:], xc[:], wide(0), ALU.mult))
                            c(v.tensor_tensor(xc[:], xc[:], wide(1), ALU.add))
                            new = xc[:]
                        elif layer == 1:
                            v.tensor_tensor(xc[:], node_rows, wide(0), ALU.add).then_inc(ev["pre"].sem, 1)
                            ev["act_"].wait(dve, it)
                            new = sq[:]
                        else:
                            dve.sem_inc(ev["pre"].sem, 1)
                            new = node_rows
                        v.tensor_tensor(xout[:, r], xin[:, r], new, ALU.add).then_inc(ev["xnew_"].sem, 1)
                        ev["xnew_"].wait(dve, it)
                        norm_vector(nc, dve, c, ev, it, 2 if layer == 0 else 1, xout[:, r], xc[:], sq[:], s)
                        v.tensor_single_scalar(hout[:, r], xc[:], 0.0, ALU.max).then_inc(ev["hnew"].sem, 1)
                        assert c.n == links, c.n



def phase_last(env, x3, table, WlT, WrT, bl, gamma, beta, out):
    nc, dstf, srci, identf, iotaf, epsc, meta, pairs, baseB, sums, aux, visit_base, visit_pair = env
    with ExitStack() as ctx:
        sb = lambda n, s, d=F32: ctx.enter_context(nc.sbuf_tensor("l_" + n, s, d))
        ps = lambda n, s, d=F32: ctx.enter_context(nc.psum_tensor("l_" + n, s, d))
        sem = phase_semaphores(nc, ctx, "l_")
        hin = sb("hin", [P, 2, BATCH, D])
        xin = sb("xin", [P, 2, BATCH, D])
        xout = sb("xout", [P, 2, BATCH, D])
        hT = sb("hT", [P, BC])
        mean = sb("mean", [P, BC])
        wl, wr = sb("wl", [P, D]), sb("wr", [P, D])
        par = sb("par", [P, 3, D])
        ones = sb("ones", [P, P])
        stat = sb("stat", [P, 8, D])
        tot = sb("tot", [P, BATCH, D])
        pT = ps("pT", [P, 1024])
        py = ps("py", [P, 1024])
        pst = ps("pst", [P, 512])
        hl = [sem("hl0"), sem("hl1")]
        xl = [sem("xl0"), sem("xl1")]
        stored = [sem("stored0"), sem("stored1")]
        loaded, setup, chain, schain, stm, ychain, roots = (
            sem(n) for n in ("loaded", "setup", "chain", "schain", "stm", "ychain", "roots"))
        ev = {n: Event(sem(n)) for n in ("mean_", "turned", "hT_", "y_", "kept", "done", "saved")}
        y = sums[:, 0:NP].rearrange("p (b f) -> p b f", f=D)
        LAST = N - (NB - 1) * P

        with nc.Block() as block:
            @block.sync
            def _(sp):
                for t, src in ((wl[:], WlT), (wr[:], WrT), (par[:, 0, :], bl.to_broadcast([P, D])),
                               (par[:, 1, :], gamma.to_broadcast([P, D])), (par[:, 2, :], beta.to_broadcast([P, D]))):
                    sp.dma_start(t, src).then_inc(loaded, 16)
                ev["saved"].start(sp)
                with sp.Fori(0, STEPS // 2) as half:
                    i = half * 2
                    for r in range(2):
                        ev["done"].wait(sp, i + r)
                        sp.dma_start(blocks_of(out, i + r), xout[:, r]).then_inc(stored[r], 16)
                        sp.wait_ge(stored[r], i * 8 + 16)
                        sp.sem_inc(ev["saved"].sem, 1)

            @block.gpsimd
            def _(pool):
                load_blocks(nc, pool, ((table, hin, hl),), ev["turned"])
                load_blocks(nc, pool, ((x3, xin, xl),), ev["done"])

            @block.tensor
            def _(pe):
                for n in ("turned", "y_"):
                    ev[n].start(pe)
                pe.wait_ge(loaded, 80)
                with pe.Fori(0, STEPS // 2) as half:
                    i = half * 2
                    for r in range(2):
                        it = i + r
                        pe.wait_ge(hl[r], i * 8 + 16)
                        ev["hT_"].wait(pe, it - 1)
                        for b in range(BATCH):
                            ins = pe.transpose(pT[:, b * P:(b + 1) * P], hin[:, r, b, :], identf[:])
                        ins.then_inc(ev["turned"].sem, 1)
                        ev["hT_"].wait(pe, it)
                        ev["mean_"].wait(pe, it)
                        ev["kept"].wait(pe, it - 1)
                        for b in range(BATCH):
                            c = slice(b * P, (b + 1) * P)
                            pe.matmul(py[:, c], mean[:, c], wl[:], start=True, stop=False)
                            ins = pe.matmul(py[:, c], hT[:, c], wr[:], start=False, stop=True)
                        ins.then_inc(ev["y_"].sem, 1)
                for n in range(2):
                    pe.wait_ge(stm, n + 1)
                    pe.matmul(pst[:, n * D:(n + 1) * D], ones[:], stat[:, 2 * n, :], start=True, stop=False)
                    pe.matmul(pst[:, n * D:(n + 1) * D], ones[0:LAST, :], stat[0:LAST, 2 * n + 1, :], start=False, stop=True).then_inc(setup, 1)

            @block.scalar
            def _(act):
                a = nc.scalar
                ev["hT_"].start(act)
                with act.Fori(0, STEPS) as it:
                    ev["turned"].wait(act, it)
                    ev["y_"].wait(act, it - 1)
                    a.activation(hT[:], pT[:, 0:BC], ACT.Copy).then_inc(ev["hT_"].sem, 1)
                act.wait_ge(roots, 1)
                a.activation(stat[:, 5, :], stat[:, 4, :], ACT.Sqrt, bias=epsc[:], scale=1.0 / N).then_inc(roots, 1)

            @block.vector
            def _(dve):
                v = nc.vector
                for n in ("mean_", "kept", "done"):
                    ev[n].start(dve)
                c = Chain(dve, schain)
                c(v.memset(ones[:], 1.0))
                dve.wait_ge(loaded, 80)
                with dve.Fori(0, STEPS) as it:
                    cc = Chain(dve, chain, it * 3)
                    cols = ds(it * BC, BC)
                    ev["y_"].wait(dve, it - 1)
                    cc(v.tensor_scalar(mean[:], aux[:, cols], 1.0, None, ALU.max))
                    cc(v.reciprocal(mean[:], mean[:]))
                    v.tensor_tensor(mean[:], mean[:], sums[:, cols], ALU.mult).then_inc(ev["mean_"].sem, 1)
                    ev["mean_"].wait(dve, it)
                    ev["y_"].wait(dve, it)
                    cc(v.tensor_tensor(sums[:, cols].rearrange("p (b f) -> p b f", f=D), py[:, 0:BC].rearrange("p (b f) -> p b f", f=D),
                                    par[:, 0, :].unsqueeze(1).to_broadcast([P, BATCH, D]), ALU.add))
                    dve.sem_inc(ev["kept"].sem, 1)
                by_feature = y[:, 0:NB - 1, :].rearrange("p b f -> p f b")
                c(v.tensor_reduce(stat[:, 0, :], by_feature, AX, ALU.add))
                c(v.tensor_copy(stat[:, 1, :], y[:, NB - 1, :]))
                dve.sem_inc(stm, 1)
                dve.wait_ge(setup, 1)
                c(v.tensor_scalar(stat[:, 6, :], pst[:, 0:D], -1.0 / N, None, ALU.mult))
                c(v.tensor_tensor(y, y, stat[:, 6, :].unsqueeze(1).to_broadcast([P, NB, D]), ALU.add))
                sqv = aux[:, 0:NP].rearrange("p (b f) -> p b f", f=D)
                c(v.tensor_tensor(sqv, y, y, ALU.mult))
                c(v.tensor_reduce(stat[:, 2, :], sqv[:, 0:NB - 1, :].rearrange("p b f -> p f b"), AX, ALU.add))
                c(v.tensor_copy(stat[:, 3, :], sqv[:, NB - 1, :]))
                dve.sem_inc(stm, 1)
                dve.wait_ge(setup, 2)
                c(v.tensor_copy(stat[:, 4, :], pst[:, D:2 * D]))
                dve.sem_inc(roots, 1)
                dve.wait_ge(roots, 2)
                c(v.reciprocal(stat[:, 7, :], stat[:, 5, :]))
                c(v.tensor_tensor(stat[:, 7, :], stat[:, 7, :], par[:, 1, :], ALU.mult))
                with dve.Fori(0, STEPS // 2) as half:
                    i = half * 2
                    for r in range(2):
                        it = i + r
                        cc = Chain(dve, ychain, it * 2)
                        dve.wait_ge(xl[r], i * 8 + 16)
                        ev["saved"].wait(dve, it - 2)
                        ev["done"].wait(dve, it - 1)
                        ys = sums[:, ds(it * BC, BC)].rearrange("p (b f) -> p b f", f=D)
                        cc(v.tensor_tensor(tot[:], ys, stat[:, 7, :].unsqueeze(1).to_broadcast([P, BATCH, D]), ALU.mult))
                        cc(v.tensor_tensor(tot[:], tot[:], par[:, 2, :].unsqueeze(1).to_broadcast([P, BATCH, D]), ALU.add))
                        v.tensor_tensor(xout[:, r], tot[:], xin[:, r], ALU.add).then_inc(ev["done"].sem, 1)



def kernel(x, src, dst, edge_attr_16, edge_attr_9, edge_weight, edge_weight1, L0_gnn_W, L0_gnn_W_e, L0_gnn_a,
           L0_gnn_ln_scale, L0_gnn_ln_bias, L1_gnn_W, L1_gnn_b, L2_gnn_weights, L3_gnn_W_l, L3_gnn_b_l,
           L3_gnn_W_r, L3_gnn_gamma, L3_gnn_beta):
    import concourse.bacc as bacc
    from concourse.bass_utils import run_bass_kernel_spmd

    def by_tile(a, fill=0):
        a = np.asarray(a)
        full = np.full((T * P,) + a.shape[1:], fill, a.dtype)
        full[:E] = a
        return np.ascontiguousarray(np.swapaxes(full.reshape((T, P) + a.shape[1:]), 0, 1))

    xp = np.zeros((NP, D), np.float32)
    xp[:N] = np.asarray(x)
    ef = np.zeros((STEPS * EC * G * P, 16), np.float32)
    ef[:E] = np.asarray(edge_attr_16)
    ef = np.ascontiguousarray(ef.reshape(STEPS * EC, G, P, 16).transpose(1, 3, 0, 2)).reshape(P, STEPS * EC, P)
    CG = clebsch_gordan()
    W2 = np.asarray(L2_gnn_weights)
    a0, a1 = 1.0 / math.sqrt(2 * 32), 1.0 / math.sqrt(3 * 32)
    w2b = np.zeros((3, P, D), np.float32)
    scale = np.ones((3, P), np.float32)
    w2b[0, 0:32, 0:32] = W2[0]
    scale[0, 0:32] = a0 * float(CG[0][0, 0, 0])
    for k in range(3):
        w2b[0, 32 + k:P:3, 32 + k:P:3] = W2[2]
        scale[0, 32 + k:P:3] = a1 * float(CG[2][k, 0, k])
        w2b[1, 32 * k:32 * k + 32, 32 + k:P:3] = W2[1]
        w2b[2, 32 * k:32 * k + 32, 32 + k:P:3] = W2[4]
    scale[1, 0:96] = a1
    w2b[1, 96:128, 0:32] = W2[3]
    scale[1, 96:128] = a0
    scale[2, 0:96] = a1
    flat = lambda a: np.ascontiguousarray(np.asarray(a))
    arrays = dict(
        x=xp, src=by_tile(src), dst=by_tile(dst, -1), w1e=by_tile(np.asarray(edge_weight1)[:, 0]),
        sh=by_tile(edge_attr_9).reshape(P, T * 9), ef=ef, W0=flat(L0_gnn_W), W0T=flat(np.asarray(L0_gnn_W).T),
        WeT=flat(np.asarray(L0_gnn_W_e).T), aT=flat(np.asarray(L0_gnn_a).T),
        ln_scale=flat(L0_gnn_ln_scale)[None], ln_bias=flat(L0_gnn_ln_bias)[None],
        W1T=flat(np.asarray(L1_gnn_W).T), b1=flat(L1_gnn_b)[None], W2b=flat(w2b.transpose(1, 0, 2)),
        W2scale=flat(scale.T), WlT=flat(np.asarray(L3_gnn_W_l).T), bl=flat(L3_gnn_b_l)[None],
        WrT=flat(np.asarray(L3_gnn_W_r).T), gamma=flat(L3_gnn_gamma)[None], beta=flat(L3_gnn_beta)[None],
        ident=np.eye(P, dtype=np.float32), iota=np.tile(np.arange(PG, dtype=np.float32), (P, 1)),
    )
    nc = bacc.Bacc("TRN2", target_bir_lowering=False, num_devices=1)
    given = {k: nc.dram_tensor("in_" + k, a.shape, mybir.dt.from_np(a.dtype), kind="ExternalInput").ap()
             for k, a in arrays.items()}
    out = nc.dram_tensor("out_x", [NP, D], F32, kind="ExternalOutput").ap()
    build(nc, out=out, **given)
    r = run_bass_kernel_spmd(nc, [{"in_" + k: a for k, a in arrays.items()}], core_ids=[0])
    return r.results[0]["out_x"][:N]
```

```python
import math
from contextlib import ExitStack

import numpy as np
import concourse.bass as bass
from concourse import mybir

ALU = mybir.AluOpType
ACT = mybir.ActivationFunctionType
AX = mybir.AxisListType.X
F32 = mybir.dt.float32
BF16 = mybir.dt.bfloat16
I32 = mybir.dt.int32
ds = bass.ds

P = 128
N = 12500
E = 212500
D = 128
H = 4
HD = D // H
G = 8
NCH = -(-E // (P * G))
T = (NCH + 1) * G
NB = -(-N // P)
NP = NB * P
NW = NP + P
BATCH = 7
STEPS = NB // BATCH
BC = BATCH * P
EC = -(-T // (G * STEPS))
FT = -(-T // STEPS)
HC = BC // 2
PG = 512
R = 4
PAGES = -(-NCH * NB // PG)
DW = D + H
BIG = float(2.0 ** 100)
FAR = float(1 << 20)
EPS = 1e-5
NSH = 16
PAGE_LINKS = 11
TW = 352
assert NB % BATCH == 0 and NCH < 2 * P and G * P * NCH >= E


def clebsch_gordan():
    def fact(n):
        return math.factorial(int(round(n)))

    def su2(j1, j2, j3):
        c3 = np.zeros((2 * j1 + 1, 2 * j2 + 1, 2 * j3 + 1))
        for m1 in range(-j1, j1 + 1):
            for m2 in range(-j2, j2 + 1):
                m3 = m1 + m2
                if abs(m3) > j3:
                    continue
                vmin = int(max(-j1 + j2 + m3, -j1 + m1, 0))
                vmax = int(min(j2 + j3 + m1, j3 - j1 + j2, j3 + m3))
                c = math.sqrt((2 * j3 + 1) * fact(j3 + j1 - j2) * fact(j3 - j1 + j2) * fact(j1 + j2 - j3)
                              / fact(j1 + j2 + j3 + 1))
                c *= math.sqrt(fact(j3 + m3) * fact(j3 - m3) * fact(j1 - m1) * fact(j1 + m1)
                               * fact(j2 - m2) * fact(j2 + m2))
                s = 0.0
                for v in range(vmin, vmax + 1):
                    s += (-1.0) ** (v + j2 + m2) * fact(j2 + j3 + m1 - v) * fact(j1 - m1 + v) / (
                        fact(v) * fact(j3 - j1 + j2 - v) * fact(j3 + m3 - v) * fact(v + j1 - j2 - m3))
                c3[j1 + m1, j2 + m2, j3 + m3] = c * s
        return c3

    def basis(l):
        q = np.zeros((2 * l + 1, 2 * l + 1), dtype=np.complex128)
        for m in range(-l, 0):
            q[l + m, l + abs(m)] = 1.0 / np.sqrt(2.0)
            q[l + m, l - abs(m)] = -1j / np.sqrt(2.0)
        q[l, l] = 1.0
        for m in range(1, l + 1):
            q[l + m, l + abs(m)] = (-1.0) ** m / np.sqrt(2.0)
            q[l + m, l - abs(m)] = 1j * (-1.0) ** m / np.sqrt(2.0)
        return (-1j) ** l * q

    out = []
    for l1, l2, l3 in [(0, 0, 0), (0, 1, 1), (1, 0, 1), (1, 1, 0), (1, 2, 1)]:
        c = np.einsum("ij,kl,mn,ikn->jlm", basis(l1), basis(l2), np.conj(basis(l3).T), su2(l1, l2, l3))
        c = np.real(c)
        out.append((c / np.linalg.norm(c)).astype(np.float32))
    return out


class Event:

    def __init__(self, sem, per=1):
        self.sem, self.per, self.credit = sem, per, R * per

    def start(self, eng):
        eng.sem_inc(self.sem, self.credit)

    def wait(self, eng, v, k=None):
        eng.wait_ge(self.sem, v * self.per + (self.credit + (self.per if k is None else k)))


class Chain:

    def __init__(self, eng, sem, base=0):
        self.eng, self.sem, self.base, self.n = eng, sem, base, 0

    def __call__(self, ins):
        self.n += 1
        ins.then_inc(self.sem, 1)
        self.eng.wait_ge(self.sem, self.base + self.n)


def phase_semaphores(nc, ctx, prefix):
    made = []

    def give_back():
        nc.clear_and_free_semaphores(made)
        nc.all_engine_barrier()

    ctx.callback(give_back)

    def sem(name):
        made.append(nc.alloc_semaphore(prefix + name))
        return made[-1]

    return sem


def build(nc, x, src, dst, w1e, sh, ef, W0, W0T, WeT, aT, ln_scale, ln_bias, W1T, b1, W2b, W2scale,
          WlT, bl, WrT, gamma, beta, ident, iota, out):
    CG = clebsch_gordan()
    outer = ExitStack()

    def dram(name, shape, dt=F32):
        return nc.dram_tensor(name, shape, dt).ap()

    table0 = dram("table0", [NP, DW])
    table1 = dram("table1", [NP, D])
    table2 = dram("table2", [NP, D])
    table3 = dram("table3", [NP, D])
    x1 = dram("x1", [NP, D])
    x2 = dram("x2", [NP, D])
    x3 = dram("x3", [NP, D])
    shx = dram("shx", [P, STEPS * FT * NSH])
    visit_base = dram("visit_base", [PAGES, PG])
    visit_pair = dram("visit_pair", [PAGES, 2 * PG], I32)

    with outer:
        def psb(name, shape, dt=F32):
            return outer.enter_context(nc.sbuf_tensor(name, shape, dt))

        sums = psb("sums", [P, NW])
        aux = psb("aux", [P, NW])
        dstf = psb("dstf", [P, T])
        srci = psb("srci", [P, T], I32)
        identf = psb("identf", [P, P])
        iotaf = psb("iotaf", [P, P])
        epsc = psb("epsc", [P, 1])
        meta = psb("meta", [1, 64], I32)
        pairs = psb("pairs", [1, 2 * PG], I32)
        baseB = psb("baseB", [P, PG])

        phase_visits(nc, dst, src, ident, iota, dstf, srci, identf, iotaf, epsc, meta, sums, aux,
                     visit_base, visit_pair)
        env = (nc, dstf, srci, identf, iotaf, epsc, meta, pairs, baseB, sums, aux, visit_base, visit_pair)
        with nc.sbuf_tensor("efw", [P, STEPS * EC * G * H], F32) as efw:
            phase_first_table(env, x, W0, W0T, aT, WeT, ef, efw, table0, sh, shx, CG)
            phase_attention(env, efw, table0)
        phase_node(env, 0, x, x1, table1, dict(scale=ln_scale, bias=ln_bias))
        phase_sum(env, 1, table1, w1e)
        phase_node(env, 1, x1, x2, table2, dict(W=W1T, b=b1))
        phase_tensor_product(env, table2, shx, W2b, W2scale)
        phase_node(env, 2, x2, x3, table3, {})
        phase_sum(env, 3, table3, None)
        phase_last(env, x3, table3, WlT, WrT, bl, gamma, beta, out)



def phase_visits(nc, dst, src, ident, iota, dstf, srci, identf, iotaf, epsc, meta, sums, aux,
                 visit_base, visit_pair):
    with ExitStack() as ctx:
        sb = lambda n, s, d=F32: ctx.enter_context(nc.sbuf_tensor(n, s, d))
        ps = lambda n, s, d=F32: ctx.enter_context(nc.psum_tensor(n, s, d))
        sem = phase_semaphores(nc, ctx, "")
        CP = 2 * P
        dsti = sb("v_dsti", [P, T], I32)
        dpos = sb("v_dpos", [P, T])
        hi = sb("v_hi", [P, CP])
        lo = sb("v_lo", [P, CP])
        k0 = sb("v_k0", [P, PG])
        kcur = sb("v_kcur", [P, PG])
        ind = sb("v_ind", [P, 2, PG])
        tmp = sb("v_tmp", [P, PG])
        ones = sb("v_ones", [P, P])
        tri = sb("v_tri", [P, P])
        st = sb("v_st", [P, 32])
        sti = sb("v_sti", [P, 2], I32)
        ki = sb("v_ki", [1, 1], I32)
        kf = sb("v_kf", [1, 128])
        vb = sb("v_vb", [P, 4, P])
        baserow = sb("v_baserow", [P, PG])
        tilerow = sb("v_tilerow", [P, PG])
        pairrow = sb("v_pairrow", [1, PG, 2], I32)
        pt = ps("v_pt", [P, 4, P])
        pc = ps("v_pc", [P, 512])
        pbase = ps("v_pbase", [P, PG])
        ptile = ps("v_ptile", [P, PG])
        loaded, chain, red, turned, mm, mmd, pgd, pgm, stored, metac = (
            sem(n) for n in ("v_loaded", "v_chain", "v_red", "v_turned", "v_mm", "v_mmd", "v_pgd", "v_pgm",
                             "v_stored", "v_metac"))
        page_stored, chain2 = sem("v_page_stored"), sem("v_chain2")
        HI, LO, CNT, IDX, CUM, END, VAL, PRE = (slice(2 * i, 2 * i + 2) for i in range(8))

        with nc.Block() as block:
            @block.sync
            def _(sp):
                sp.dma_start(dsti[:], dst).then_inc(loaded, 16)
                sp.dma_start(srci[:], src).then_inc(loaded, 16)
                sp.dma_start(identf[:], ident).then_inc(loaded, 16)
                sp.dma_start(iotaf[:], iota[:, 0:P]).then_inc(loaded, 16)
                sp.dma_start(k0[:], iota).then_inc(loaded, 16)
                sp.wait_ge(metac, 1)
                npages = sp.value_load(meta[0:1, 0:1], min_val=1, max_val=PAGES)
                with sp.Fori(0, npages) as pg:
                    sp.wait_ge(pgd, pg + 1)
                    sp.dma_start(visit_base[ds(pg, 1), :], baserow[0:1, :]).then_inc(stored, 16)
                    sp.dma_start(visit_pair[ds(pg, 1), :], pairrow[:].rearrange("o k c -> o (k c)")).then_inc(stored, 16)
                    sp.wait_ge(stored, pg * 32 + 32)
                    sp.sem_inc(page_stored, 1)

            @block.tensor
            def _(pe):
                pe.wait_ge(red, 1)
                pe.wait_ge(loaded, 80)
                for j in range(2):
                    pe.transpose(pt[:, j, :], hi[:, j * P:(j + 1) * P], identf[:])
                    ins = pe.transpose(pt[:, 2 + j, :], lo[:, j * P:(j + 1) * P], identf[:])
                ins.then_inc(turned, 1)
                pe.wait_ge(mm, 1)
                pe.matmul(pc[:, 0:2], tri[:], st[:, CNT], start=True, stop=False)
                pe.matmul(pc[:, 0:2], ones[:], st[:, PRE], start=False, stop=True).then_inc(mmd, 1)
                pe.wait_ge(mm, 2)
                pe.matmul(pc[:, 2:3], ones[:], st[:, 18:19], start=True, stop=True).then_inc(mmd, 1)
                pe.wait_ge(metac, 1)
                npages = pe.value_load(meta[0:1, 0:1], min_val=1, max_val=PAGES)
                with pe.Fori(0, npages) as pg:
                    pe.wait_ge(pgm, pg + 1)
                    for q in range(PG // 512):
                        c = slice(512 * q, 512 * q + 512)
                        for j in range(2):
                            pe.matmul(pbase[:, c], vb[:, j, :], ind[:, j, c], start=(j == 0), stop=(j == 1))
                        for j in range(2):
                            ins = pe.matmul(ptile[:, c], vb[:, 2 + j, :], ind[:, j, c], start=(j == 0), stop=(j == 1))
                    ins.then_inc(mmd, 1)

            @block.vector
            def _(dve):
                v = nc.vector
                c = Chain(dve, chain)
                v.memset(sums[:], 0.0)
                v.memset(aux[:], 0.0)
                v.memset(ones[:], 1.0)
                v.memset(epsc[:], EPS)
                v.memset(st[:], 0.0)
                v.memset(hi[:], 0.0)
                c(v.memset(lo[:], 0.0))
                c(v.memset(aux[0:H, :], -1e9))
                dve.wait_ge(loaded, 80)
                c(v.tensor_copy(dstf[:], dsti[:]))
                c(v.tensor_scalar(dpos[:], dstf[:], 0.0, FAR, ALU.is_lt, ALU.mult))
                c(v.tensor_tensor(dpos[:], dpos[:], dstf[:], ALU.add))
                c(v.tensor_reduce(hi[:, 0:NCH + 1], dstf[:].rearrange("p (c g) -> p c g", g=G), AX, ALU.max))
                v.tensor_reduce(lo[:, 0:NCH + 1], dpos[:].rearrange("p (c g) -> p c g", g=G), AX, ALU.min).then_inc(red, 1)
                dve.wait_ge(turned, 1)
                c(v.tensor_reduce(st[:, HI], pt[:, 0:2, :], AX, ALU.max))
                c(v.tensor_reduce(st[:, LO], pt[:, 2:4, :], AX, ALU.min))
                c(v.tensor_tensor(st[:, CNT], st[:, HI], st[:, LO], ALU.subtract))
                c(v.tensor_copy(sti[:], st[:, CNT]))
                c(v.tensor_single_scalar(sti[:], sti[:], 7, ALU.arith_shift_right))
                c(v.tensor_copy(st[:, CNT], sti[:]))
                c(v.tensor_tensor(tri[:], identf[:], iotaf[:], ALU.mult))
                c(v.tensor_reduce(st[:, 6:7], tri[:], AX, ALU.add))
                c(v.tensor_scalar(st[:, 7:8], st[:, 6:7], float(P), None, ALU.add))
                c(v.tensor_scalar(st[:, 16:18], st[:, IDX], float(NCH), None, ALU.is_lt))
                c(v.tensor_scalar(st[:, CNT], st[:, CNT], 1.0, None, ALU.add))
                c(v.tensor_tensor(st[:, CNT], st[:, CNT], st[:, 16:18], ALU.mult))
                c(v.tensor_scalar(st[:, 16:18], st[:, 16:18], -FAR, FAR, ALU.mult, ALU.add))
                c(v.tensor_tensor(st[:, CNT], st[:, CNT], st[:, 16:18], ALU.add))
                c(v.tensor_copy(st[:, PRE.start + 1:PRE.stop], st[:, CNT.start:CNT.start + 1]))
                v.tensor_scalar(tri[:], iotaf[:], st[:, 6:7], None, ALU.is_gt).then_inc(mm, 1)
                dve.wait_ge(mm, 1)
                dve.wait_ge(mmd, 1)
                c(v.tensor_copy(st[:, CUM], pc[:, 0:2]))
                c(v.tensor_tensor(st[:, END], st[:, CUM], st[:, CNT], ALU.add))
                c(v.tensor_scalar(st[:, 16:18], st[:, CUM], -float(P), None, ALU.mult))
                c(v.tensor_tensor(st[:, VAL], st[:, 16:18], st[:, LO], ALU.add))
                for j in range(2):
                    c(v.tensor_scalar(vb[:, j, :], ones[:], st[:, VAL.start + j:VAL.start + j + 1], None, ALU.mult))
                    c(v.tensor_scalar(vb[:, 2 + j, :], ones[:], st[:, IDX.start + j:IDX.start + j + 1], float(G),
                                      ALU.mult, ALU.mult))
                lr, lp = NCH % P, NCH // P
                v.tensor_scalar(st[:, 18:19], identf[:, lr:lr + 1], st[:, CUM.start + lp:CUM.start + lp + 1],
                                None, ALU.mult).then_inc(mm, 1)
                dve.wait_ge(mmd, 2)
                c(v.tensor_copy(ki[:, 0:1], pc[0:1, 2:3]))
                c(v.tensor_single_scalar(ki[:, 0:1], ki[:, 0:1], R - 1, ALU.add))
                c(v.tensor_single_scalar(ki[:, 0:1], ki[:, 0:1], R.bit_length() - 1, ALU.arith_shift_right))
                c(v.tensor_copy(kf[:, 0:1], ki[:, 0:1]))
                turns = PG // R
                c(v.tensor_scalar(kf[:, 1:1 + PAGES], k0[0:1, 0:PAGES], -float(turns), kf[:, 0:1], ALU.mult, ALU.add))
                c(v.tensor_scalar(kf[:, 64:64 + PAGES], kf[:, 1:1 + PAGES], 0.0, None, ALU.is_gt))
                c(v.tensor_scalar(kf[:, 1:1 + PAGES], kf[:, 1:1 + PAGES], 2.0, float(turns), ALU.max, ALU.min))
                c(v.tensor_scalar(kf[:, 1:1 + PAGES], kf[:, 1:1 + PAGES], -2.0, None, ALU.add))
                c(v.tensor_reduce(kf[:, 0:1], kf[:, 64:64 + PAGES], AX, ALU.add))
                c(v.tensor_copy(meta[0:1, 0:1 + PAGES], kf[:, 0:1 + PAGES]))
                c(v.tensor_scalar(kcur[:], k0[:], -float(PG), None, ALU.add))
                dve.engine_nop().then_inc(metac, 1)
                dve.wait_ge(metac, 1)
                npages = dve.value_load(meta[0:1, 0:1], min_val=1, max_val=PAGES)
                with dve.Fori(0, npages) as pg:
                    c = Chain(dve, chain2, pg * PAGE_LINKS)
                    c(v.tensor_scalar(kcur[:], kcur[:], float(PG), None, ALU.add))
                    for j in range(2):
                        c(v.tensor_scalar(tmp[:], kcur[:], st[:, CUM.start + j:CUM.start + j + 1], None, ALU.is_ge))
                        c(v.scalar_tensor_tensor(out=ind[:, j, :], in0=kcur[:], scalar=st[:, END.start + j:END.start + j + 1],
                                                 in1=tmp[:], op0=ALU.is_lt, op1=ALU.mult))
                    dve.sem_inc(pgm, 1)
                    dve.wait_ge(mmd, pg + 3)
                    c(v.tensor_copy(tilerow[:], ptile[:]))
                    c(v.tensor_scalar(baserow[:], kcur[:], float(P), None, ALU.mult))
                    c(v.tensor_tensor(baserow[:], baserow[:], pbase[:], ALU.add))
                    c(v.tensor_scalar(baserow[:], baserow[:], 0.0, float(NP), ALU.max, ALU.min))
                    c(v.tensor_copy(pairrow[:, :, 0], tilerow[0:1, :]))
                    c(v.tensor_copy(pairrow[:, :, 1], baserow[0:1, :]))
                    assert c.n == PAGE_LINKS
                    dve.sem_inc(pgd, 1)
                    dve.wait_ge(page_stored, pg + 1)



class Visits:

    def __init__(self, env, sem):
        (self.nc, self.dstf, self.srci, self.identf, self.iotaf, self.epsc, self.meta, self.pairs, self.baseB,
         self.sums, self.aux, self.visit_base, self.visit_pair) = env
        self.page_loaded, self.page_done = sem("page_loaded"), sem("page_done")
        self.regs = {}

    def serve(self, sp, users, turn=None):
        npages = sp.value_load(self.meta[0:1, 0:1], min_val=1, max_val=PAGES)
        sp.sem_inc(self.page_done, 1)
        with sp.Fori(0, npages) as pg:
            sp.wait_ge(self.page_done, pg * users + 1)
            sp.dma_start(self.pairs[:], self.visit_pair[ds(pg, 1), :]).then_inc(self.page_loaded, 16)
            sp.dma_start(self.baseB[:], self.visit_base[ds(pg, 1), :].to_broadcast([P, PG])).then_inc(self.page_loaded, 16)
            if turn:
                self.page(sp, pg, turn, 0)

    def page(self, eng, pg, turn, depth):
        assert depth <= R
        eng.wait_ge(self.page_loaded, pg * 32 + 32)
        groups = eng.value_load(self.meta[0:1, ds(pg + 1, 1)], min_val=0, max_val=PG // R - 2) + 2

        def visit(first, off):
            return first + off, off % R, pg * PG + first + off

        for u in range(R):
            turn(*(visit(0, u - lag) if u >= lag else None for lag in range(depth + 1)))
        with eng.Fori(0, groups - 1) as g:
            for u in range(R):
                turn(*(visit(g * R, R + u - lag) for lag in range(depth + 1)))
        for u in range(depth):
            turn(*(visit(groups * R - R, R + u - lag) if lag > u else None for lag in range(depth + 1)))

    def loop(self, eng, turn, depth=0):
        npages = eng.value_load(self.meta[0:1, 0:1], min_val=1, max_val=PAGES)
        with eng.Fori(0, npages) as pg:
            self.page(eng, pg, turn, depth)
            eng.drain().then_inc(self.page_done, 1)

    def pair(self, eng, i, slot=None):
        if (eng, slot) not in self.regs:
            self.regs[eng, slot] = [eng.alloc_register(f"pair{k}_{self.nc.next_id()}") for k in range(2)]
        regs = self.regs[eng, slot]
        eng.load(regs, self.pairs[0:1, ds(i * 2, 2)])
        return self.held(eng, slot)

    def held(self, eng, slot):
        tile, node = self.regs[eng, slot]
        return eng.snap(tile, min_val=0, max_val=T - G), eng.snap(node, min_val=0, max_val=NP)


def gather_rows(vis, pool, table, width, slots, rows, copied, landed, free):
    g = vis.nc.gpsimd
    copied.start(pool)

    def turn(visit):
        i, r, v = visit
        tile, _ = vis.pair(pool, i)
        for used in free:
            used.wait(pool, v - R)
        g.tensor_copy(slots[:, r * G:(r + 1) * G], vis.srci[:, ds(tile, G)]).then_inc(copied.sem, 1)
        copied.wait(pool, v)
        g.nop(nofuse=True)
        for t in range(G):
            g.indirect_dma_start(rows[:, r, t, 0:width], None, table,
                                 bass.IndirectOffsetOnAxis(slots[:, r * G + t:r * G + t + 1], 0)).then_inc(landed[r], 16)

    vis.loop(pool, turn)


def wait_landed(eng, landed, r, v):
    eng.wait_ge(landed[r], (v - r) * (16 * G // R) + 16 * G)


def in_pairs(eng, turn):
    turn((0, 0), None)
    turn((1, 1), (0, 0))
    with eng.Fori(0, STEPS // 2 - 1) as half:
        i = half * 2 + 2
        turn((i, 0), (i - 1, 1))
        turn((i + 1, 1), (i, 0))
    turn(None, (STEPS - 1, 1))


def norm_vector(nc, dve, c, ev, it, k, xin, xc, sq, s, squaring=None, rooting=None):
    v = nc.vector
    c(v.tensor_reduce(s[:, 0:BATCH], xin, AX, ALU.add))
    c(v.tensor_scalar(s[:, 8:8 + BATCH], s[:, 0:BATCH], -1.0 / D, None, ALU.mult))
    v.tensor_tensor(xc, xin, s[:, 8:8 + BATCH].unsqueeze(2).to_broadcast([P, BATCH, D]), ALU.add).then_inc(ev["centred"].sem, 1)
    if squaring:
        squaring()
    ev["squared"].wait(dve, it, k)
    v.tensor_reduce(s[:, 16:16 + BATCH], sq, AX, ALU.add).then_inc(ev["varied"].sem, 1)
    if rooting:
        rooting()
    ev["rooted"].wait(dve, it, k)
    c(v.reciprocal(s[:, 32:32 + BATCH], s[:, 24:24 + BATCH]))
    c(v.tensor_tensor(xc, xc, s[:, 32:32 + BATCH].unsqueeze(2).to_broadcast([P, BATCH, D]), ALU.mult))


def norm_scalar(nc, act, ev, it, k, xc, sq, s, epsc):
    ev["centred"].wait(act, it, k)
    nc.scalar.activation(sq, xc, ACT.Square).then_inc(ev["squared"].sem, 1)
    ev["varied"].wait(act, it, k)
    nc.scalar.activation(s[:, 24:24 + BATCH], s[:, 16:16 + BATCH], ACT.Sqrt, bias=epsc[:], scale=1.0 / D).then_inc(ev["rooted"].sem, 1)


def blocks_of(table, it):
    return table.rearrange("(b p) f -> p b f", p=P)[:, ds(it * BATCH, BATCH), :]


def load_blocks(nc, pool, streams, used):
    with pool.Fori(0, STEPS // 2) as half:
        i = half * 2
        for r in range(2):
            used.wait(pool, i + r - 2)
            pool.nop(nofuse=True)
            for table, slot, landed in streams:
                pool.dma_start(slot[:, r], blocks_of(table, i + r)).then_inc(landed[r], 16)



def factor_plan(CG):
    C011, C110, C121 = CG[1], CG[3], CG[4]
    plan = [(0, [(0, 1.0)])]
    plan += [(1 + k, [(1 + k, float(C011[0, k, k]))]) for k in range(3)]
    plan += [(4 + i, [(1 + i, float(C110[i, i, 0]))]) for i in range(3)]
    for i in range(3):
        for k in range(3):
            plan.append((7 + 3 * i + k, [(4 + j, float(C121[i, j, k])) for j in range(5) if abs(C121[i, j, k]) > 1e-7]))
    return plan


def phase_first_table(env, x, W0, W0T, aT, WeT, ef, efw, table0, sh, shx, CG):
    nc, dstf, srci, identf, iotaf, epsc, meta, pairs, baseB, sums, aux, visit_base, visit_pair = env
    with ExitStack() as ctx:
        sb = lambda n, s, d=F32: ctx.enter_context(nc.sbuf_tensor(n, s, d))
        ps = lambda n, s, d=F32: ctx.enter_context(nc.psum_tensor(n, s, d))
        sem = phase_semaphores(nc, ctx, "")
        WX = DW + H
        w0 = sb("t_w0", [P, D])
        wext = sb("t_wext", [P, DW + H])
        asrc = sb("t_asrc", [P, H])
        adst = sb("t_adst", [P, H])
        we = sb("t_we", [P, G * H])
        xin = sb("t_xin", [P, 2, BATCH, D])
        xc = sb("t_xc", [P, BATCH, D])
        sq = sb("t_sq", [P, BATCH, D])
        s = sb("t_s", [P, 40])
        hT = sb("t_hT", [P, BC])
        row = sb("t_row", [P, BATCH, DW])
        sdp = sb("t_sdp", [P, BATCH, 32 + 3 * H])
        sdh = sb("t_sdh", [P, 2, BATCH, H], BF16)
        sdf = sb("t_sdf", [P, BATCH, H])
        raw = sb("t_raw", [P, 2, FT, 9])
        fac = sb("t_fac", [P, FT, NSH])
        eft = sb("t_eft", [P, 2, EC, P])
        pT = ps("t_pT", [P, 1024])
        pw = ps("t_pw", [P, 3, 512])
        pd = ps("t_pd", [P, 2, 512])
        pe_ = ps("t_pe", [P, 512])
        loaded, zeroed, placed, wready = (sem(n) for n in ("t_loaded", "t_zeroed", "t_placed", "t_wready"))
        xl = [sem("t_xl0"), sem("t_xl1")]
        stored, chain, nchain, fchain = (sem(n) for n in ("t_stored", "t_chain", "t_nchain", "t_fchain"))
        efl, rawl = ([sem(f"t_{n}{r}") for r in range(2)] for n in ("efl", "rawl"))
        facs = sem("t_facs")
        plan = factor_plan(CG)
        TERMS = max(len(terms) for _, terms in plan)
        ev = {n: Event(sem("t_" + n)) for n in
              ("centred", "squared", "varied", "rooted", "normed", "turned", "copied", "projected", "rowed", "ef_mm", "ef_out", "kept", "parted", "spread", "made")}

        with nc.Block() as block:
            @block.sync
            def _(sp):
                sp.dma_start(w0[:], W0).then_inc(loaded, 16)
                sp.dma_start(wext[:, 0:D], W0T).then_inc(loaded, 16)
                sp.wait_ge(zeroed, 1)
                with nc.allow_non_contiguous_dma(reason="attention vectors and W_e into block diagonals"):
                    for h in range(H):
                        sp.dma_start(asrc[h * HD:(h + 1) * HD, h:h + 1], aT[0:HD, h:h + 1]).then_inc(placed, 16)
                        sp.dma_start(adst[h * HD:(h + 1) * HD, h:h + 1], aT[HD:2 * HD, h:h + 1]).then_inc(placed, 16)
                    for t in range(G):
                        sp.dma_start(we[16 * t:16 * t + 16, H * t:H * t + H], WeT).then_inc(placed, 16)
                ev["kept"].start(sp)
                sp.sem_inc(facs, 16)
                with sp.Fori(0, STEPS // 2) as half:
                    i = half * 2
                    for r in range(2):
                        ev["made"].wait(sp, i + r)
                        sp.dma_start(shx[:, ds((i + r) * (FT * NSH), FT * NSH)], fac[:].rearrange("p t j -> p (t j)"))\
                            .then_inc(facs, 16)
                        ev["rowed"].wait(sp, i + r)
                        sp.dma_start(blocks_of(table0, i + r), row[:]).then_inc(stored, 16)
                        sp.wait_ge(stored, (i + r) * 16 + 16)
                        sp.sem_inc(ev["kept"].sem, 1)
                sp.wait_ge(facs, STEPS * 16 + 16)

            @block.gpsimd
            def _(pool):
                with pool.Fori(0, STEPS // 2) as half:
                    i = half * 2
                    for r in range(2):
                        ev["centred"].wait(pool, i + r - 2)
                        ev["ef_mm"].wait(pool, i + r - 2)
                        pool.nop(nofuse=True)
                        pool.dma_start(xin[:, r], blocks_of(x, i + r)).then_inc(xl[r], 16)
                        ev["made"].wait(pool, i + r - 2)
                        pool.nop(nofuse=True)
                        pool.dma_start(raw[:, r].rearrange("p t j -> p (t j)"), sh[:, ds((i + r) * (FT * 9), FT * 9)])\
                            .then_inc(rawl[r], 16)
                        pool.dma_start(eft[:, r], ef[:, ds((i + r) * EC, EC), :]).then_inc(efl[r], 16)

            @block.tensor
            def _(pe):
                for n in ("turned", "projected", "spread", "ef_mm"):
                    ev[n].start(pe)
                pe.wait_ge(loaded, 32)
                pe.wait_ge(placed, 16 * (2 * H + G))
                pe.matmul(pe_[:, 0:H], w0[:], asrc[:], start=True, stop=True)
                pe.matmul(pe_[:, H:2 * H], w0[:], adst[:], start=True, stop=True).then_inc(wready, 1)
                pe.wait_ge(wready, 2)

                def turn(now, last):
                    if now:
                        it, r = now
                        pe.wait_ge(efl[r], (it - r) * 8 + 16)
                        ev["ef_out"].wait(pe, it - 1)
                        for k in range(EC):
                            ins = pe.matmul(pe_[:, k * G * H:(k + 1) * G * H], eft[:, r, k, :], we[:], start=True, stop=True)
                        ins.then_inc(ev["ef_mm"].sem, 1)
                    if last:
                        ev["parted"].wait(pe, last[0])
                        pe.nop(nofuse=True)
                        for b in range(BATCH):
                            ins = pe.transpose(pd[0:32 + 3 * H, b // 4, (b % 4) * P:(b % 4 + 1) * P], sdp[:, b, :], identf[:])
                        ins.then_inc(ev["spread"].sem, 1)
                    if now:
                        ev["normed"].wait(pe, it)
                        ev["copied"].wait(pe, it - 1)
                        pe.nop(nofuse=True)
                        for b in range(BATCH):
                            ins = pe.transpose(pT[:, b * P:(b + 1) * P], xc[:, b, :], identf[:])
                        ins.then_inc(ev["turned"].sem, 1)
                        ev["copied"].wait(pe, it)
                        ev["rowed"].wait(pe, it - 1)
                        for b in range(BATCH):
                            ins = pe.matmul(pw[:, b // 3, (b % 3) * WX:(b % 3 + 1) * WX], hT[:, b * P:(b + 1) * P], wext[:],
                                            start=True, stop=True)
                        ins.then_inc(ev["projected"].sem, 1)

                in_pairs(pe, turn)

            @block.scalar
            def _(act):
                for n in ("squared", "rooted", "copied", "ef_out"):
                    ev[n].start(act)
                with act.Fori(0, STEPS) as it:
                    norm_scalar(nc, act, ev, it, 1, xc[:], sq[:], s, epsc)
                    ev["ef_mm"].wait(act, it)
                    act.nop(nofuse=True)
                    nc.scalar.activation(efw[:, ds(it * (EC * G * H), EC * G * H)], pe_[:, 0:EC * G * H], ACT.Copy)\
                        .then_inc(ev["ef_out"].sem, 1)
                    ev["turned"].wait(act, it)
                    ev["projected"].wait(act, it - 1)
                    nc.scalar.activation(hT[:], pT[:, 0:BC], ACT.Copy).then_inc(ev["copied"].sem, 1)

            @block.vector
            def _(dve):
                v = nc.vector
                for n in ("centred", "varied", "normed", "rowed", "parted", "made"):
                    ev[n].start(dve)
                v.memset(asrc[:], 0.0)
                v.memset(adst[:], 0.0)
                v.memset(we[:], 0.0).then_inc(zeroed, 1)
                dve.wait_ge(wready, 1)
                dve.wait_ge(loaded, 32)
                v.memset(sdp[:], 0.0)
                v.tensor_copy(wext[:, D:WX], pe_[:, 0:2 * H]).then_inc(wready, 1)

                def turn(now, last):
                    c = Chain(dve, chain, last[0] * 8) if last else None
                    part = lambda k: sdp[:, :, 32 + k * H:32 + (k + 1) * H]

                    def rows():
                        if last:
                            ev["projected"].wait(dve, last[0])
                            ev["kept"].wait(dve, last[0] - 1)
                            three = lambda q, n: pw[:, q, 0:n * WX].rearrange("p (b f) -> p b f", f=WX)
                            for q, n in ((0, 3), (1, 3), (2, 1)):
                                v.tensor_copy(row[:, 3 * q:3 * q + n, :], three(q, n)[:, :, 0:DW])
                                ins = v.tensor_copy(sdf[:, 3 * q:3 * q + n, :], three(q, n)[:, :, DW:WX])
                            c(ins)
                            dve.sem_inc(ev["rowed"].sem, 1)
                            c(v.tensor_copy(sdh[:, 0], sdf[:]))
                            c(v.tensor_copy(part(0), sdh[:, 0]))

                    def parts():
                        if last:
                            c(v.tensor_tensor(sdf[:], sdf[:], part(0), ALU.subtract))
                            c(v.tensor_copy(sdh[:, 1], sdf[:]))
                            c(v.tensor_copy(part(1), sdh[:, 1]))
                            c(v.tensor_tensor(part(2), sdf[:], part(1), ALU.subtract))
                            dve.sem_inc(ev["parted"].sem, 1)

                    if now:
                        it, r = now
                        n = Chain(dve, nchain, it * 4)
                        dve.wait_ge(xl[r], (it - r) * 8 + 16)
                        ev["turned"].wait(dve, it - 1)
                        norm_vector(nc, dve, n, ev, it, 1, xin[:, r], xc[:], sq[:], s, rows, parts)
                        assert n.n == 4
                        v.tensor_single_scalar(xc[:], xc[:], 0.0, ALU.max).then_inc(ev["normed"].sem, 1)
                        f = Chain(dve, fchain, it * TERMS)
                        dve.wait_ge(rawl[r], (it - r) * 8 + 16)
                        dve.wait_ge(facs, it * 16 + 16)
                        for k in range(TERMS):
                            for col, terms in plan:
                                if k == 0:
                                    ins = v.tensor_scalar(fac[:, :, col], raw[:, r, :, terms[0][0]], terms[0][1], None, ALU.mult)
                                elif k < len(terms):
                                    ins = v.scalar_tensor_tensor(out=fac[:, :, col], in0=raw[:, r, :, terms[k][0]], scalar=terms[k][1],
                                                                 in1=fac[:, :, col], op0=ALU.mult, op1=ALU.add)
                            f(ins)
                        dve.sem_inc(ev["made"].sem, 1)
                    else:
                        rows()
                        parts()
                    if last:
                        lt = last[0]
                        ev["spread"].wait(dve, lt)
                        v.tensor_copy(aux[32:32 + 3 * H, ds(lt * BC, 4 * P)], pd[32:32 + 3 * H, 0, :])
                        c(v.tensor_copy(aux[32:32 + 3 * H, ds(lt * BC + 4 * P, 3 * P)], pd[32:32 + 3 * H, 1, 0:3 * P]))
                        assert c.n == 8, c.n

                in_pairs(dve, turn)



def phase_attention(env, efw, table0):
    nc, dstf, srci, identf, iotaf, epsc, meta, pairs, baseB, sums, aux, visit_base, visit_pair = env
    with ExitStack() as ctx:
        sb = lambda n, s, d=F32: ctx.enter_context(nc.sbuf_tensor(n, s, d))
        ps = lambda n, s, d=F32: ctx.enter_context(nc.psum_tensor(n, s, d))
        sem = phase_semaphores(nc, ctx, "a_")
        vis = Visits(env, sem)
        GH = G * H
        GV = 5
        PH = 3 * H
        slots = sb("a_slots", [P, R * G], I32)
        rows = sb("a_rows", [P, R, G, DW])
        rel = sb("a_rel", [P, 2, G])
        far = sb("a_far", [P, R, G, P], BF16)
        hot = sb("a_hot", [P, G, P])
        hotT = sb("a_hotT", [P, R, G, P], BF16)
        wsd = sb("a_wsd", [PH, P])
        sdn = sb("a_sdn", [P, PH], BF16)
        zs = sb("a_zs", [P, GH])
        z = sb("a_z", [P, GH])
        z2 = sb("a_z2", [P, GH])
        attn = sb("a_attn", [P, R, GH])
        parts = sb("a_parts", [P, 3, GH], BF16)
        rest = sb("a_rest", [P, GH])
        partsT = sb("a_partsT", [3 * GH, 2, P], BF16)
        pick = sb("a_pick", [3 * GH, GH, P], BF16)
        id3 = sb("a_id3", [3 * GH, GH])
        identb = sb("a_identb", [P, P], BF16)
        ident4 = sb("a_ident4", [P, H, P], BF16)
        iotab = sb("a_iotab", [P, P], BF16)
        tmax = sb("a_tmax", [P, H, G])
        cmax = sb("a_cmax", [P, 2, H])
        wm = sb("a_wm", [H, P])
        top = sb("a_top", [P, H])
        pack = sb("a_pack", [P, 68])
        pack2 = sb("a_pack2", [P, 2, 68])
        mparts = sb("a_mparts", [P, 3, H], BF16)
        mrest = sb("a_mrest", [P, H])
        dm = sb("a_dm", [P, H])
        ms = sb("a_ms", [P, GH])
        e1 = sb("a_e1", [P, GH])
        e2 = sb("a_e2", [P, GH])
        msg = sb("a_msg", [P, 2, G, DW])
        agg = sb("a_agg", [P, D])
        scale_rows = sb("a_scale_rows", [P, 2, D])
        pz = ps("a_pz", [P, 3, 512])
        phT = ps("a_phT", [P, G * P], BF16)
        pa = ps("a_pa", [P, 512])
        pm = ps("a_pm", [P, 512])
        pagg = ps("a_pagg", [P, 512])
        ptr = ps("a_ptr", [P, 512])
        SD, NM, EDGES = slice(0, PH), slice(0, H), slice(32, 32 + G * PH)
        ptop = phT[:, 0:2 * P].bitcast(F32)
        ppT = pa[:, 256:256 + P // 2].bitcast(BF16)
        landed = [sem(f"landed{r}") for r in range(R)]
        setup, setup_chain = sem("setup"), sem("setup_chain")
        names = ("copied rel_ far_ wsd_ sdn_ hot_ phT_ hotT_ sd sg zs_ z_ z2_ attn_ hi_ r1_ mid_ lo_ ppT_ partsT_ "
                 "cmax_ wm_ nm mnew dm_ mhi_ mr1_ mmid_ mlo_ sc mg ms_ e1_ e2_ ex msg_ weighed pagg_ aggden topT_ ptr_ num1 num2 "
                 "den1 den2 mput").split()
        ev = {n: Event(sem(n)) for n in names}
        ev["zmm"], ev["zred"] = Event(sem("zmm"), G), Event(sem("zred"), G)

        def owns(eng, names):
            for n in names.split():
                ev[n].start(eng)

        with nc.Block() as block:
            @block.sync
            def _(sp):
                vis.serve(sp, 4)

            @block.gpsimd
            def _(pool):
                gather_rows(vis, pool, table0, DW, slots, rows, ev["copied"], landed, [ev["msg_"], ev["weighed"]])

            @block.tensor
            def _(pe):
                owns(pe, "sd sg phT_ ppT_ zmm nm mg pagg_ topT_ ptr_")
                pe.wait_ge(setup, 1)

                def turn(now, mid, old, fin):
                    def highest(*tiles):
                        if mid:
                            i, r, v = mid
                            for t in tiles:
                                if t == 0:
                                    ev["partsT_"].wait(pe, v)
                                ev["zred"].wait(pe, v, (-1, 0, 0)[t] if t < 3 else t - 2)
                                pe.matmul(pz[:, t % 3, :], far[:, r, t, :], ident4[:].rearrange("p h e -> p (h e)"),
                                          start=True, stop=False)
                                for h in range(H):
                                    ins = pe.matmul(pz[:, t % 3, h * P:(h + 1) * P], pick[:, t * H + h, :], partsT[:, r % 2],
                                                    start=False, stop=(h == H - 1))
                                ins.then_inc(ev["zmm"].sem, 1)

                    highest(0, 1, 2)
                    if now:
                        i, r, v = now
                        ev["wsd_"].wait(pe, v)
                        ev["partsT_"].wait(pe, v - 1)
                        pe.nop(nofuse=True)
                        pe.transpose(pa[:, SD], wsd[:], identf[0:PH, 0:PH]).then_inc(ev["sd"].sem, 1)
                        ev["far_"].wait(pe, v)
                        ev["hotT_"].wait(pe, v - 1)
                        ev["mput"].wait(pe, v - 3)
                        for t in range(G):
                            ins = pe.transpose(phT[:, t * P:(t + 1) * P], far[:, r, t, :], identb[:])
                        ins.then_inc(ev["phT_"].sem, 1)
                    highest(3)
                    if old:
                        i, r, v = old
                        ev["mlo_"].wait(pe, v)
                        ev["dm_"].wait(pe, v)
                        for t in range(G):
                            ins = pe.matmul(pm[:, 32 + t * PH:32 + (t + 1) * PH], hotT[:, r, t, :],
                                            mparts[:].rearrange("p k h -> p (k h)"), start=True, stop=True)
                        ins.then_inc(ev["mg"].sem, 1)
                    if now:
                        i, r, v = now
                        ev["sdn_"].wait(pe, v)
                        ev["hotT_"].wait(pe, v)
                        for t in range(G):
                            ins = pe.matmul(pa[:, 32 + t * PH:32 + (t + 1) * PH], hotT[:, r, t, :], sdn[:], start=True, stop=True)
                        ins.then_inc(ev["sg"].sem, 1)
                    if old:
                        pe.transpose(ptop[0:H, 0:P], top[:], identf[:]).then_inc(ev["topT_"].sem, 1)
                    highest(4, 5)
                    highest(6)
                    if mid:
                        i, r, v = mid
                        ev["wm_"].wait(pe, v)
                        ev["ms_"].wait(pe, v - 1)
                        pe.nop(nofuse=True)
                        pe.transpose(pm[:, NM], wm[:], identf[0:H, 0:H]).then_inc(ev["nm"].sem, 1)
                    highest(7)
                    if fin:
                        i, r, v = fin
                        q = r % 2
                        ev["msg_"].wait(pe, v)
                        ev["weighed"].wait(pe, v)
                        ev["hot_"].wait(pe, v)
                        ev["aggden"].wait(pe, v - 1)
                        for t in range(G):
                            ins = pe.matmul(pagg[:, 0:DW], hot[:, t, :], msg[:, q, t, :], start=(t == 0), stop=(t == G - 1))
                        ins.then_inc(ev["pagg_"].sem, 1)
                        ev["sc"].wait(pe, v)
                        ev["aggden"].wait(pe, v)
                        ev["num2"].wait(pe, v - 1)
                        ev["den2"].wait(pe, v - 1)
                        pe.transpose(ptr[:, 0:P], agg[:], identf[:])
                        pe.matmul(ptr[:, P:2 * P], scale_rows[:, q], identf[:], start=True, stop=True)
                        pe.transpose(ptr[0:68, 2 * P:3 * P], pack[:], identf[:])
                        pe.transpose(ptr[0:68, 3 * P:4 * P], pack2[:, q], identf[:]).then_inc(ev["ptr_"].sem, 1)
                    if now:
                        i, r, v = now
                        ev["lo_"].wait(pe, v)
                        pe.transpose(ppT[0:3 * GH, :], parts[:].rearrange("p a b -> p (a b)"), identb[:]).then_inc(ev["ppT_"].sem, 1)

                vis.loop(pe, turn, 3)

            @block.scalar
            def _(act):
                a = nc.scalar
                owns(act, "weighed wsd_ sdn_ hot_ hotT_ partsT_ wm_ sc ex aggden mput")
                act.wait_ge(setup, 1)

                def turn(now, mid, old, fin):
                    if now:
                        i, r, v = now
                        _, node = vis.pair(act, i)
                        ev["sd"].wait(act, v - 1)
                        act.nop(nofuse=True)
                        a.activation(wsd[:], aux[32:32 + PH, ds(node, P)], ACT.Copy).then_inc(ev["wsd_"].sem, 1)
                    if old:
                        i, r, v = old
                        q = r % 2
                        _, old_node = vis.pair(act, i)
                        ev["dm_"].wait(act, v)
                        ev["ptr_"].wait(act, v - 2)
                        a.activation(pack2[:, q, 64:68], dm[:], ACT.Exp).then_inc(ev["sc"].sem, 1)
                    if now:
                        i, r, v = now
                        ev["sd"].wait(act, v)
                        ev["sg"].wait(act, v - 1)
                        a.activation(sdn[:], pa[:, SD], ACT.Copy).then_inc(ev["sdn_"].sem, 1)
                    if old:
                        i, r, v = old
                        ev["sc"].wait(act, v)
                        a.activation(scale_rows[:, q].rearrange("p (h d) -> p h d", h=H),
                                     pack2[:, q, 64:68].unsqueeze(2).to_broadcast([P, H, HD]), ACT.Copy)
                    if now:
                        i, r, v = now
                        ev["phT_"].wait(act, v)
                        ev["mg"].wait(act, v - R)
                        a.activation(hotT[:, r].rearrange("p t e -> p (t e)"), phT[:], ACT.Copy, scale=1.0 / BIG, bias=1.0)\
                            .then_inc(ev["hotT_"].sem, 1)
                    if fin:
                        i, r, v = fin
                        ev["pagg_"].wait(act, v - 1)
                        a.activation(hot[:], far[:, r], ACT.Copy, scale=1.0 / BIG, bias=1.0).then_inc(ev["hot_"].sem, 1)
                    if old:
                        i, r, v = old
                        q = r % 2
                        ev["topT_"].wait(act, v)
                        act.nop(nofuse=True)
                        a.activation(aux[0:H, ds(old_node, P)], ptop[0:H, 0:P], ACT.Copy).then_inc(ev["mput"].sem, 1)
                    if mid:
                        i, r, v = mid
                        _, mid_node = vis.pair(act, i)
                        ev["mput"].wait(act, v - 1)
                        ev["nm"].wait(act, v - 1)
                        act.nop(nofuse=True)
                        a.activation(wm[:], aux[0:H, ds(mid_node, P)], ACT.Copy).then_inc(ev["wm_"].sem, 1)
                    if old:
                        i, r, v = old
                        ev["e2_"].wait(act, v)
                        ev["pagg_"].wait(act, v - 2)
                        a.activation(msg[:, q, :, D:DW], e2[:].rearrange("p (t h) -> p t h", h=H), ACT.Exp).then_inc(ev["ex"].sem, 1)
                        ev["ex"].wait(act, v)
                        for t in range(GV, G):
                            for h in range(H):
                                ins = a.activation(msg[:, q, t, h * HD:(h + 1) * HD], rows[:, r, t, h * HD:(h + 1) * HD],
                                                   ACT.Copy, scale=msg[:, q, t, D + h:D + h + 1])
                        ins.then_inc(ev["weighed"].sem, 1)
                    if fin:
                        i, r, v = fin
                        ev["pagg_"].wait(act, v)
                        ev["ptr_"].wait(act, v - 1)
                        a.activation(agg[:], pagg[:, 0:D], ACT.Copy)
                        a.activation(pack[:, 64:68], pagg[:, D:DW], ACT.Copy).then_inc(ev["aggden"].sem, 1)
                    if now:
                        i, r, v = now
                        ev["ppT_"].wait(act, v)
                        ev["zmm"].wait(act, v - 2)
                        a.activation(partsT[:, r % 2], ppT[0:3 * GH, :], ACT.Copy).then_inc(ev["partsT_"].sem, 1)

                vis.loop(act, turn, 3)

            @block.vector
            def _(dve):
                v_ = nc.vector
                owns(dve, "rel_ far_ zs_ z_ z2_ attn_ hi_ r1_ mid_ lo_ zred cmax_ mnew dm_ mhi_ mr1_ mmid_ mlo_ ms_ e1_ e2_ "
                          "msg_ num1 num2 den1 den2")
                c = Chain(dve, setup_chain)
                c(v_.memset(pack[:], 0.0))
                c(v_.memset(pack2[:], 0.0))
                for k in range(3):
                    c(v_.tensor_copy(id3[k * GH:(k + 1) * GH, :], identf[k * GH:(k + 1) * GH, k * GH:(k + 1) * GH]))
                c(v_.tensor_copy(pick[:], id3[:].unsqueeze(2).to_broadcast([3 * GH, GH, P])))
                c(v_.tensor_copy(identb[:], identf[:]))
                c(v_.tensor_copy(iotab[:], iotaf[:]))
                c(v_.tensor_copy(ident4[:], identf[:].unsqueeze(1).to_broadcast([P, H, P])))
                dve.sem_inc(setup, 1)
                by_head = lambda ap: ap.rearrange("p (t h) -> p t h", h=H)
                by_part = lambda bank: bank[:, EDGES].rearrange("p (t k h) -> p t h k", t=G, k=3)

                def turn(now, mid, old, _, fin):
                    def highest(t):
                        if mid:
                            i, r, v = mid
                            ev["zmm"].wait(dve, v, t + 1)
                            if t == 0:
                                ev["cmax_"].wait(dve, v - 1)
                            v_.tensor_reduce(tmax[:, :, t], pz[:, t % 3, :].rearrange("p (h e) -> p h e", h=H), AX, ALU.max)\
                                .then_inc(ev["zred"].sem, 1)

                    def fars(t0, t1):
                        if now:
                            i, r, v = now
                            for t in range(t0, t1):
                                ins = v_.tensor_scalar(far[:, r, t, :], iotab[:], rel[:, r % 2, t:t + 1], -BIG, ALU.not_equal, ALU.mult)
                            if t1 == G:
                                ins.then_inc(ev["far_"].sem, 1)

                    if fin:
                        _, fr, fv = fin
                        _, fin_node = vis.held(dve, fr)
                    if now:
                        i, r, v = now
                        tile, _ = vis.pair(dve, i, r)
                        ev["zmm"].wait(dve, v - R)
                        ev["hot_"].wait(dve, v - R)
                        ev["far_"].wait(dve, v - 1)
                        v_.tensor_scalar(rel[:, r % 2], dstf[:, ds(tile, G)], baseB[:, ds(i, 1)], None, ALU.subtract).then_inc(ev["rel_"].sem, 1)
                    if old:
                        i, r, v = old
                        q = r % 2
                        ev["nm"].wait(dve, v)
                        ev["cmax_"].wait(dve, v)
                        ev["topT_"].wait(dve, v - 1)
                        ev["mg"].wait(dve, v - 1)
                        v_.tensor_tensor(top[:], pm[:, NM], cmax[:, q], ALU.max).then_inc(ev["mnew"].sem, 1)
                    if now:
                        ev["rel_"].wait(dve, now[2])
                    fars(0, 4)
                    if old:
                        ev["mnew"].wait(dve, v)
                        v_.tensor_copy(mparts[:, 0], top[:]).then_inc(ev["mhi_"].sem, 1)
                        ev["sc"].wait(dve, v - 1)
                        v_.tensor_tensor(dm[:], pm[:, NM], top[:], ALU.subtract).then_inc(ev["dm_"].sem, 1)
                    fars(4, 8)
                    if fin:
                        win = ds(fin_node, P)
                        ev["num2"].wait(dve, fv - 1)
                        ev["den2"].wait(dve, fv - 1)
                        ev["ptr_"].wait(dve, fv)
                        v_.tensor_tensor(sums[:, win], sums[:, win], ptr[:, P:2 * P], ALU.mult).then_inc(ev["num1"].sem, 1)
                        v_.tensor_tensor(aux[64:68, win], aux[64:68, win], ptr[64:68, 3 * P:4 * P], ALU.mult).then_inc(ev["den1"].sem, 1)
                        ev["num1"].wait(dve, fv)
                        v_.tensor_tensor(sums[:, win], sums[:, win], ptr[:, 0:P], ALU.add).then_inc(ev["num2"].sem, 1)
                        ev["den1"].wait(dve, fv)
                        v_.tensor_tensor(aux[64:68, win], aux[64:68, win], ptr[64:68, 2 * P:3 * P], ALU.add).then_inc(ev["den2"].sem, 1)
                    if old:
                        ev["mhi_"].wait(dve, v)
                        v_.tensor_tensor(mrest[:], top[:], mparts[:, 0], ALU.subtract).then_inc(ev["mr1_"].sem, 1)
                    highest(0)
                    if old:
                        ev["mr1_"].wait(dve, v)
                        v_.tensor_copy(mparts[:, 1], mrest[:]).then_inc(ev["mmid_"].sem, 1)
                    highest(1)
                    if old:
                        ev["mmid_"].wait(dve, v)
                        v_.tensor_tensor(mparts[:, 2], mrest[:], mparts[:, 1], ALU.subtract).then_inc(ev["mlo_"].sem, 1)
                    highest(2)
                    if old:
                        ev["mg"].wait(dve, v)
                        v_.tensor_reduce(by_head(ms[:]), by_part(pm), AX, ALU.add).then_inc(ev["ms_"].sem, 1)
                    highest(3)
                    if old:
                        ev["ms_"].wait(dve, v)
                        v_.tensor_tensor(e1[:], attn[:, r], ms[:], ALU.subtract).then_inc(ev["e1_"].sem, 1)
                    if now:
                        _, r1, v1 = now
                        ev["sg"].wait(dve, v1)
                        v_.tensor_reduce(by_head(zs[:]), by_part(pa), AX, ALU.add).then_inc(ev["zs_"].sem, 1)
                    if old:
                        ev["e1_"].wait(dve, v)
                        ev["ex"].wait(dve, v - 1)
                        v_.tensor_single_scalar(e2[:], e1[:], 0.0, ALU.min).then_inc(ev["e2_"].sem, 1)
                    highest(4)
                    if now:
                        wait_landed(dve, landed, r1, v1)
                        ev["zs_"].wait(dve, v1)
                        v_.tensor_tensor(by_head(z[:]), rows[:, r1, :, D:DW], by_head(zs[:]), ALU.add).then_inc(ev["z_"].sem, 1)
                    highest(5)
                    if now:
                        ev["z_"].wait(dve, v1)
                        v_.scalar_tensor_tensor(out=z2[:], in0=z[:], scalar=0.2, in1=z[:], op0=ALU.mult, op1=ALU.max).then_inc(ev["z2_"].sem, 1)
                    highest(6)
                    if now:
                        ev["z2_"].wait(dve, v1)
                        v_.tensor_tensor(attn[:, r1], z2[:], efw[:, ds(tile * H, GH)], ALU.add).then_inc(ev["attn_"].sem, 1)
                    highest(7)
                    if now:
                        ev["attn_"].wait(dve, v1)
                        ev["ppT_"].wait(dve, v1 - 1)
                        v_.tensor_copy(parts[:, 0], attn[:, r1]).then_inc(ev["hi_"].sem, 1)
                    if mid:
                        _, rm, vm = mid
                        ev["zred"].wait(dve, vm)
                        v_.tensor_reduce(cmax[:, rm % 2], tmax[:], AX, ALU.max).then_inc(ev["cmax_"].sem, 1)
                    if now:
                        ev["hi_"].wait(dve, v1)
                        v_.tensor_tensor(rest[:], attn[:, r1], parts[:, 0], ALU.subtract).then_inc(ev["r1_"].sem, 1)
                    def weigh(t0, t1):
                        if old:
                            if t0 == 0:
                                ev["ex"].wait(dve, v)
                            part = slice(t0, t1)
                            ins = v_.tensor_tensor(msg[:, q, part, 0:D].rearrange("p t (h d) -> p t h d", h=H),
                                                   rows[:, r, part, 0:D].rearrange("p t (h d) -> p t h d", h=H),
                                                   msg[:, q, part, D:DW].unsqueeze(3).to_broadcast([P, t1 - t0, H, HD]), ALU.mult)
                            if t1 == GV:
                                ins.then_inc(ev["msg_"].sem, 1)
                    weigh(0, 1)
                    if now:
                        ev["r1_"].wait(dve, v1)
                        v_.tensor_copy(parts[:, 1], rest[:]).then_inc(ev["mid_"].sem, 1)
                    weigh(1, 2)
                    if now:
                        ev["mid_"].wait(dve, v1)
                        v_.tensor_tensor(parts[:, 2], rest[:], parts[:, 1], ALU.subtract).then_inc(ev["lo_"].sem, 1)
                    weigh(2, GV)

                vis.loop(dve, turn, 4)



def phase_sum(env, layer, table, weights):
    nc, dstf, srci, identf, iotaf, epsc, meta, pairs, baseB, sums, aux, visit_base, visit_pair = env
    counts = weights is None
    with ExitStack() as ctx:
        sb = lambda n, s, d=F32: ctx.enter_context(nc.sbuf_tensor(f"s{layer}_" + n, s, d))
        sem = phase_semaphores(nc, ctx, f"s{layer}_")
        vis = Visits(env, sem)
        slots = sb("slots", [P, R * G], I32)
        rows = sb("rows", [P, R, G, D])
        rel = sb("rel", [P, 2, G])
        hot = sb("hot", [P, 2, G, P])
        wts = sb("wts", [P, T])
        ones = sb("ones", [P, P])
        pagg = ctx.enter_context(nc.psum_tensor(f"s{layer}_pagg", [P, 2, 2, 512], F32))
        landed = [sem(f"landed{r}") for r in range(R)]
        loaded, cleared = sem("loaded"), sem("cleared")
        ev = {n: Event(sem(n)) for n in ("copied", "rel_", "hot_", "agg", "added", "counted")}

        with nc.Block() as block:
            @block.sync
            def _(sp):
                if not counts:
                    sp.dma_start(wts[:], weights).then_inc(loaded, 16)
                vis.serve(sp, 3)

            @block.gpsimd
            def _(pool):
                gather_rows(vis, pool, table, D, slots, rows, ev["copied"], landed, [ev["agg"]])

            @block.vector
            def _(dve):
                v_ = nc.vector
                for n in ("rel_", "hot_", "added", "counted"):
                    ev[n].start(dve)
                v_.memset(ones[:], 1.0).then_inc(cleared, 1)
                v_.memset(sums[:], 0.0).then_inc(cleared, 1)
                v_.memset(aux[:], 0.0).then_inc(cleared, 1)
                dve.wait_ge(cleared, 3)
                if not counts:
                    dve.wait_ge(loaded, 16)

                def turn(now, last):
                    if now:
                        i, r, v = now
                        tile, node = vis.pair(dve, i)
                        q = r % 2
                        ev["agg"].wait(dve, v - 2)
                        v_.tensor_scalar(rel[:, q], dstf[:, ds(tile, G)], baseB[:, ds(i, 1)], None, ALU.subtract).then_inc(ev["rel_"].sem, 1)
                        ev["rel_"].wait(dve, v)
                        for t in range(G):
                            if counts:
                                ins = v_.tensor_scalar(hot[:, q, t, :], iotaf[:], rel[:, q, t:t + 1], None, ALU.is_equal)
                            else:
                                ins = v_.tensor_scalar(hot[:, q, t, :], iotaf[:], rel[:, q, t:t + 1], wts[:, ds(tile + t, 1)],
                                                       ALU.is_equal, ALU.mult)
                        ins.then_inc(ev["hot_"].sem, 1)
                    if last:
                        i, r, v = last
                        tile, node = vis.pair(dve, i)
                        q = r % 2
                        ev["agg"].wait(dve, v)
                        ev["added"].wait(dve, v - 1)
                        v_.tensor_tensor(sums[:, ds(node, P)], sums[:, ds(node, P)], pagg[:, q, 0, 0:P], ALU.add).then_inc(ev["added"].sem, 1)
                        if counts:
                            ev["counted"].wait(dve, v - 1)
                            v_.tensor_tensor(aux[:, ds(node, P)], aux[:, ds(node, P)], pagg[:, q, 1, 0:P], ALU.add).then_inc(ev["counted"].sem, 1)

                vis.loop(dve, turn, 1)

            @block.tensor
            def _(pe):
                ev["agg"].start(pe)
                pe.wait_ge(cleared, 1)

                def turn(visit):
                    i, r, v = visit
                    q = r % 2
                    wait_landed(pe, landed, r, v)
                    ev["hot_"].wait(pe, v)
                    ev["added"].wait(pe, v - 2)
                    if counts:
                        ev["counted"].wait(pe, v - 2)
                        for t in range(G):
                            pe.matmul(pagg[:, q, 1, 0:P], ones[:], hot[:, q, t, :], start=(t == 0), stop=(t == G - 1))
                    for t in range(G):
                        ins = pe.matmul(pagg[:, q, 0, 0:P], rows[:, r, t, :], hot[:, q, t, :], start=(t == 0), stop=(t == G - 1))
                    ins.then_inc(ev["agg"].sem, 1)

                vis.loop(pe, turn)



def phase_tensor_product(env, table, shx, W2b, W2scale):
    nc, dstf, srci, identf, iotaf, epsc, meta, pairs, baseB, sums, aux, visit_base, visit_pair = env
    with ExitStack() as ctx:
        sb = lambda n, s, d=F32: ctx.enter_context(nc.sbuf_tensor("p_" + n, s, d))
        ps = lambda n, s, d=F32: ctx.enter_context(nc.psum_tensor("p_" + n, s, d))
        sem = phase_semaphores(nc, ctx, "p_")
        vis = Visits(env, sem)
        slots = sb("slots", [P, R * G], I32)
        rows = sb("rows", [P, R, G, D])
        rel = sb("rel", [P, 2, G])
        hot = sb("hot", [P, 2, G, P])
        fac = sb("fac", [P, R, G, NSH])
        prod = sb("prod", [P, 2, G, TW])
        t4 = sb("t4", [P, 3, G, 3, 32])
        t3 = sb("t3", [P, 3, G, 32])
        a4 = sb("a4", [P, G, 3, 32])
        a3 = sb("a3", [P, G, 32])
        w2 = sb("w2", [P, 3, D])
        w2s = sb("w2s", [P, 3])
        win = sb("win", [P, 3, P])
        pagg = ps("pagg", [P, 2, 3, 512])
        pmsg = ps("pmsg", [P, 2, 512])
        landed = [sem(f"landed{r}") for r in range(R)]
        facl = [sem(f"facl{r}") for r in range(R)]
        loaded, cleared, wchain = sem("loaded"), sem("cleared"), sem("wchain")
        ev = {n: Event(sem(n)) for n in
              ("copied", "rel_", "hot_", "t4_", "a4_", "a3_", "x1_", "made", "scalars", "agg", "win_", "msg_", "added")}
        BLK = ((0, 128), (128, 128), (256, 96))

        with nc.Block() as block:
            @block.sync
            def _(sp):
                sp.dma_start(w2[:], W2b).then_inc(loaded, 16)
                sp.dma_start(w2s[:], W2scale).then_inc(loaded, 16)
                def turn(visit):
                    i, r, v = visit
                    tile, node = vis.pair(sp, i)
                    ev["made"].wait(sp, v - R)
                    ev["scalars"].wait(sp, v - R)
                    sp.dma_start(fac[:, r].rearrange("p t j -> p (t j)"), shx[:, ds(tile * NSH, G * NSH)]).then_inc(facl[r], 16)

                vis.serve(sp, 4, turn)

            @block.gpsimd
            def _(pool):
                gather_rows(vis, pool, table, D, slots, rows, ev["copied"], landed, [ev["scalars"], ev["x1_"]])

            @block.scalar
            def _(act):
                a = nc.scalar
                for n in ("scalars", "win_"):
                    ev[n].start(act)

                def turn(now, last):
                    if now:
                        i, r, v = now
                        q = r % 2
                        wait_landed(act, landed, r, v)
                        act.wait_ge(facl[r], (v - r) * (16 // R) + 16)
                        ev["agg"].wait(act, v - 2)
                        for t in range(G):
                            a.activation(prod[:, q, t, 0:D], rows[:, r, t, :], ACT.Copy, scale=fac[:, r, t, 0:1])
                        for k in range(3):
                            for t in range(G):
                                ins = a.activation(prod[:, q, t, D + 32 * k:D + 32 * k + 32], rows[:, r, t, 0:32], ACT.Copy,
                                                   scale=fac[:, r, t, 1 + k:2 + k])
                        ins.then_inc(ev["scalars"].sem, 1)
                    if last:
                        i, r, v = last
                        q = r % 2
                        ev["agg"].wait(act, v)
                        ev["msg_"].wait(act, v - 1)
                        for b, (o, w) in enumerate(BLK):
                            ins = a.activation(win[0:w, b, :], pagg[0:w, q, b, 0:P], ACT.Copy)
                        ins.then_inc(ev["win_"].sem, 1)

                vis.loop(act, turn, 1)

            @block.vector
            def _(dve):
                v_ = nc.vector
                for n in ("rel_", "hot_", "t4_", "a4_", "a3_", "x1_", "made", "added"):
                    ev[n].start(dve)
                v_.memset(sums[:], 0.0).then_inc(cleared, 1)
                dve.wait_ge(loaded, 32)
                c = Chain(dve, wchain)
                for b in range(3):
                    c(v_.tensor_scalar(w2[:, b, :], w2[:, b, :], w2s[:, b:b + 1], None, ALU.mult))
                dve.sem_inc(cleared, 1)
                dve.wait_ge(cleared, 2)

                def turn(now, _, old):
                    if now:
                        i, r, v = now
                        tile, node = vis.pair(dve, i)
                        q = r % 2
                        ev["agg"].wait(dve, v - 2)
                        v_.tensor_scalar(rel[:, q], dstf[:, ds(tile, G)], baseB[:, ds(i, 1)], None, ALU.subtract).then_inc(ev["rel_"].sem, 1)
                        wait_landed(dve, landed, r, v)
                        dve.wait_ge(facl[r], (v - r) * (16 // R) + 16)
                        ev["made"].wait(dve, v - 1)
                        x1 = rows[:, r, :, 32:D].rearrange("p t (u i) -> p t i u", i=3)
                        for i1 in range(3):
                            ins = v_.tensor_tensor(t4[:, i1], x1[:, :, i1, :].unsqueeze(2).to_broadcast([P, G, 3, 32]),
                                             fac[:, r, :, 7 + 3 * i1:10 + 3 * i1].unsqueeze(3).to_broadcast([P, G, 3, 32]), ALU.mult)
                        ins.then_inc(ev["t4_"].sem, 1)
                        for i1 in range(3):
                            ins = v_.tensor_tensor(t3[:, i1], x1[:, :, i1, :],
                                             fac[:, r, :, 4 + i1].unsqueeze(2).to_broadcast([P, G, 32]), ALU.mult)
                        ins.then_inc(ev["x1_"].sem, 1)
                        ev["t4_"].wait(dve, v)
                        v_.tensor_tensor(a4[:], t4[:, 0], t4[:, 1], ALU.add).then_inc(ev["a4_"].sem, 1)
                        ev["x1_"].wait(dve, v)
                        v_.tensor_tensor(a3[:], t3[:, 0], t3[:, 1], ALU.add).then_inc(ev["a3_"].sem, 1)
                        ev["rel_"].wait(dve, v)
                        for t in range(G):
                            ins = v_.tensor_scalar(hot[:, q, t, :], iotaf[:], rel[:, q, t:t + 1], None, ALU.is_equal)
                        ins.then_inc(ev["hot_"].sem, 1)
                        ev["a4_"].wait(dve, v)
                        v_.tensor_tensor(prod[:, q, :, 256:352].rearrange("p t (k u) -> p t k u", k=3), a4[:], t4[:, 2], ALU.add)
                        ev["a3_"].wait(dve, v)
                        v_.tensor_tensor(prod[:, q, :, 224:256], a3[:], t3[:, 2], ALU.add).then_inc(ev["made"].sem, 1)
                    if old:
                        i, r, v = old
                        tile, node = vis.pair(dve, i)
                        ev["msg_"].wait(dve, v)
                        ev["added"].wait(dve, v - 1)
                        v_.tensor_tensor(sums[:, ds(node, P)], sums[:, ds(node, P)], pmsg[:, r % 2, 0:P], ALU.add).then_inc(ev["added"].sem, 1)

                vis.loop(dve, turn, 2)

            @block.tensor
            def _(pe):
                for n in ("agg", "msg_"):
                    ev[n].start(pe)
                pe.wait_ge(cleared, 2)

                def turn(now, last):
                    if now:
                        i, r, v = now
                        q = r % 2
                        ev["hot_"].wait(pe, v)
                        ev["made"].wait(pe, v)
                        ev["scalars"].wait(pe, v)
                        ev["win_"].wait(pe, v - 2)
                        for b, (o, w) in enumerate(BLK):
                            for t in range(G):
                                ins = pe.matmul(pagg[0:w, q, b, 0:P], prod[:, q, t, o:o + w], hot[:, q, t, :],
                                                start=(t == 0), stop=(t == G - 1))
                        ins.then_inc(ev["agg"].sem, 1)
                    if last:
                        i, r, v = last
                        q = r % 2
                        ev["win_"].wait(pe, v)
                        ev["added"].wait(pe, v - 2)
                        for b, (o, w) in enumerate(BLK):
                            ins = pe.matmul(pmsg[:, q, 0:P], w2[0:w, b, :], win[0:w, b, :], start=(b == 0), stop=(b == 2))
                        ins.then_inc(ev["msg_"].sem, 1)

                vis.loop(pe, turn, 1)



def phase_node(env, layer, xold, xnew, table, params):
    nc, dstf, srci, identf, iotaf, epsc, meta, pairs, baseB, sums, aux, visit_base, visit_pair = env
    with ExitStack() as ctx:
        sb = lambda n, s, d=F32: ctx.enter_context(nc.sbuf_tensor(f"n{layer}_" + n, s, d))
        ps = lambda n, s, d=F32: ctx.enter_context(nc.psum_tensor(f"n{layer}_" + n, s, d))
        sem = phase_semaphores(nc, ctx, f"n{layer}_")
        xin = sb("xin", [P, 2, BATCH, D])
        xout = sb("xout", [P, 2, BATCH, D])
        hout = sb("hout", [P, 2, BATCH, D])
        xc = sb("xc", [P, BATCH, D])
        nrm = sb("nrm", [P, BATCH, D])
        sq = sb("sq", [P, BATCH, D])
        s = sb("s", [P, 40])
        new = sb("new", [P, BATCH, D])
        gm = sb("gm", [P, BC])
        dens = sb("dens", [68, BC])
        rden = sb("rden", [P, BATCH, H])
        row = sb("row", [P, 2, D])
        w = sb("w", [P, D])
        pden = ps("pden", [P, 512])
        pT = ps("pT", [P, 1024])
        xl = [sem("xl0"), sem("xl1")]
        stored = [sem("stored0"), sem("stored1")]
        loaded, chain = sem("loaded"), sem("chain")
        ev = {n: Event(sem(n)) for n in ("dens_", "gm_", "nodes", "pre", "act_", "xnew_", "normed", "hnew", "kept")}
        for n in ("centred", "squared", "varied", "rooted"):
            ev[n] = Event(sem(n), 2 if layer == 0 else 1)
        ev["rden_"] = Event(sem("rden_"), 2)

        with nc.Block() as block:
            @block.sync
            def _(sp):
                if layer == 0:
                    sp.dma_start(row[:, 0, :], params["scale"].to_broadcast([P, D])).then_inc(loaded, 16)
                    sp.dma_start(row[:, 1, :], params["bias"].to_broadcast([P, D])).then_inc(loaded, 16)
                if layer == 1:
                    sp.dma_start(row[:, 0, :], params["b"].to_broadcast([P, D])).then_inc(loaded, 16)
                    sp.dma_start(w[:], params["W"]).then_inc(loaded, 16)
                ev["kept"].start(sp)
                with sp.Fori(0, STEPS // 2) as half:
                    i = half * 2
                    for r in range(2):
                        ev["hnew"].wait(sp, i + r)
                        sp.dma_start(blocks_of(xnew, i + r), xout[:, r]).then_inc(stored[r], 16)
                        sp.dma_start(blocks_of(table, i + r), hout[:, r]).then_inc(stored[r], 16)
                        sp.wait_ge(stored[r], i * 16 + 32)
                        sp.sem_inc(ev["kept"].sem, 1)

            @block.gpsimd
            def _(pool):
                load_blocks(nc, pool, ((xold, xin, xl),), ev["xnew_"])

            @block.tensor
            def _(pe):
                ev["nodes"].start(pe)
                if layer == 1:
                    pe.wait_ge(loaded, 32)

                def turn(now, _):
                    if now:
                        it, r = now
                        ev["gm_"].wait(pe, it)
                        ev["xnew_" if layer == 2 else "pre"].wait(pe, it - 1)
                        for b in range(BATCH):
                            c = slice(b * P, (b + 1) * P)
                            if layer == 1:
                                ins = pe.matmul(pT[:, c], gm[:, c], w[:], start=True, stop=True)
                            else:
                                ins = pe.transpose(pT[:, c], gm[:, c], identf[:])
                        if layer == 0:
                            ev["dens_"].wait(pe, it)
                            pe.nop(nofuse=True)
                            for b in range(BATCH):
                                ins = pe.transpose(pden[:, 68 * b:68 * b + 68], dens[:, b * P:(b + 1) * P], identf[0:68, 0:68])
                        ins.then_inc(ev["nodes"].sem, 1)

                in_pairs(pe, turn)

            @block.scalar
            def _(act):
                a = nc.scalar
                for n in ("squared", "rooted", "dens_", "gm_", "act_", "hnew"):
                    ev[n].start(act)

                def turn(now, last):
                    if now:
                        it, _ = now
                        ev["nodes"].wait(act, it - 1)
                        act.nop(nofuse=True)
                        a.activation(gm[:], sums[:, ds(it * BC, BC)], ACT.Gelu_apprx_tanh if layer == 1 else ACT.Copy)\
                            .then_inc(ev["gm_"].sem, 1)
                        if layer == 0:
                            a.activation(dens[:], aux[0:68, ds(it * BC, BC)], ACT.Copy).then_inc(ev["dens_"].sem, 1)
                    if last:
                        lt, lr = last
                        if layer == 0:
                            norm_scalar(nc, act, ev, lt, 1, xc[:], sq[:], s, epsc)
                            norm_scalar(nc, act, ev, lt, 2, nrm[:], sq[:], s, epsc)
                        else:
                            ev["centred"].wait(act, lt)
                            a.activation(sq[:], nrm[:], ACT.Square).then_inc(ev["squared"].sem, 1)
                    if now and layer < 2:
                        ev["pre"].wait(act, it)
                        ev["xnew_"].wait(act, it - 1)
                        if layer == 0:
                            a.activation(new[:], new[:], ACT.Gelu).then_inc(ev["act_"].sem, 1)
                        else:
                            a.activation(new[:], xc[:], ACT.Gelu_apprx_tanh).then_inc(ev["act_"].sem, 1)
                    if last:
                        if layer > 0:
                            ev["varied"].wait(act, lt)
                            a.activation(s[:, 24:24 + BATCH], s[:, 16:16 + BATCH], ACT.Sqrt, bias=epsc[:], scale=1.0 / D)\
                                .then_inc(ev["rooted"].sem, 1)
                        ev["normed"].wait(act, lt)
                        ev["kept"].wait(act, lt - 2)
                        a.activation(hout[:, lr], nrm[:], ACT.Relu).then_inc(ev["hnew"].sem, 1)

                in_pairs(act, turn)

            @block.vector
            def _(dve):
                v = nc.vector
                for n in ("centred", "varied", "rden_", "pre", "xnew_", "normed"):
                    ev[n].start(dve)
                if layer < 2:
                    dve.wait_ge(loaded, 32)
                node_rows = pT[:, 0:BC].rearrange("p (b f) -> p b f", f=D)
                wide = lambda k: row[:, k, :].unsqueeze(1).to_broadcast([P, BATCH, D])
                by_head = lambda ap: ap.rearrange("p b (h d) -> p (b h) d", h=H)
                links = {0: 10, 1: 4, 2: 4}[layer]

                def turn(now, last):
                    def take():
                        if now and layer < 2:
                            it, r = now
                            ev["nodes"].wait(dve, it)
                            if layer == 0:
                                dens_T = pden[:, 0:68 * BATCH].rearrange("p (b k) -> p b k", k=68)[:, :, 64:68]
                                v.tensor_scalar(rden[:], dens_T, 1e-9, None, ALU.add).then_inc(ev["rden_"].sem, 1)
                                ev["rden_"].wait(dve, it, 1)
                                v.reciprocal(rden[:], rden[:]).then_inc(ev["rden_"].sem, 1)
                                ev["rden_"].wait(dve, it)
                                if last:
                                    ev["centred"].wait(dve, last[0], 1)
                                v.tensor_tensor(by_head(new[:]), pT[:, 0:BC].rearrange("p (c d) -> p c d", d=HD),
                                                rden[:].rearrange("p b h -> p (b h)").unsqueeze(2).to_broadcast([P, BATCH * H, HD]),
                                                ALU.mult).then_inc(ev["pre"].sem, 1)
                            else:
                                ev["act_"].wait(dve, it - 1)
                                v.tensor_tensor(xc[:], node_rows, wide(0), ALU.add).then_inc(ev["pre"].sem, 1)

                    def add(step, what):
                        it, r = step
                        dve.wait_ge(xl[r], (it - r) * 8 + 16)
                        ev["kept"].wait(dve, it - 2)
                        v.tensor_tensor(xout[:, r], xin[:, r], what, ALU.add).then_inc(ev["xnew_"].sem, 1)

                    def renew():
                        if now and layer > 0:
                            ev["act_" if layer == 1 else "nodes"].wait(dve, now[0])
                            add(now, new[:] if layer == 1 else node_rows)

                    if last:
                        it, r = last
                        c = Chain(dve, chain, it * links)
                        if layer == 0:
                            ev["act_"].wait(dve, it)
                            norm_vector(nc, dve, c, ev, it, 1, new[:], xc[:], sq[:], s, take)
                            c(v.tensor_tensor(xc[:], xc[:], wide(0), ALU.mult))
                            c(v.tensor_tensor(xc[:], xc[:], wide(1), ALU.add))
                            add(last, xc[:])
                        ev["xnew_"].wait(dve, it)
                        ev["hnew"].wait(dve, it - 1)
                        if layer == 0:
                            norm_vector(nc, dve, c, ev, it, 2, xout[:, r], nrm[:], sq[:], s)
                        else:
                            norm_vector(nc, dve, c, ev, it, 1, xout[:, r], nrm[:], sq[:], s, take, renew)
                        dve.sem_inc(ev["normed"].sem, 1)
                        assert c.n == links, c.n
                    else:
                        take()
                        renew()

                in_pairs(dve, turn)



def phase_last(env, x3, table, WlT, WrT, bl, gamma, beta, out):
    nc, dstf, srci, identf, iotaf, epsc, meta, pairs, baseB, sums, aux, visit_base, visit_pair = env
    with ExitStack() as ctx:
        sb = lambda n, s, d=F32: ctx.enter_context(nc.sbuf_tensor("l_" + n, s, d))
        ps = lambda n, s, d=F32: ctx.enter_context(nc.psum_tensor("l_" + n, s, d))
        sem = phase_semaphores(nc, ctx, "l_")
        hin = sb("hin", [P, 2, BATCH, D])
        xin = sb("xin", [P, 2, BATCH, D])
        xout = sb("xout", [P, 2, BATCH, D])
        hT = sb("hT", [P, 2, BC])
        total = sb("total", [P, 2, BC])
        count = sb("count", [P, 2, BC])
        rcount = sb("rcount", [P, BATCH])
        wl, wr = sb("wl", [P, D]), sb("wr", [P, D])
        par = sb("par", [P, 3, D])
        ones = sb("ones", [P, P])
        stat = sb("stat", [P, 8, D])
        tot = sb("tot", [P, BATCH, D])
        pT = ps("pT", [P, 1024])
        pl = ps("pl", [P, 1024])
        pr = ps("pr", [P, 1024])
        pc = ps("pc", [P, 4 * BATCH])
        pst = ps("pst", [P, 512])
        hl = [sem("hl0"), sem("hl1")]
        xl = [sem("xl0"), sem("xl1")]
        stored = [sem("stored0"), sem("stored1")]
        loaded, setup, chain, schain, stm, ychain, roots = (
            sem(n) for n in ("loaded", "setup", "chain", "schain", "stm", "ychain", "roots"))
        ev = {n: Event(sem(n)) for n in ("taken", "drawn", "turned", "hT_", "y_", "kept", "done", "saved")}
        y = sums[:, 0:NP].rearrange("p (b f) -> p b f", f=D)
        LAST = N - (NB - 1) * P

        with nc.Block() as block:
            @block.sync
            def _(sp):
                for t, src in ((wl[:], WlT), (wr[:], WrT), (par[:, 0, :], bl.to_broadcast([P, D])),
                               (par[:, 1, :], gamma.to_broadcast([P, D])), (par[:, 2, :], beta.to_broadcast([P, D]))):
                    sp.dma_start(t, src).then_inc(loaded, 16)
                ev["saved"].start(sp)
                with sp.Fori(0, STEPS // 2) as half:
                    i = half * 2
                    for r in range(2):
                        ev["done"].wait(sp, i + r)
                        sp.dma_start(blocks_of(out, i + r), xout[:, r]).then_inc(stored[r], 16)
                        sp.wait_ge(stored[r], i * 8 + 16)
                        sp.sem_inc(ev["saved"].sem, 1)

            @block.gpsimd
            def _(pool):
                load_blocks(nc, pool, ((table, hin, hl),), ev["turned"])
                load_blocks(nc, pool, ((x3, xin, xl),), ev["done"])

            @block.tensor
            def _(pe):
                for n in ("turned", "y_"):
                    ev[n].start(pe)
                pe.wait_ge(loaded, 80)

                def turn(now, last):
                    if last:
                        lt, lr = last
                        ev["hT_"].wait(pe, lt)
                        ev["taken"].wait(pe, lt)
                        ev["drawn"].wait(pe, lt - 1)
                        for b in range(BATCH):
                            c = slice(b * P, (b + 1) * P)
                            pe.matmul(pl[:, c], total[:, lr, c], wl[:], start=True, stop=True)
                            pe.matmul(pr[:, c], hT[:, lr, c], wr[:], start=True, stop=True)
                            ins = pe.matmul(pc[:, 4 * b:4 * b + 4], count[:, lr, c], identf[:, 0:4], start=True, stop=True)
                        ins.then_inc(ev["y_"].sem, 1)
                    if now:
                        it, r = now
                        pe.wait_ge(hl[r], (it - r) * 8 + 16)
                        ev["hT_"].wait(pe, it - 1)
                        pe.nop(nofuse=True)
                        for b in range(BATCH):
                            ins = pe.transpose(pT[:, b * P:(b + 1) * P], hin[:, r, b, :], identf[:])
                        ins.then_inc(ev["turned"].sem, 1)

                in_pairs(pe, turn)
                for n in range(2):
                    pe.wait_ge(stm, n + 1)
                    pe.matmul(pst[:, n * D:(n + 1) * D], ones[:], stat[:, 2 * n, :], start=True, stop=False)
                    pe.matmul(pst[:, n * D:(n + 1) * D], ones[0:LAST, :], stat[0:LAST, 2 * n + 1, :], start=False, stop=True).then_inc(setup, 1)

            @block.scalar
            def _(act):
                a = nc.scalar
                ev["hT_"].start(act)
                ev["taken"].start(act)
                with act.Fori(0, STEPS // 2) as half:
                    i = half * 2
                    for r in range(2):
                        it = i + r
                        ev["y_"].wait(act, it - 2)
                        act.nop(nofuse=True)
                        a.activation(total[:, r], sums[:, ds(it * BC, BC)], ACT.Copy)
                        a.activation(count[:, r], aux[:, ds(it * BC, BC)], ACT.Copy).then_inc(ev["taken"].sem, 1)
                        ev["turned"].wait(act, it)
                        a.activation(hT[:, r], pT[:, 0:BC], ACT.Copy).then_inc(ev["hT_"].sem, 1)
                act.wait_ge(roots, 1)
                a.activation(stat[:, 5, :], stat[:, 4, :], ACT.Sqrt, bias=epsc[:], scale=1.0 / N).then_inc(roots, 1)

            @block.vector
            def _(dve):
                v = nc.vector
                for n in ("drawn", "kept", "done"):
                    ev[n].start(dve)
                c = Chain(dve, schain)
                c(v.memset(ones[:], 1.0))
                dve.wait_ge(loaded, 80)
                with dve.Fori(0, STEPS) as it:
                    cc = Chain(dve, chain, it * 3)
                    ev["y_"].wait(dve, it)
                    cc(v.tensor_scalar(rcount[:], pc[:].rearrange("p (b k) -> p b k", k=4)[:, :, 0], 1.0, None, ALU.max))
                    cc(v.reciprocal(rcount[:], rcount[:]))
                    cc(v.tensor_tensor(tot[:], pl[:, 0:BC].rearrange("p (b f) -> p b f", f=D),
                                       rcount[:].unsqueeze(2).to_broadcast([P, BATCH, D]), ALU.mult))
                    v.tensor_tensor(tot[:], tot[:], pr[:, 0:BC].rearrange("p (b f) -> p b f", f=D), ALU.add).then_inc(ev["drawn"].sem, 1)
                    ev["drawn"].wait(dve, it)
                    v.tensor_tensor(sums[:, ds(it * BC, BC)].rearrange("p (b f) -> p b f", f=D), tot[:],
                                    par[:, 0, :].unsqueeze(1).to_broadcast([P, BATCH, D]), ALU.add).then_inc(ev["kept"].sem, 1)
                    ev["kept"].wait(dve, it)
                by_feature = y[:, 0:NB - 1, :].rearrange("p b f -> p f b")
                c(v.tensor_reduce(stat[:, 0, :], by_feature, AX, ALU.add))
                c(v.tensor_copy(stat[:, 1, :], y[:, NB - 1, :]))
                dve.sem_inc(stm, 1)
                dve.wait_ge(setup, 1)
                c(v.tensor_scalar(stat[:, 6, :], pst[:, 0:D], -1.0 / N, None, ALU.mult))
                c(v.tensor_tensor(y, y, stat[:, 6, :].unsqueeze(1).to_broadcast([P, NB, D]), ALU.add))
                sqv = aux[:, 0:NP].rearrange("p (b f) -> p b f", f=D)
                c(v.tensor_tensor(sqv, y, y, ALU.mult))
                c(v.tensor_reduce(stat[:, 2, :], sqv[:, 0:NB - 1, :].rearrange("p b f -> p f b"), AX, ALU.add))
                c(v.tensor_copy(stat[:, 3, :], sqv[:, NB - 1, :]))
                dve.sem_inc(stm, 1)
                dve.wait_ge(setup, 2)
                c(v.tensor_copy(stat[:, 4, :], pst[:, D:2 * D]))
                dve.sem_inc(roots, 1)
                dve.wait_ge(roots, 2)
                c(v.reciprocal(stat[:, 7, :], stat[:, 5, :]))
                c(v.tensor_tensor(stat[:, 7, :], stat[:, 7, :], par[:, 1, :], ALU.mult))
                with dve.Fori(0, STEPS // 2) as half:
                    i = half * 2
                    for r in range(2):
                        it = i + r
                        cc = Chain(dve, ychain, it * 2)
                        dve.wait_ge(xl[r], i * 8 + 16)
                        ev["saved"].wait(dve, it - 2)
                        ev["done"].wait(dve, it - 1)
                        ys = sums[:, ds(it * BC, BC)].rearrange("p (b f) -> p b f", f=D)
                        cc(v.tensor_tensor(tot[:], ys, stat[:, 7, :].unsqueeze(1).to_broadcast([P, BATCH, D]), ALU.mult))
                        cc(v.tensor_tensor(tot[:], tot[:], par[:, 2, :].unsqueeze(1).to_broadcast([P, BATCH, D]), ALU.add))
                        v.tensor_tensor(xout[:, r], tot[:], xin[:, r], ALU.add).then_inc(ev["done"].sem, 1)



def kernel(x, src, dst, edge_attr_16, edge_attr_9, edge_weight, edge_weight1, L0_gnn_W, L0_gnn_W_e, L0_gnn_a,
           L0_gnn_ln_scale, L0_gnn_ln_bias, L1_gnn_W, L1_gnn_b, L2_gnn_weights, L3_gnn_W_l, L3_gnn_b_l,
           L3_gnn_W_r, L3_gnn_gamma, L3_gnn_beta):
    import concourse.bacc as bacc
    from concourse.bass_utils import run_bass_kernel_spmd

    def by_tile(a, fill=0):
        a = np.asarray(a)
        full = np.full((T * P,) + a.shape[1:], fill, a.dtype)
        full[:E] = a
        return np.ascontiguousarray(np.swapaxes(full.reshape((T, P) + a.shape[1:]), 0, 1))

    xp = np.zeros((NP, D), np.float32)
    xp[:N] = np.asarray(x)
    ef = np.zeros((STEPS * EC * G * P, 16), np.float32)
    ef[:E] = np.asarray(edge_attr_16)
    ef = np.ascontiguousarray(ef.reshape(STEPS * EC, G, P, 16).transpose(1, 3, 0, 2)).reshape(P, STEPS * EC, P)
    harmonics = np.zeros((P, STEPS * FT, 9), np.float32)
    harmonics[:, :T] = by_tile(edge_attr_9)
    CG = clebsch_gordan()
    W2 = np.asarray(L2_gnn_weights)
    a0, a1 = 1.0 / math.sqrt(2 * 32), 1.0 / math.sqrt(3 * 32)
    w2b = np.zeros((3, P, D), np.float32)
    scale = np.ones((3, P), np.float32)
    w2b[0, 0:32, 0:32] = W2[0]
    scale[0, 0:32] = a0 * float(CG[0][0, 0, 0])
    for k in range(3):
        w2b[0, 32 + k:P:3, 32 + k:P:3] = W2[2]
        scale[0, 32 + k:P:3] = a1 * float(CG[2][k, 0, k])
        w2b[1, 32 * k:32 * k + 32, 32 + k:P:3] = W2[1]
        w2b[2, 32 * k:32 * k + 32, 32 + k:P:3] = W2[4]
    scale[1, 0:96] = a1
    w2b[1, 96:128, 0:32] = W2[3]
    scale[1, 96:128] = a0
    scale[2, 0:96] = a1
    flat = lambda a: np.ascontiguousarray(np.asarray(a))
    arrays = dict(
        x=xp, src=by_tile(src), dst=by_tile(dst, -1), w1e=by_tile(np.asarray(edge_weight1)[:, 0]),
        sh=harmonics.reshape(P, STEPS * FT * 9), ef=ef, W0=flat(L0_gnn_W), W0T=flat(np.asarray(L0_gnn_W).T),
        WeT=flat(np.asarray(L0_gnn_W_e).T), aT=flat(np.asarray(L0_gnn_a).T),
        ln_scale=flat(L0_gnn_ln_scale)[None], ln_bias=flat(L0_gnn_ln_bias)[None],
        W1T=flat(np.asarray(L1_gnn_W).T), b1=flat(L1_gnn_b)[None], W2b=flat(w2b.transpose(1, 0, 2)),
        W2scale=flat(scale.T), WlT=flat(np.asarray(L3_gnn_W_l).T), bl=flat(L3_gnn_b_l)[None],
        WrT=flat(np.asarray(L3_gnn_W_r).T), gamma=flat(L3_gnn_gamma)[None], beta=flat(L3_gnn_beta)[None],
        ident=np.eye(P, dtype=np.float32), iota=np.tile(np.arange(PG, dtype=np.float32), (P, 1)),
    )
    nc = bacc.Bacc("TRN2", target_bir_lowering=False, num_devices=1)
    given = {k: nc.dram_tensor("in_" + k, a.shape, mybir.dt.from_np(a.dtype), kind="ExternalInput").ap()
             for k, a in arrays.items()}
    out = nc.dram_tensor("out_x", [NP, D], F32, kind="ExternalOutput").ap()
    build(nc, out=out, **given)
    r = run_bass_kernel_spmd(nc, [{"in_" + k: a for k, a in arrays.items()}], core_ids=[0])
    return r.results[0]["out_x"][:N]
```
